# Optimizing a Trainium2 kernel written in Bass

```python
import numpy as np
import jax
import jax.numpy as jnp

def _softmax(x, axis=-1):
    return jax.nn.softmax(x, axis=axis)

def _gelu(x):
    return jax.nn.gelu(x, approximate=True)

def _silu(x):
    return jax.nn.silu(x)

def _sigmoid(x):
    return jax.nn.sigmoid(x)

def _layernorm(x, axis=-1, eps=1e-05):
    m = jnp.mean(x, axis=axis, keepdims=True)
    v = jnp.var(x, axis=axis, keepdims=True)
    return (x - m) / jnp.sqrt(v + eps)

def _scatter_add(tgt, idx, src, axis=0):
    return tgt.at[idx].add(src)

def _segment_sum(src, seg, n):
    return jax.ops.segment_sum(src, seg, n)
kernel_name = 'mk_xattn_ffn_d2_seqx_r4_e7946f'

def setup_inputs(seed: int=0):
    np.random.seed(seed)
    _w = jnp.asarray

    def _rec_inputs():
        import jax
        import jax.numpy as jnp
        _rk = jax.random.key(seed)
        x = 7.22e-05 + 1 * jax.random.normal(jax.random.fold_in(_rk, 1), (4, 1024, 256), jnp.float32)
        _lenS = 1024 - jax.random.randint(jax.random.fold_in(_rk, 7), (4,), 0, max(1, 1024 // 4) + 1, jnp.int32)
        _lenS2 = 77 - jax.random.randint(jax.random.fold_in(_rk, 8), (4,), 0, max(1, 77 // 4) + 1, jnp.int32)
        _ctx_768P = jax.random.normal(jax.random.fold_in(_rk, 11), (4, 16, 192), jnp.float32)
        _ctx_768c = jax.random.dirichlet(jax.random.fold_in(_rk, 511), 0.3 * jnp.ones((16,), jnp.float32), (4, 77))
        _ctx_768t = jnp.einsum('bsk,bkd->bsd', _ctx_768c, _ctx_768P)
        _ctx_768t = _ctx_768t * jax.lax.rsqrt(jnp.mean(jnp.square(_ctx_768t)) + 1e-12) * 0.953939
        ctx_768 = -0.000191848 + 0.999787 * (_ctx_768t + 0.3 * jax.random.normal(jax.random.fold_in(_rk, 611), (4, 77, 192), jnp.float32))
        return (x, ctx_768)
    x, ctx_768 = _rec_inputs()

    def _L0_xattn_setup():
        import jax, jax.numpy as jnp
        import numpy as np
        HEADS = 8
        DIM_HEAD = 64
        SCALE = DIM_HEAD ** (-0.5)
        key = jax.random.key(seed)
        ks = jax.random.split(key, 7)
        B, Nq, Nc = (4, 512, 512)
        Dq, Dc = (256, 192)
        inner = HEADS * DIM_HEAD
        x = jax.random.normal(ks[0], (B, Nq, Dq), dtype=jnp.float32)
        context = jax.random.normal(ks[1], (B, Nc, Dc), dtype=jnp.float32)
        Wq = jax.random.normal(ks[2], (Dq, inner), dtype=jnp.float32) * Dq ** (-0.5)
        Wk = jax.random.normal(ks[3], (Dc, inner), dtype=jnp.float32) * Dc ** (-0.5)
        Wv = jax.random.normal(ks[4], (Dc, inner), dtype=jnp.float32) * Dc ** (-0.5)
        Wo = jax.random.normal(ks[5], (inner, Dq), dtype=jnp.float32) * inner ** (-0.5)
        bo = jax.random.normal(ks[6], (Dq,), dtype=jnp.float32) * 0.01
        return {'x': x, 'context': context, 'Wq': Wq, 'Wk': Wk, 'Wv': Wv, 'Wo': Wo, 'bo': bo}
    _L0_xattn_all = _L0_xattn_setup()
    _L0_xattn_in = {k: v for k, v in _L0_xattn_all.items() if k in ('Wq', 'Wk', 'Wv', 'Wo', 'bo')}
    del _L0_xattn_all

    def _L0_ffn_setup():
        import jax, jax.numpy as jnp
        import numpy as np
        B, T, H = (8, 512, 256)
        F = 1024
        E = 8
        TOP_K = 2
        key = jax.random.key(seed)
        ks = jax.random.split(key, 6)
        s_h = 1.0 / np.sqrt(H)
        s_f = 1.0 / np.sqrt(F)
        return {'hidden_states': jax.random.normal(ks[0], (B, T, H), dtype=jnp.float32), 'gate_w': jax.random.uniform(ks[1], (H, E), minval=-s_h, maxval=s_h, dtype=jnp.float32), 'w1': jax.random.uniform(ks[2], (E, H, F), minval=-s_h, maxval=s_h, dtype=jnp.float32), 'b1': jax.random.uniform(ks[3], (E, F), minval=-s_h, maxval=s_h, dtype=jnp.float32), 'w2': jax.random.uniform(ks[4], (E, F, H), minval=-s_f, maxval=s_f, dtype=jnp.float32), 'b2': jax.random.uniform(ks[5], (E, H), minval=-s_f, maxval=s_f, dtype=jnp.float32)}
    _L0_ffn_all = _L0_ffn_setup()
    _L0_ffn_in = {k: v for k, v in _L0_ffn_all.items() if k in ('gate_w', 'w1', 'b1', 'w2', 'b2')}
    del _L0_ffn_all

    def _L1_xattn_setup():
        import jax, jax.numpy as jnp
        import numpy as np
        HEADS = 16
        DIM_HEAD = 64
        key = jax.random.key(seed)
        ks = jax.random.split(key, 7)
        B, Nq, Dq = (4, 512, 256)
        Nk, Dc = (256, 192)
        inner = HEADS * DIM_HEAD
        sq = 1.0 / np.sqrt(Dq)
        sc = 1.0 / np.sqrt(Dc)
        si = 1.0 / np.sqrt(inner)
        return {'x': jax.random.normal(ks[0], (B, Nq, Dq), dtype=jnp.float32), 'context': jax.random.normal(ks[1], (B, Nk, Dc), dtype=jnp.float32), 'Wq': jax.random.normal(ks[2], (Dq, inner), dtype=jnp.float32) * sq, 'Wk': jax.random.normal(ks[3], (Dc, inner), dtype=jnp.float32) * sc, 'Wv': jax.random.normal(ks[4], (Dc, inner), dtype=jnp.float32) * sc, 'Wo': jax.random.normal(ks[5], (inner, Dq), dtype=jnp.float32) * si, 'bo': jax.random.normal(ks[6], (Dq,), dtype=jnp.float32) * 0.01}
    _L1_xattn_all = _L1_xattn_setup()
    _L1_xattn_in = {k: v for k, v in _L1_xattn_all.items() if k in ('Wq', 'Wk', 'Wv', 'Wo', 'bo')}
    del _L1_xattn_all

    def _L1_ffn_setup():
        import jax, jax.numpy as jnp
        import numpy as np
        K = 64
        key = jax.random.key(seed)
        ks = jax.random.split(key, 9)
        B, S, D, O, E = (8, 512, 256, 256, 16)

        def xavier(k_, shape):
            fan_in, fan_out = (shape[-2], shape[-1])
            lim = (6.0 / (fan_in + fan_out)) ** 0.5
            return jax.random.uniform(k_, shape, jnp.float32, -lim, lim)
        return {'x': jax.random.normal(ks[0], (B, S, D), jnp.float32), 'Wg': xavier(ks[1], (D, E)), 'bg': jnp.zeros((E,), jnp.float32), 'w1': xavier(ks[2], (E, D, O)), 'b1': xavier(ks[3], (E, 1)), 'w2': xavier(ks[4], (E, O, O)), 'b2': xavier(ks[5], (E, 1)), 'w3': xavier(ks[6], (E, O, O)), 'b3': xavier(ks[7], (E, 1))}
    _L1_ffn_all = _L1_ffn_setup()
    _L1_ffn_in = {k: v for k, v in _L1_ffn_all.items() if k in ('Wg', 'bg', 'w1', 'b1', 'w2', 'b2', 'w3', 'b3')}
    del _L1_ffn_all
    return {'x': x, 'ctx_768': ctx_768, 'L0_xattn_Wq': _L0_xattn_in['Wq'], 'L0_xattn_Wk': _L0_xattn_in['Wk'], 'L0_xattn_Wv': _L0_xattn_in['Wv'], 'L0_xattn_Wo': _L0_xattn_in['Wo'], 'L0_xattn_bo': _L0_xattn_in['bo'], 'L0_ffn_gate_w': _L0_ffn_in['gate_w'], 'L0_ffn_w1': _L0_ffn_in['w1'], 'L0_ffn_b1': _L0_ffn_in['b1'], 'L0_ffn_w2': _L0_ffn_in['w2'], 'L0_ffn_b2': _L0_ffn_in['b2'], 'L1_xattn_Wq': _L1_xattn_in['Wq'], 'L1_xattn_Wk': _L1_xattn_in['Wk'], 'L1_xattn_Wv': _L1_xattn_in['Wv'], 'L1_xattn_Wo': _L1_xattn_in['Wo'], 'L1_xattn_bo': _L1_xattn_in['bo'], 'L1_ffn_Wg': _L1_ffn_in['Wg'], 'L1_ffn_bg': _L1_ffn_in['bg'], 'L1_ffn_w1': _L1_ffn_in['w1'], 'L1_ffn_b1': _L1_ffn_in['b1'], 'L1_ffn_w2': _L1_ffn_in['w2'], 'L1_ffn_b2': _L1_ffn_in['b2'], 'L1_ffn_w3': _L1_ffn_in['w3'], 'L1_ffn_b3': _L1_ffn_in['b3']}

def reference(x, ctx_768, L0_xattn_Wq, L0_xattn_Wk, L0_xattn_Wv, L0_xattn_Wo, L0_xattn_bo, L0_ffn_gate_w, L0_ffn_w1, L0_ffn_b1, L0_ffn_w2, L0_ffn_b2, L1_xattn_Wq, L1_xattn_Wk, L1_xattn_Wv, L1_xattn_Wo, L1_xattn_bo, L1_ffn_Wg, L1_ffn_bg, L1_ffn_w1, L1_ffn_b1, L1_ffn_w2, L1_ffn_b2, L1_ffn_w3, L1_ffn_b3):
    import jax
    import jax.numpy as jnp

    def _L0_xattn_ref(x, context, Wq, Wk, Wv, Wo, bo):
        import jax, jax.numpy as jnp
        import numpy as np
        HEADS = 8
        DIM_HEAD = 64
        SCALE = DIM_HEAD ** (-0.5)
        B, Nq, _ = x.shape
        q = (x @ Wq).reshape(B, Nq, HEADS, DIM_HEAD)
        k = (context @ Wk).reshape(B, context.shape[1], HEADS, DIM_HEAD)
        v = (context @ Wv).reshape(B, context.shape[1], HEADS, DIM_HEAD)
        sim = jnp.einsum('bihd,bjhd->bhij', q, k) * SCALE
        attn = jax.nn.softmax(sim, axis=-1)
        out = jnp.einsum('bhij,bjhd->bihd', attn, v)
        out = out.reshape(B, Nq, HEADS * DIM_HEAD)
        return out @ Wo + bo

    def _L0_ffn_ref(hidden_states, gate_w, w1, b1, w2, b2):
        import jax, jax.numpy as jnp
        import numpy as np
        B, T, H = (8, 512, 256)
        F = 1024
        E = 8
        TOP_K = 2
        b, t, h = hidden_states.shape
        seq_rep = hidden_states.mean(axis=1)
        router_logits = seq_rep @ gate_w
        probs = jax.nn.softmax(router_logits.astype(jnp.float32), axis=-1)
        top_w, top_i = jax.lax.top_k(probs, TOP_K)
        top_w = top_w / top_w.sum(axis=-1, keepdims=True)
        top_w = top_w.astype(hidden_states.dtype)
        combine = jnp.zeros((b, E), dtype=hidden_states.dtype)
        combine = combine.at[jnp.arange(b)[:, None], top_i].set(top_w)
        out = jnp.zeros_like(hidden_states)
        for e in range(E):
            hmid = jax.nn.gelu(jnp.einsum('bth,hf->btf', hidden_states, w1[e]) + b1[e], approximate=False)
            y = jnp.einsum('btf,fh->bth', hmid, w2[e]) + b2[e]
            out = out + combine[:, e][:, None, None] * y
        return out

    def _L1_xattn_ref(x, context, Wq, Wk, Wv, Wo, bo):
        import jax, jax.numpy as jnp
        import numpy as np
        HEADS = 16
        DIM_HEAD = 64
        B, Nq, _ = x.shape
        Nk = context.shape[1]
        h, dh = (HEADS, DIM_HEAD)
        q = (x @ Wq).reshape(B, Nq, h, dh)
        k = (context @ Wk).reshape(B, Nk, h, dh)
        v = (context @ Wv).reshape(B, Nk, h, dh)
        scale = 1.0 / jnp.sqrt(jnp.asarray(dh, dtype=x.dtype))
        scores = jnp.einsum('bqhd,bkhd->bhqk', q, k) * scale
        attn = jax.nn.softmax(scores, axis=-1)
        out = jnp.einsum('bhqk,bkhd->bqhd', attn, v).reshape(B, Nq, h * dh)
        return out @ Wo + bo

    def _L1_ffn_ref(x, Wg, bg, w1, b1, w2, b2, w3, b3):
        import jax, jax.numpy as jnp
        import numpy as np
        K = 64
        B, S, D = x.shape
        E, _, O = w1.shape
        logits = jnp.einsum('bsd,de->bse', x, Wg) + bg
        probs = jax.nn.softmax(logits, axis=-2)
        pv = jnp.transpose(probs, (0, 2, 1))
        vals, idx = jax.lax.top_k(pv, K)
        bidx = jnp.arange(B)[:, None, None]
        tok = x[bidx, idx]
        b1b = b1[None, :, None, :]
        b2b = b2[None, :, None, :]
        b3b = b3[None, :, None, :]
        h = jax.nn.relu(jnp.einsum('bekd,edo->beko', tok, w1) + b1b)
        h = jax.nn.relu(jnp.einsum('bekd,edo->beko', h, w2) + b2b)
        h = jnp.einsum('bekd,edo->beko', h, w3) + b3b
        out = h * vals[..., None]
        outputs = jnp.zeros((B, S, O), x.dtype).at[bidx, idx].add(out)
        return outputs
    x = x + _L0_xattn_ref(_layernorm(x, axis=-1), ctx_768, L0_xattn_Wq, L0_xattn_Wk, L0_xattn_Wv, L0_xattn_Wo, L0_xattn_bo)
    x = x + _L0_ffn_ref(_layernorm(x, axis=-1), L0_ffn_gate_w, L0_ffn_w1, L0_ffn_b1, L0_ffn_w2, L0_ffn_b2)
    x = x + _L1_xattn_ref(_layernorm(x, axis=-1), ctx_768, L1_xattn_Wq, L1_xattn_Wk, L1_xattn_Wv, L1_xattn_Wo, L1_xattn_bo)
    x = x + _L1_ffn_ref(_layernorm(x, axis=-1), L1_ffn_Wg, L1_ffn_bg, L1_ffn_w1, L1_ffn_b1, L1_ffn_w2, L1_ffn_b2, L1_ffn_w3, L1_ffn_b3)
    return x

_drawn_inputs = setup_inputs


def setup_inputs(seed=0):
    import zlib

    import numpy as np

    out = dict(_drawn_inputs(seed))
    spreads = {'L1_ffn_bg': (0.0, 2.0)}
    factors = {'L0_xattn_bo': 6.588,
     'L0_ffn_b1': 7.437,
     'L0_ffn_b2': 5.445,
     'L1_xattn_bo': 6.919,
     'L1_ffn_Wg': 8.0,
     'L1_ffn_w1': 8.0,
     'L1_ffn_b1': 8.0,
     'L1_ffn_w2': 8.0,
     'L1_ffn_b2': 8.0,
     'L1_ffn_w3': 8.0,
     'L1_ffn_b3': 56.187}
    for name, (base, spread) in spreads.items():
        noise = np.random.default_rng([zlib.crc32(name.encode()), seed]).standard_normal(out[name].shape)
        drawn = base * np.exp(spread * noise) if base else spread * noise
        out[name] = jnp.asarray(drawn.astype(out[name].dtype))
    for name, factor in factors.items():
        out[name] = (out[name] * factor).astype(out[name].dtype)
    return out
```

```python
from contextlib import ExitStack

import concourse.bass as bass
from concourse import mybir

F32 = mybir.dt.float32
F32R = mybir.dt.float32r
U32 = mybir.dt.uint32
ALU = mybir.AluOpType
ACT = mybir.ActivationFunctionType
AX_X = mybir.AxisListType.X

P = 128
B, S, D = 4, 1024, 256
KD = D // P
NT = S // P
NC, DC = 77, 192
CH = DC // 2
DH = 64
GH = 8
GP = GH // 2
GW = GH * NC
HALF = GW // 2
NCH = -(-GW // P)
PW = NCH * P
E0, F0, TOPK0 = 8, 1024, 2
FT = F0 // P
CHK = 512
NCK = S // CHK
TPC = CHK // P
E1, K1 = 16, 64
EPS = 1e-5
LOWEST = -3.0e38


class Program:

    def __init__(self, nc, ctx):
        self.nc, self.ctx = nc, ctx
        self.bank = [ctx.enter_context(nc.psum_tensor(f"bank{i}", [P, 512], F32)) for i in range(8)]
        self.x = self.sb("x_res", [P, B * NT, D])
        self.mean = self.sb("mean", [P, B * NT])
        self.rstd = self.sb("rstd", [P, B * NT])
        self.ident = self.sb("ident", [P, P])
        self.route_w = self.sb("route_w", [P, B, TOPK0])
        self.route_i = self.sb("route_i", [P, B, 8], U32)
        self.ffn_bias = self.sb("ffn_bias", [P, B, D])

        self.carry = self.sb("wait_carry", [P, 256])
        self.carries = 0
        self.one = self.sb("one", [P, 1])

    def wait_apart(self, engine, sem, value):
        engine.wait_ge(sem, value)
        spare = self.carry[:, self.carries:self.carries + 1]
        if engine is self.nc.vector:
            engine.memset(spare, 0.0)
        else:
            engine.tensor_tensor(spare, self.one[:], self.one[:], ALU.mult)
        self.carries += 1

    def sb(self, name, shape, dt=F32):
        return self.ctx.enter_context(self.nc.sbuf_tensor(name, shape, dt))

    def sem(self, name):
        return self.ctx.enter_context(self.nc.semaphore(name))


def load_phase(pr, x_in, ident_in):
    nc = pr.nc
    with ExitStack() as ctx:
        stats = ctx.enter_context(nc.sbuf_tensor("ld_stats", [P, B, NT, 6], F32))
        mv = ctx.enter_context(nc.sbuf_tensor("ld_mv", [P, B, NT, 2], F32))
        ve = ctx.enter_context(nc.sbuf_tensor("ld_ve", [P, B, NT], F32))
        power = ctx.enter_context(nc.sbuf_tensor("ld_power", [P, NT], F32))
        batch_in = [pr.sem(f"ld_batch_in{b}") for b in range(B)]
        ident_ready = pr.sem("ld_ident_in")
        stats_done = pr.sem("ld_stats_done")
        mv_done = pr.sem("ld_mv_done")
        ve_done = pr.sem("ld_ve_done")
        power_set = pr.sem("ld_power_set")
        block = ctx.enter_context(nc.Block())

        @block.sync
        def _(sp):
            for b in range(B):
                sp.dma_start(pr.x[:, bass.ts(b, NT), :],
                             x_in[b].rearrange("(t p) d -> p t d", p=P)).then_inc(batch_in[b], 16)
            sp.dma_start(pr.ident[:], ident_in).then_inc(ident_ready, 16)
            sp.wait_ge(ident_ready, 16)

        @block.vector
        def _(dve):
            for b in range(B):
                dve.wait_ge(batch_in[b], 16)
                for t in range(NT):
                    dve.bn_stats(stats[:, b, t, :], pr.x[:, b * NT + t, :]).then_inc(stats_done, 1)
                for t in range(NT):
                    dve.wait_ge(stats_done, b * NT + t + 1)
                    dve.bn_aggr(mv[:, b, t, :], stats[:, b, t, :]).then_inc(mv_done, 1)
                dve.wait_ge(mv_done, b * NT + NT)
                dve.tensor_copy(pr.mean[:, bass.ts(b, NT)], mv[:, b, :, 0])
                dve.tensor_scalar(ve[:, b, :], mv[:, b, :, 1], EPS, None, ALU.add).then_inc(ve_done, 1)

        @block.gpsimd
        def _(pool):
            pool.memset(pr.one[:], 1.0)
            pool.memset(power[:], -0.5).then_inc(power_set, 1)
            pool.wait_ge(power_set, 1)
            for b in range(B):
                pool.wait_ge(ve_done, b + 1)
                pool.tensor_tensor(pr.rstd[:, bass.ts(b, NT)], ve[:, b, :], power[:], ALU.pow)

        @block.scalar
        def _(act):
            pass

        @block.tensor
        def _(pe):
            pass


def attention_phase(pr, name, heads, ctxT_in, wqT_in, wk_in, wv_in, wo_in, bo_in):
    nc = pr.nc
    groups = heads // GH
    pairs = heads // 2
    bodies = B * groups // 2
    UB = 2 * NT
    preps_per_body = NT * (2 // groups)
    n = name

    def batch_of(it, p):
        return it * 2 + p if groups == 1 else it

    def group_of(p):
        return 0 if groups == 1 else p

    def prep_of(k):
        p, t = divmod(k, NT)
        if groups == 2 and p == 1:
            return None
        return k

    with ExitStack() as ctx:
        def sb(nm, shape, dt=F32):
            return ctx.enter_context(nc.sbuf_tensor(f"{n}.{nm}", shape, dt))

        def sem(nm):
            return pr.sem(f"{n}_{nm}")

        kT = sb("kT", [P, pairs, B * NC])
        vT = sb("vT", [P, pairs, B * NC])
        wqT = sb("wqT", [P, pairs, D])
        wo = sb("wo", [P, pairs, D])
        bo = sb("bo", [P, D])
        vdiag = sb("vdiag", [P, GP * (PW + 2 * NC)])
        kb = sb("kb", [P, GP, NC])
        g_hi = sb("g_hi", [P, 2, KD, GW], F32R)
        g_lo = sb("g_lo", [P, 2, KD, GW], F32R)
        v_hi = sb("v_hi", [P, 2, NCH, D], F32R)
        v_lo = sb("v_lo", [P, 2, NCH, D], F32R)
        xT_hi = sb("xT_hi", [P, KD, S], F32R)
        xT_lo = sb("xT_lo", [P, KD, S], F32R)
        ER = 4
        ex = sb("ex", [P, ER, PW])
        pT_hi = sb("pT_hi", [P, 2, PW], F32R)
        pT_lo = sb("pT_lo", [P, 2, PW], F32R)
        xn = sb("xn", [P, 2, D])
        mx = sb("mx", [P, 2, GH])
        sm = sb("sm", [P, 2, GH])
        rc = sb("rc", [P, 2, GH])
        stats = sb("stats", [P, NT, 6])
        mv = sb("mv", [P, NT, 2])
        ve = sb("ve", [P, NT])
        power = sb("power", [P, NT])

        wk = sb("wk", [CH, 2, heads * DH])
        wv = sb("wv", [CH, 2, heads * DH])
        cT = sb("ctxT", [CH, 2, B * NC])

        weights_in = sem("weights_in")
        proj_done, proj_copied = sem("proj_done"), sem("proj_copied")
        zeroed = sem("zeroed")
        misc_written, misc_hi, misc_free = sem("misc_written"), sem("misc_hi"), sem("misc_free")
        vdiag_ready, vdiag_used = sem("vdiag_ready"), sem("vdiag_used")
        xn_ready, bo_added = sem("xn_ready"), sem("bo_added")
        sc_done, max_done, sub_done = sem("scores_done"), sem("max_done"), sem("sub_done")
        exp_done, sum_done, rec_done, mul_done = sem("exp_done"), sem("sum_done"), sem("rec_done"), sem("mul_done")
        tr_done, pT_hi_done, pT_lo_done = sem("probsT_done"), sem("pT_hi_done"), sem("pT_lo_done")
        av_done, res_done = sem("av_done"), sem("res_done")
        stats_done, mv_done, ve_done = sem("stats_done"), sem("mv_done"), sem("ve_done")
        rstd_done = sem("rstd_done")

        score_bank = [[pr.bank[0], pr.bank[1]], [pr.bank[2], pr.bank[3]]]
        probT_bank = [pr.bank[4], pr.bank[5]]
        av_bank, misc_bank = pr.bank[6], pr.bank[7]
        CPB = 4

        SETUP_USES = 2 * KD + 3
        MISC_PER_BODY = 2 * SETUP_USES + preps_per_body

        def misc_setup(it, p, k):
            return it * MISC_PER_BODY + p * SETUP_USES + k

        def misc_prep(it, k):
            return it * MISC_PER_BODY + 2 * SETUP_USES + k

        def vdiag_rows(lo, off):
            v = vdiag[lo:lo + DH, :].rearrange("p (g z) -> p g z", g=GP)
            return v[:, :, off:off + NC]

        def misc_heads():
            return misc_bank[:, 0:HALF].rearrange("p (h j) -> p h j", h=GP)

        def heads_of(g, p, kd, odd):
            return g[:, p, kd, :].rearrange("p (h o j) -> p h o j", o=2, j=NC)[:, :, odd, :]

        AHEAD = 2
        block = ctx.enter_context(nc.Block())

        @block.sync
        def _(sp):
            for dst, src in ((cT[:], ctxT_in.rearrange("(c p) n -> p c n", p=CH)),
                             (wk[:], wk_in.rearrange("(c p) n -> p c n", p=CH)),
                             (wv[:], wv_in.rearrange("(c p) n -> p c n", p=CH)),
                             (wqT[:], wqT_in.rearrange("(c p) n -> p c n", p=P)),
                             (wo[:], wo_in.rearrange("(c p) n -> p c n", p=P)),
                             (bo[:], bo_in.to_broadcast([P, D]))):
                sp.dma_start(dst, src).then_inc(weights_in, 16)
            sp.wait_ge(weights_in, 96)

        @block.tensor
        def _(pe):
            pe.wait_ge(weights_in, 96)
            for j in range(2 * pairs):
                if j >= 4:
                    pe.wait_ge(proj_copied, j - 3)
                w = (wk if j < pairs else wv)[:, :, bass.ts(j % pairs, P)]
                for c in range(2):
                    mm = pe.matmul(pr.bank[j % 4][:, 0:B * NC], w[:, c, :], cT[:, c, :], start=(c == 0), stop=(c == 1))
                mm.then_inc(proj_done, 1)
            pe.wait_ge(proj_copied, 2 * pairs)

            def setup(it, p):
                b, g = batch_of(it, p), group_of(p)
                use = 0
                pe.wait_ge(vdiag_ready, it * 2 + p + 1)
                for hh in range(2):
                    for kd in range(KD):
                        pe.wait_ge(misc_free, misc_setup(it, p, use) + 1)
                        for h in range(hh, GH, 2):
                            lo = DH * hh
                            pair = g * GP + h // 2
                            mm = pe.matmul(misc_bank[:, bass.ts(h // 2, NC)],
                                           wqT[lo:lo + DH, pair, bass.ts(kd, P)],
                                           kb[lo:lo + DH, h // 2, :], start=True, stop=True)
                        mm.then_inc(misc_written, 1)
                        use += 1
                for c0 in range(0, NCH, 2):
                    pe.wait_ge(misc_free, misc_setup(it, p, use) + 1)
                    for c in range(c0, min(c0 + 2, NCH)):
                        inside = [q for q in range(GP) if q * 2 * NC < (c + 1) * P and (q + 1) * 2 * NC > c * P]
                        for q in inside:
                            mm = pe.matmul(misc_bank[:, bass.ts(c - c0, D)], vdiag[:, q * PW + c * P:q * PW + c * P + P],
                                           wo[:, g * GP + q, :], start=(q == inside[0]), stop=(q == inside[-1]))
                    mm.then_inc(misc_written, 1)
                    use += 1

            def prep(it, k):
                cnt = it * preps_per_body + k
                pe.wait_ge(xn_ready, cnt + 1)
                pe.wait_ge(misc_free, misc_prep(it, k) + 1)
                for kd in range(KD):
                    mm = pe.transpose(misc_bank[:, bass.ts(kd, P)], xn[:, k % 2, bass.ts(kd, P)], pr.ident[:])
                mm.then_inc(misc_written, 1)

            def scores(it, k):
                u = it * UB + k
                p, t = divmod(k, NT)
                pe.wait_ge(sub_done, u + 1)
                if prep_of(k) is not None:
                    pe.wait_ge(misc_free, misc_prep(it, prep_of(k)) + 2)
                for half in range(2):
                    cols = bass.ts(half, HALF)
                    i = 0
                    for kd in range(KD):
                        for xt, gm in ((xT_hi, g_hi), (xT_lo, g_hi), (xT_hi, g_lo)):
                            mm = pe.matmul(score_bank[k % 2][half][:, 0:HALF], xt[:, kd, bass.ts(t, P)],
                                           gm[:, p, kd, cols], start=(i == 0), stop=(i == 3 * KD - 1))
                            i += 1
                mm.then_inc(sc_done, 1)

            def probs_transpose(it, k):
                u = it * UB + k
                pe.wait_ge(mul_done, u + 1)
                pe.wait_ge(pT_lo_done, u + 1)
                for c in range(NCH):
                    bk = probT_bank[c // CPB]
                    mm = pe.transpose(bk[:, bass.ts(c % CPB, P)], ex[:, k % ER, bass.ts(c, P)], pr.ident[:])
                mm.then_inc(tr_done, 1)

            def attend(it, k):
                u = it * UB + k
                p = k // NT
                pe.wait_ge(pT_lo_done, u + 2)
                pe.wait_ge(res_done, u + 1)
                i = 0
                for c in range(NCH):
                    for pt, vm in ((pT_hi, v_hi), (pT_lo, v_hi), (pT_hi, v_lo)):
                        mm = pe.matmul(av_bank[:, 0:D], pt[:, k % 2, bass.ts(c, P)], vm[:, p, c, :],
                                       start=(i == 0), stop=(i == 3 * NCH - 1))
                        i += 1
                mm.then_inc(av_done, 1)

            with pe.Fori(0, bodies) as it:
                setup(it, 0)
                setup(it, 1)
                for k in range(AHEAD):
                    prep(it, k)
                for k in range(UB + 3):
                    if k < UB:
                        scores(it, k)
                        if k + AHEAD < preps_per_body:
                            prep(it, k + AHEAD)
                    if 2 <= k < UB + 2:
                        probs_transpose(it, k - 2)
                    if k >= 3:
                        attend(it, k - 3)

        @block.scalar
        def _(act):
            for j in range(2 * pairs):
                act.wait_ge(proj_done, j + 1)
                dst = (kT if j < pairs else vT)[:, j % pairs, :]
                act.activation(dst, pr.bank[j % 4][:, 0:B * NC], ACT.Copy).then_inc(proj_copied, 1)

            def setup(it, p):
                use = 0
                for hh in range(2):
                    for kd in range(KD):
                        act.wait_ge(misc_written, misc_setup(it, p, use) + 1)
                        if use == 0:
                            act.wait_ge(av_done, it * UB + 2)
                        act.activation(heads_of(g_hi, p, kd, hh), misc_heads(), ACT.Copy,
                                       scale=float(DH) ** -0.5).then_inc(misc_hi, 1)
                        use += 1
                for c0 in range(0, NCH, 2):
                    m = min(2, NCH - c0)
                    act.wait_ge(misc_written, misc_setup(it, p, use) + 1)
                    act.activation(v_hi[:, p, c0:c0 + m, :].rearrange("p c d -> p (c d)"), misc_bank[:, 0:m * D],
                                   ACT.Copy).then_inc(misc_hi, 1)
                    use += 1

            def prep(it, k):
                act.wait_ge(misc_written, misc_prep(it, k) + 1)
                act.activation(xT_hi[:, :, bass.ts(k % NT, P)], misc_bank[:, 0:D].rearrange("p (c t) -> p c t", c=KD),
                               ACT.Copy).then_inc(misc_hi, 1)

            def exp(it, k):
                u = it * UB + k
                act.wait_ge(sub_done, u + 3)
                act.activation(ex[:, k % ER, 0:GW], ex[:, k % ER, 0:GW], ACT.Exp).then_inc(exp_done, 1)

            def probT_hi(it, k):
                u = it * UB + k
                act.wait_ge(tr_done, u + 1 + ER)
                act.wait_ge(av_done, u + 1)
                act.activation(pT_hi[:, k % 2, 0:CPB * P], probT_bank[0][:], ACT.Copy)
                act.activation(pT_hi[:, k % 2, CPB * P:PW], probT_bank[1][:, 0:PW - CPB * P],
                               ACT.Copy).then_inc(pT_hi_done, 1)

            act.wait_ge(zeroed, 2)
            act.sem_inc(av_done, 2)
            with act.Fori(0, bodies) as it:
                setup(it, 0)
                setup(it, 1)
                for k in range(AHEAD):
                    prep(it, k)
                for k in range(UB + 3):
                    if k < UB:
                        exp(it, k)
                        if k + AHEAD < preps_per_body:
                            prep(it, k + AHEAD)
                    if 2 <= k < UB + 2:
                        probT_hi(it, k - 2)

        @block.vector
        def _(dve):
            dve.memset(vdiag[:], 0.0).then_inc(zeroed, 1)
            dve.memset(ex[:, :, GW:PW], 0.0).then_inc(zeroed, 1)
            dve.sem_inc(sub_done, 2)
            dve.sem_inc(tr_done, ER)
            dve.sem_inc(pT_lo_done, 1)
            dve.sem_inc(res_done, 1)
            dve.sem_inc(misc_free, 1)
            dve.wait_ge(zeroed, 2)
            dve.wait_ge(proj_copied, 2 * pairs)

            def setup(it, p):
                b, g = batch_of(it, p), group_of(p)
                pr.wait_apart(dve, misc_free, misc_setup(it, p, 0) + 1)
                for odd in range(2):
                    lo = DH * odd
                    cp = dve.tensor_copy(vdiag_rows(lo, NC * odd), vT[lo:lo + DH, g * GP:(g + 1) * GP, bass.ts(b, NC)])
                cp = dve.tensor_copy(kb[:], kT[:, g * GP:(g + 1) * GP, bass.ts(b, NC)])
                cp.then_inc(vdiag_ready, 1)
                use = 0
                for hh in range(2):
                    for kd in range(KD):
                        dve.wait_ge(misc_hi, misc_setup(it, p, use) + 1)
                        dve.scalar_tensor_tensor(out=heads_of(g_lo, p, kd, hh), in0=misc_heads(),
                                                 scalar=float(DH) ** -0.5, in1=heads_of(g_hi, p, kd, hh).bitcast(F32),
                                                 op0=ALU.mult, op1=ALU.subtract).then_inc(misc_free, 1)
                        use += 1
                for c0 in range(0, NCH, 2):
                    m = min(2, NCH - c0)
                    dve.wait_ge(misc_hi, misc_setup(it, p, use) + 1)
                    dve.tensor_tensor(v_lo[:, p, c0:c0 + m, :].rearrange("p c d -> p (c d)"), misc_bank[:, 0:m * D],
                                      v_hi[:, p, c0:c0 + m, :].bitcast(F32).rearrange("p c d -> p (c d)"),
                                      ALU.subtract).then_inc(misc_free, 1)
                    use += 1

            def normalise(it, k):
                cnt = it * preps_per_body + k
                p, t = divmod(k, NT)
                b = batch_of(it, p)
                dve.wait_ge(misc_free, misc_prep(it, k))
                dve.tensor_scalar(xn[:, k % 2, :], pr.x[:, b * NT + t, :], pr.mean[:, bass.ds(b * NT + t, 1)],
                                  pr.rstd[:, bass.ds(b * NT + t, 1)], ALU.subtract, ALU.mult).then_inc(xn_ready, 1)

            def prep_lo(it, k):
                dve.wait_ge(misc_hi, misc_prep(it, k) + 1)
                cols = bass.ts(k % NT, P)
                dve.tensor_tensor(xT_lo[:, :, cols], misc_bank[:, 0:D].rearrange("p (c t) -> p c t", c=KD),
                                  xT_hi[:, :, cols].bitcast(F32), ALU.subtract).then_inc(misc_free, 1)

            def score_max(it, k):
                u = it * UB + k
                dve.wait_ge(sc_done, u + 1)
                for half in range(2):
                    rd = dve.tensor_reduce(mx[:, k % 2, bass.ts(half, GH // 2)],
                                           score_bank[k % 2][half][:, 0:HALF].rearrange("p (h j) -> p h j", h=GH // 2),
                                           AX_X, ALU.max)
                rd.then_inc(max_done, 1)

            def score_sub(it, k):
                u = it * UB + k
                dve.wait_ge(max_done, u + 1)
                dve.wait_ge(tr_done, u + 1)
                for half in range(2):
                    m = mx[:, k % 2, bass.ts(half, GH // 2)].unsqueeze(2).to_broadcast([P, GH // 2, NC])
                    ss = dve.tensor_tensor(ex[:, k % ER, bass.ts(half, HALF)].rearrange("p (h j) -> p h j", h=GH // 2),
                                           score_bank[k % 2][half][:, 0:HALF].rearrange("p (h j) -> p h j", h=GH // 2),
                                           m, ALU.subtract)
                ss.then_inc(sub_done, 1)

            def exp_sum(it, k):
                u = it * UB + k
                dve.wait_ge(exp_done, u + 1)
                dve.tensor_reduce(sm[:, k % 2, :], ex[:, k % ER, 0:GW].rearrange("p (h j) -> p h j", h=GH),
                                  AX_X, ALU.add).then_inc(sum_done, 1)

            def exp_rec(it, k):
                u = it * UB + k
                dve.wait_ge(sum_done, u + 1)
                dve.reciprocal(rc[:, k % 2, :], sm[:, k % 2, :]).then_inc(rec_done, 1)

            def probT_lo(it, k):
                u = it * UB + k
                dve.wait_ge(pT_hi_done, u + 1)
                dve.tensor_tensor(pT_lo[:, k % 2, 0:CPB * P], probT_bank[0][:], pT_hi[:, k % 2, 0:CPB * P].bitcast(F32),
                                  ALU.subtract)
                dve.tensor_tensor(pT_lo[:, k % 2, CPB * P:PW], probT_bank[1][:, 0:PW - CPB * P],
                                  pT_hi[:, k % 2, CPB * P:PW].bitcast(F32), ALU.subtract).then_inc(pT_lo_done, 1)

            def residual(it, k):
                u = it * UB + k
                p, t = divmod(k, NT)
                b = batch_of(it, p)
                dve.wait_ge(av_done, u + 3)
                if prep_of(k) is not None:
                    dve.wait_ge(bo_added, it * preps_per_body + k + 1)
                dve.tensor_tensor(pr.x[:, b * NT + t, :], pr.x[:, b * NT + t, :], av_bank[:, 0:D],
                                  ALU.add).then_inc(res_done, 1)

            def batch_stats(it, p):
                b = batch_of(it, p)
                done = it * (2 // groups) + (p if groups == 1 else 0)
                pr.wait_apart(dve, rstd_done, done + 1)
                pr.wait_apart(dve, res_done, it * UB + (p + 1) * NT + 1)
                for t in range(NT):
                    dve.bn_stats(stats[:, t, :], pr.x[:, b * NT + t, :]).then_inc(stats_done, 1)
                pr.wait_apart(dve, stats_done, done * NT + NT)
                for t in range(NT):
                    dve.bn_aggr(mv[:, t, :], stats[:, t, :]).then_inc(mv_done, 1)
                pr.wait_apart(dve, mv_done, done * NT + NT)
                dve.tensor_copy(pr.mean[:, bass.ts(b, NT)], mv[:, :, 0])
                dve.tensor_scalar(ve[:], mv[:, :, 1], EPS, None, ALU.add).then_inc(ve_done, 1)

            with dve.Fori(0, bodies) as it:
                setup(it, 0)
                setup(it, 1)
                for k in range(AHEAD):
                    normalise(it, k)
                for k in range(AHEAD):
                    prep_lo(it, k)
                for k in range(UB + 4):
                    if k >= 4:
                        residual(it, k - 4)
                    if k < UB and k + AHEAD < preps_per_body:
                        normalise(it, k + AHEAD)
                    if k < UB:
                        score_max(it, k)
                        score_sub(it, k)
                    if 1 <= k <= UB:
                        exp_sum(it, k - 1)
                        exp_rec(it, k - 1)
                    if k < UB and k + AHEAD < preps_per_body:
                        prep_lo(it, k + AHEAD)
                    if 2 <= k < UB + 2:
                        probT_lo(it, k - 2)
                    if groups == 1 and k == NT + 3:
                        batch_stats(it, 0)
                batch_stats(it, 1)

        @block.gpsimd
        def _(pool):
            pool.memset(power[:], -0.5).then_inc(rstd_done, 1)
            pool.wait_ge(rstd_done, 1)
            pool.wait_ge(weights_in, 96)

            def normalise_probs(it, k):
                u = it * UB + k
                pool.wait_ge(rec_done, u + 1)
                e3 = ex[:, k % ER, 0:GW].rearrange("p (h j) -> p h j", h=GH)
                pool.tensor_tensor(e3, e3, rc[:, k % 2, :].unsqueeze(2).to_broadcast([P, GH, NC]),
                                   ALU.mult).then_inc(mul_done, 1)

            def add_bo(it, k):
                cnt = it * preps_per_body + k
                p, t = divmod(k, NT)
                b = batch_of(it, p)
                pr.wait_apart(pool, xn_ready, cnt + 1)
                pool.tensor_tensor(pr.x[:, b * NT + t, :], pr.x[:, b * NT + t, :], bo[:], ALU.add).then_inc(bo_added, 1)

            def rstd(it, p):
                b = batch_of(it, p)
                done = it * (2 // groups) + (p if groups == 1 else 0)
                pr.wait_apart(pool, ve_done, done + 1)
                pool.tensor_tensor(pr.rstd[:, bass.ts(b, NT)], ve[:], power[:], ALU.pow).then_inc(rstd_done, 1)

            with pool.Fori(0, bodies) as it:
                for k in range(AHEAD):
                    add_bo(it, k)
                for k in range(UB + 4):
                    if 1 <= k <= UB:
                        normalise_probs(it, k - 1)
                    if k < UB and k + AHEAD < preps_per_body:
                        add_bo(it, k + AHEAD)
                    if groups == 1 and k == NT + 3:
                        rstd(it, 0)
                rstd(it, 1)


def router_phase(pr, gate_in, b2_in, iota_in):
    nc = pr.nc
    with ExitStack() as ctx:
        def sb(nm, shape, dt=F32):
            return ctx.enter_context(nc.sbuf_tensor(f"rt.{nm}", shape, dt))

        def sem(nm):
            return pr.sem(f"rt_{nm}")

        XR = 4
        STEPS = 8 + 4 * B
        xn = sb("xn", [P, XR, D])
        ones = sb("ones", [P, 1])
        gate = sb("gate", [P, KD, E0])
        b2 = sb("b2", [E0, D])
        iota = sb("iota", [P, E0])
        meanT = sb("meanT", [P, B, KD, P])
        top = sb("top", [P, B, 8])
        neg = sb("neg", [P, B])
        ez = sb("ez", [P, B, E0])
        tot = sb("tot", [P, B])
        rtot = sb("rtot", [P, B])
        probs = sb("probs", [P, B, E0])
        topi = sb("topi", [P, B, 8])
        pair = sb("pair", [P, B])
        rpair = sb("rpair", [P, B])
        hit = sb("hit", [P, B, TOPK0, E0])
        comb = sb("comb", [P, B, E0])
        combT = sb("combT", [E0, B, P])
        const_in, ones_set = sem("const_in"), sem("ones_set")
        xn_ready, summed = sem("xn_ready"), sem("summed")
        mean_copied, logits_done = sem("mean_copied"), sem("logits_done")
        step, exp_done = sem("step"), sem("exp_done")
        combT_done, combT_copied, bias_done = sem("combT_done"), sem("combT_copied"), sem("bias_done")
        mean_bank, logit_bank, comb_bank = pr.bank[0], pr.bank[1], pr.bank[2]
        bias_bank = [pr.bank[3], pr.bank[4]]
        block = ctx.enter_context(nc.Block())

        @block.sync
        def _(sp):
            sp.dma_start(gate[:], gate_in.rearrange("(c p) e -> p c e", p=P)).then_inc(const_in, 16)
            sp.dma_start(b2[:], b2_in).then_inc(const_in, 16)
            sp.dma_start(iota[:], iota_in).then_inc(const_in, 16)
            sp.wait_ge(const_in, 48)

        @block.tensor
        def _(pe):
            pe.wait_ge(ones_set, 1)
            for b in range(B):
                for t in range(NT):
                    i = b * NT + t
                    pe.wait_ge(xn_ready, i + 1)
                    for kd in range(KD):
                        mm = pe.matmul(mean_bank[:, b * KD + kd:b * KD + kd + 1], xn[:, i % XR, bass.ts(kd, P)], ones[:],
                                       start=(i == 0 and kd == 0), stop=(t == NT - 1), skip_group_check=True)
                    mm.then_inc(summed, 1)
            pe.wait_ge(mean_copied, 1)
            pe.wait_ge(const_in, 48)
            for b in range(B):
                for kd in range(KD):
                    mm = pe.matmul(logit_bank[:, bass.ts(b, E0)], meanT[:, b, kd, :], gate[:, kd, :],
                                   start=(kd == 0), stop=(kd == KD - 1))
            mm.then_inc(logits_done, 1)
            pe.wait_ge(step, STEPS)
            for b in range(B):
                mm = pe.transpose(comb_bank[0:E0, bass.ts(b, P)], comb[:, b, :], pr.ident[:])
            mm.then_inc(combT_done, 1)
            pe.wait_ge(combT_copied, 1)
            for b in range(B):
                mm = pe.matmul(bias_bank[b // 2][:, bass.ts(b % 2, D)], combT[:, b, :], b2[:], start=True, stop=True)
            mm.then_inc(bias_done, 1)

        @block.vector
        def _(dve):
            dve.memset(ones[:], 1.0).then_inc(ones_set, 1)
            for i in range(B * NT):
                if i >= XR:
                    dve.wait_ge(summed, i - XR + 1)
                dve.tensor_scalar(xn[:, i % XR, :], pr.x[:, i, :], pr.mean[:, i:i + 1], pr.rstd[:, i:i + 1],
                                  ALU.subtract, ALU.mult).then_inc(xn_ready, 1)
            dve.wait_ge(summed, B * NT)
            dve.tensor_scalar(meanT[:].rearrange("p b k m -> p (b k) m"),
                              mean_bank[:, 0:B * KD].unsqueeze(2).to_broadcast([P, B * KD, P]), 1.0 / S, None,
                              ALU.mult).then_inc(mean_copied, 1)
            dve.wait_ge(logits_done, 1)
            lg = logit_bank[:, 0:B * E0].rearrange("p (b e) -> p b e", b=B)
            count = [0]

            def then(ins):
                count[0] += 1
                ins.then_inc(step, 1)
                dve.wait_ge(step, count[0])

            def each(n):
                return n.unsqueeze(2).to_broadcast([P, B, E0])

            then(dve.tensor_reduce(neg[:], lg, AX_X, ALU.max))
            then(dve.tensor_tensor(ez[:], lg, each(neg[:]), ALU.subtract))
            dve.wait_ge(exp_done, 1)
            then(dve.tensor_reduce(tot[:], ez[:], AX_X, ALU.add))
            then(dve.reciprocal(rtot[:], tot[:]))
            then(dve.tensor_tensor(probs[:], ez[:], each(rtot[:]), ALU.mult))
            for b in range(B):
                then(dve.max(top[:, b, :], probs[:, b, :]))
                then(dve.max_index(pr.route_i[:, b, :], top[:, b, :], probs[:, b, :]))
            then(dve.tensor_copy(topi[:], pr.route_i[:]))
            then(dve.tensor_tensor(pair[:], top[:, :, 0], top[:, :, 1], ALU.add))
            then(dve.reciprocal(rpair[:], pair[:]))
            dve.tensor_tensor(pr.route_w[:], top[:, :, 0:TOPK0], rpair[:].unsqueeze(2).to_broadcast([P, B, TOPK0]),
                              ALU.mult).then_inc(bias_done, 2)
            dve.wait_ge(bias_done, 2)
            for b in range(B):
                dve.tensor_scalar(hit[:, b, 0, :], iota[:], topi[:, b, 0:1], pr.route_w[:, b, 0:1], ALU.is_equal, ALU.mult)
                then(dve.tensor_scalar(hit[:, b, 1, :], iota[:], topi[:, b, 1:2], pr.route_w[:, b, 1:2],
                                       ALU.is_equal, ALU.mult))
                then(dve.tensor_tensor(comb[:, b, :], hit[:, b, 0, :], hit[:, b, 1, :], ALU.add))
            assert count[0] == STEPS, count
            dve.wait_ge(combT_done, 1)
            dve.tensor_copy(combT[:].rearrange("e b p -> e (b p)"), comb_bank[0:E0, 0:B * P]).then_inc(combT_copied, 1)
            dve.wait_ge(bias_done, 3)
            for h in range(2):
                dve.tensor_copy(pr.ffn_bias[:, 2 * h:2 * h + 2, :].rearrange("p b d -> p (b d)"), bias_bank[h][:])

        @block.scalar
        def _(act):
            act.wait_ge(step, 2)
            act.activation(ez[:], ez[:], ACT.Exp).then_inc(exp_done, 1)

        @block.gpsimd
        def _(pool):
            pass


def ffn0_phase(pr, w1_in, b1_in, w2_in):
    nc = pr.nc
    JOBS = TOPK0
    SP_PIECES = 8
    W1C = KD * F0
    WC = W1C + FT * D
    PIECE = WC // SP_PIECES
    HT = JOBS * NCK * FT
    with ExitStack() as ctx:
        def sb(nm, shape, dt=F32):
            return ctx.enter_context(nc.sbuf_tensor(f"f0.{nm}", shape, dt))

        def sem(nm):
            return pr.sem(f"f0_{nm}")

        raw = sb("raw", [P, WC])
        w_hi = sb("w_hi", [P, JOBS, WC], F32R)
        w_lo = sb("w_lo", [P, JOBS, WC], F32R)
        b1 = sb("b1", [P, JOBS, FT])
        xT_hi = sb("xT_hi", [P, KD, S], F32R)
        xT_lo = sb("xT_lo", [P, KD, S], F32R)
        xn = sb("xn", [P, 2, D])
        hid = sb("hid", [P, 2, CHK])
        h_hi = sb("h_hi", [P, 2, CHK], F32R)
        h_lo = sb("h_lo", [P, 2, CHK], F32R)
        stats = sb("stats", [P, NT, 6])
        mv = sb("mv", [P, NT, 2])
        ve = sb("ve", [P, NT])
        power = sb("power", [P, NT])
        raw_in, raw_hi, raw_free, b1_in_done = sem("raw_in"), sem("raw_hi"), sem("raw_free"), sem("b1_in")
        xn_ready, bias_added = sem("xn_ready"), sem("bias_added")
        xT_written, xT_hi_done, xT_lo_done = sem("xT_written"), sem("xT_hi_done"), sem("xT_lo_done")
        h_done, gelu_done, h_hi_done, h_lo_done = sem("h_done"), sem("gelu_done"), sem("h_hi_done"), sem("h_lo_done")
        y_step, y_read = sem("y_step"), sem("y_read")
        stats_done, mv_done, ve_done, rstd_done = sem("stats_done"), sem("mv_done"), sem("ve_done"), sem("rstd_done")
        h_bank = [pr.bank[0], pr.bank[1]]
        y_bank = pr.bank[2:6]
        t_bank = [pr.bank[6], pr.bank[7]]
        block = ctx.enter_context(nc.Block())

        def w1_of(w, j, kd, f):
            return w[:, j, kd * F0 + f * P:kd * F0 + f * P + P]

        def w2_of(w, j, f):
            return w[:, j, W1C + f * D:W1C + f * D + D]

        @block.sync
        def _(sp):
            with sp.Fori(0, B) as b:
                for j in range(JOBS):
                    e = sp.value_load(pr.route_i[0:1, b, j:j + 1], min_val=0, max_val=E0 - 1)
                    sp.wait_ge(raw_free, b * (JOBS * SP_PIECES) + j * SP_PIECES + 1)
                    sp.dma_start(raw[:, 0:W1C].rearrange("p (c f) -> p c f", c=KD),
                                 w1_in[bass.ds(e, 1)].rearrange("o (c p) f -> p (o c) f", p=P)).then_inc(raw_in, 16)
                    sp.dma_start(raw[:, W1C:WC].rearrange("p (c d) -> p c d", c=FT),
                                 w2_in[bass.ds(e, 1)].rearrange("o (c p) d -> p (o c) d", p=P)).then_inc(raw_in, 16)
                    sp.wait_ge(gelu_done, b * HT + 2)
                    sp.dma_start(b1[:, j, :], b1_in[bass.ds(e, 1)].rearrange("o p f -> p (o f)")).then_inc(b1_in_done, 16)
            sp.wait_ge(raw_in, 32 * JOBS * B)
            sp.wait_ge(b1_in_done, 16 * JOBS * B)

        @block.tensor
        def _(pe):
            def prep(b, t):
                pe.wait_ge(xn_ready, b * NT + t + 1)
                pe.wait_ge(xT_lo_done, b * NT + t + 1)
                for kd in range(KD):
                    mm = pe.transpose(t_bank[t % 2][:, bass.ts(kd, P)], xn[:, t % 2, bass.ts(kd, P)], pr.ident[:])
                mm.then_inc(xT_written, 1)

            def hidden(b, i):
                j, c, f = i // (NCK * FT), i // FT % NCK, i % FT
                if i % (NCK * FT) == 0:
                    pe.wait_ge(raw_free, b * (JOBS * SP_PIECES) + (j + 1) * SP_PIECES + 1)
                if j == 0 and f == 0:
                    pe.wait_ge(xT_lo_done, b * NT + (c + 1) * TPC + 2)
                pe.wait_ge(gelu_done, b * HT + i + 1)
                n = 0
                for kd in range(KD):
                    for wt, xt in ((w_hi, xT_hi), (w_hi, xT_lo), (w_lo, xT_hi)):
                        mm = pe.matmul(h_bank[i % 2][:], w1_of(wt, j, kd, f), xt[:, kd, bass.ts(c, CHK)],
                                       start=(n == 0), stop=(n == 3 * KD - 1))
                        n += 1
                mm.then_inc(h_done, 1)

            def output(b, i):
                j, c, f = i // (NCK * FT), i // FT % NCK, i % FT
                pe.wait_ge(h_lo_done, b * HT + i + 3)
                for t in range(TPC):
                    if f == 0:
                        pe.wait_ge(y_read, b * (HT // FT * TPC) + (i // FT) * TPC + t - TPC + 1 + TPC)
                    n = 0
                    for ht, wt in ((h_hi, w_hi), (h_lo, w_hi), (h_hi, w_lo)):
                        mm = pe.matmul(y_bank[t][:, 0:D], ht[:, i % 2, bass.ts(t, P)], w2_of(wt, j, f),
                                       start=(f == 0 and n == 0), stop=(f == FT - 1 and n == 2))
                        n += 1
                mm.then_inc(y_step, 1)

            with pe.Fori(0, B) as b:
                for t in range(NT):
                    prep(b, t)
                for i in range(HT + 1):
                    if i < HT:
                        hidden(b, i)
                    if i >= 1:
                        output(b, i - 1)

        @block.scalar
        def _(act):
            def split_hi(b, piece):
                j, q = divmod(piece, SP_PIECES)
                if q == 0:
                    act.wait_ge(raw_in, b * (32 * JOBS) + 32 * (j + 1))
                    act.wait_ge(y_step, b * HT + 2)
                act.activation(w_hi[:, j, bass.ts(q, PIECE)], raw[:, bass.ts(q, PIECE)], ACT.Copy).then_inc(raw_hi, 1)

            def prep(b, t):
                act.wait_ge(xT_written, b * NT + t + 1)
                act.activation(xT_hi[:, :, bass.ts(t, P)], t_bank[t % 2][:, 0:D].rearrange("p (c t) -> p c t", c=KD),
                               ACT.Copy).then_inc(xT_hi_done, 1)

            def gelu(b, i):
                j, f = i // (NCK * FT), i % FT
                act.wait_ge(h_done, b * HT + i + 1)
                act.wait_ge(h_lo_done, b * HT + i + 1)
                if i == 0:
                    act.wait_ge(b1_in_done, b * (16 * JOBS) + 16 * JOBS)
                act.activation(hid[:, i % 2, :], h_bank[i % 2][:], ACT.Gelu, bias=b1[:, j, f:f + 1]).then_inc(gelu_done, 1)

            with act.Fori(0, B) as b:
                for t in range(NT):
                    prep(b, t)
                for q in range(SP_PIECES):
                    split_hi(b, q)
                for i in range(HT):
                    gelu(b, i)
                    if i < SP_PIECES:
                        split_hi(b, SP_PIECES + i)

        @block.vector
        def _(dve):
            dve.sem_inc(raw_free, 1)
            dve.sem_inc(xT_lo_done, 2)
            dve.sem_inc(gelu_done, 2)
            dve.sem_inc(h_lo_done, 2)
            dve.sem_inc(y_read, TPC)
            dve.sem_inc(y_step, 2)

            def normalise(b, t):
                dve.wait_ge(xT_written, b * NT + t - 1) if t >= 2 else None
                col = bass.ds(b * NT + t, 1)
                dve.tensor_scalar(xn[:, t % 2, :], pr.x[:, b * NT + t, :], pr.mean[:, col], pr.rstd[:, col],
                                  ALU.subtract, ALU.mult).then_inc(xn_ready, 1)

            def prep_lo(b, t):
                dve.wait_ge(xT_hi_done, b * NT + t + 1)
                cols = bass.ts(t, P)
                dve.tensor_tensor(xT_lo[:, :, cols], t_bank[t % 2][:, 0:D].rearrange("p (c t) -> p c t", c=KD),
                                  xT_hi[:, :, cols].bitcast(F32), ALU.subtract).then_inc(xT_lo_done, 1)

            def split_lo(b, piece):
                j, q = divmod(piece, SP_PIECES)
                dve.wait_ge(raw_hi, b * (JOBS * SP_PIECES) + piece + 1)
                cols = bass.ts(q, PIECE)
                dve.tensor_tensor(w_lo[:, j, cols], raw[:, cols], w_hi[:, j, cols].bitcast(F32),
                                  ALU.subtract).then_inc(raw_free, 1)

            def split_hidden(b, i):
                dve.wait_ge(gelu_done, b * HT + i + 3)
                dve.wait_ge(y_step, b * HT + i + 1)
                dve.tensor_copy(h_hi[:, i % 2, :], hid[:, i % 2, :]).then_inc(h_hi_done, 1)
                dve.wait_ge(h_hi_done, b * HT + i + 1)
                dve.tensor_tensor(h_lo[:, i % 2, :], hid[:, i % 2, :], h_hi[:, i % 2, :].bitcast(F32),
                                  ALU.subtract).then_inc(h_lo_done, 1)

            def residual(b, i):
                j, c = i // (NCK * FT), i // FT % NCK
                dve.wait_ge(y_step, b * HT + i + 3)
                for t in range(TPC):
                    xt = pr.x[:, b * NT + c * TPC + t, :]
                    if j == 0:
                        dve.wait_ge(bias_added, b * NT + c * TPC + t + 1)
                    elif t == 0:
                        dve.wait_ge(y_read, b * (JOBS * NCK * TPC) + TPC * (NCK + c + 1))
                    dve.scalar_tensor_tensor(out=xt, in0=y_bank[t][:, 0:D], scalar=pr.route_w[:, b, j:j + 1], in1=xt,
                                             op0=ALU.mult, op1=ALU.add).then_inc(y_read, 1)

            def batch_stats(b):
                pr.wait_apart(dve, rstd_done, b + 1)
                pr.wait_apart(dve, y_read, (b + 1) * (JOBS * NCK * TPC) + TPC)
                for t in range(NT):
                    dve.bn_stats(stats[:, t, :], pr.x[:, b * NT + t, :]).then_inc(stats_done, 1)
                pr.wait_apart(dve, stats_done, b * NT + NT)
                for t in range(NT):
                    dve.bn_aggr(mv[:, t, :], stats[:, t, :]).then_inc(mv_done, 1)
                pr.wait_apart(dve, mv_done, b * NT + NT)
                dve.tensor_copy(pr.mean[:, bass.ts(b, NT)], mv[:, :, 0])
                dve.tensor_scalar(ve[:], mv[:, :, 1], EPS, None, ALU.add).then_inc(ve_done, 1)

            with dve.Fori(0, B) as b:
                for t in range(NT):
                    normalise(b, t)
                    if t >= 1:
                        prep_lo(b, t - 1)
                prep_lo(b, NT - 1)
                for q in range(SP_PIECES):
                    split_lo(b, q)
                for i in range(HT + 1):
                    if i < HT:
                        split_hidden(b, i)
                        if i < SP_PIECES:
                            split_lo(b, SP_PIECES + i)
                    if i >= 1 and i % FT == 0:
                        residual(b, i - 1)
                batch_stats(b)

        @block.gpsimd
        def _(pool):
            pool.memset(power[:], -0.5).then_inc(rstd_done, 1)
            pool.wait_ge(rstd_done, 1)
            with pool.Fori(0, B) as b:
                for t in range(NT):
                    pr.wait_apart(pool, xn_ready, b * NT + t + 1)
                    xt = pr.x[:, b * NT + t, :]
                    pool.tensor_tensor(xt, xt, pr.ffn_bias[:, b, :], ALU.add).then_inc(bias_added, 1)
                pr.wait_apart(pool, ve_done, b + 1)
                pool.tensor_tensor(pr.rstd[:, bass.ts(b, NT)], ve[:], power[:], ALU.pow).then_inc(rstd_done, 1)


def expert_choice_phase(pr, y_out, xn_dram, wg_in, bg_in, w1_in, b1_in, w2_in, b2_in, w3_in, b3_in):
    nc = pr.nc
    Q = B // 2
    ER = 32
    WC = 3 * KD * D
    GT = Q * P
    with ExitStack() as outer:
        def osb(nm, shape, dt=F32):
            return outer.enter_context(nc.sbuf_tensor(f"f1.{nm}", shape, dt))

        rows = osb("rows", [P, Q, E1], U32)
        gatew = osb("gatew", [P, Q, E1])
        with ExitStack() as ctx:
            def sb(nm, shape, dt=F32):
                return ctx.enter_context(nc.sbuf_tensor(f"f1c.{nm}", shape, dt))

            def sem(nm):
                return pr.sem(f"f1c_{nm}")

            XR = 8
            xn = sb("xn", [P, XR, D])
            xT = sb("xT", [P, 2, KD, CHK])
            wg = sb("wg", [P, KD, ER])
            bg = sb("bg", [P, 1])
            lg = sb("lg", [P, S])
            ex = sb("ex", [P, S])
            vals = sb("vals", [P, K1])
            idx = sb("idx", [P, K1], U32)
            first_row = sb("first_row", [P, 1])
            nmax = sb("nmax", [P, 1])
            tot = sb("tot", [P, 1])
            rtot = sb("rtot", [P, 1])
            idxf = sb("idxf", [P, 2, K1])
            ev = sb("ev", [P, K1])
            pv = sb("pv", [P, 2, K1])
            const_in, row_set = sem("const_in"), sem("row_set")
            xn_ready, xn_sent = sem("xn_ready"), [sem(f"xn_sent{i}") for i in range(XR)]
            tr_done, xT_copied, logits_done = sem("tr_done"), sem("xT_copied"), sem("logits_done")
            step, nmax_done, exp_done, ev_done, pv_done = sem("step"), sem("nmax_done"), sem("exp_done"), sem("ev_done"), sem("pv_done")
            turned, x_written = sem("turned"), sem("x_written")
            idx_ready = sem("idx_ready")
            lg_bank = [pr.bank[0], pr.bank[1]]
            t_bank = [pr.bank[2], pr.bank[3]]
            i_bank, v_bank = pr.bank[4], pr.bank[5]
            NCH8 = B * NCK
            block = ctx.enter_context(nc.Block())

            @block.sync
            def _(sp):
                sp.dma_start(wg[:], wg_in.rearrange("(c p) e -> p c e", p=P)).then_inc(const_in, 16)
                sp.dma_start(bg[:], bg_in).then_inc(const_in, 16)
                for b in range(B):
                    sp.dma_start(y_out[b].rearrange("(t p) d -> p t d", p=P),
                                 pr.x[:, b * NT:(b + 1) * NT, :]).then_inc(x_written, 16)
                for i in range(B * NT):
                    sp.wait_ge(xn_ready, i + 1)
                    sp.dma_start(xn_dram[i * P:(i + 1) * P, :], xn[:, i % XR, :]).then_inc(xn_sent[i % XR], 16)
                for i in range(XR):
                    sp.wait_ge(xn_sent[i], 16 * (B * NT // XR))
                sp.wait_ge(x_written, 16 * B)

            @block.tensor
            def _(pe):
                pe.wait_ge(const_in, 32)
                for i in range(B * NT):
                    pe.wait_ge(xn_ready, i + 1)
                    if i >= 2:
                        pe.wait_ge(xT_copied, i - 1)
                    for kd in range(KD):
                        mm = pe.transpose(t_bank[i % 2][:, bass.ts(kd, P)], xn[:, i % XR, bass.ts(kd, P)], pr.ident[:])
                    mm.then_inc(tr_done, 1)
                    if i % TPC == TPC - 1:
                        c = i // TPC
                        b, half = c // NCK, c % NCK
                        pe.wait_ge(xT_copied, i + 1)
                        for kd in range(KD):
                            mm = pe.matmul(lg_bank[half][ER * b:ER * b + ER, :], wg[:, kd, :], xT[:, c % 2, kd, :],
                                           start=(kd == 0), stop=(kd == KD - 1))
                        mm.then_inc(logits_done, 1)
                pe.wait_ge(idx_ready, 1)
                pe.transpose(i_bank[:, 0:P], idxf[:].rearrange("p a k -> p (a k)"), pr.ident[:]).then_inc(turned, 1)
                pe.wait_ge(pv_done, 2)
                pe.transpose(v_bank[:, 0:P], pv[:].rearrange("p a k -> p (a k)"), pr.ident[:]).then_inc(turned, 1)

            @block.scalar
            def _(act):
                for i in range(B * NT):
                    act.wait_ge(tr_done, i + 1)
                    c, t = divmod(i, TPC)
                    if t == 0 and c >= 2:
                        act.wait_ge(logits_done, c - 1)
                    act.activation(xT[:, c % 2, :, bass.ts(t, P)],
                                   t_bank[i % 2][:, 0:D].rearrange("p (k t) -> p k t", k=KD), ACT.Copy).then_inc(xT_copied, 1)
                act.wait_ge(nmax_done, 1)
                act.activation(ex[:], lg[:], ACT.Exp, bias=nmax[:], accum_out=tot[:]).then_inc(exp_done, 1)
                act.wait_ge(ev_done, 1)
                act.activation(ev[:], vals[:], ACT.Exp, bias=nmax[:]).then_inc(ev_done, 1)

            @block.vector
            def _(dve):
                for b in range(B):
                    dve.memset(first_row[ER * b:ER * b + ER, :], float(b * S)).then_inc(row_set, 1)
                for i in range(B * NT):
                    if i >= XR:
                        dve.wait_ge(xn_sent[i % XR], 16 * (i // XR))
                        dve.wait_ge(tr_done, i - XR + 1)
                    dve.tensor_scalar(xn[:, i % XR, :], pr.x[:, i, :], pr.mean[:, i:i + 1], pr.rstd[:, i:i + 1],
                                      ALU.subtract, ALU.mult).then_inc(xn_ready, 1)
                count = [0]

                def then(ins):
                    count[0] += 1
                    ins.then_inc(step, 1)
                    dve.wait_ge(step, count[0])

                dve.wait_ge(logits_done, NCH8)
                for half in range(2):
                    ins = dve.tensor_scalar(lg[:, bass.ts(half, CHK)], lg_bank[half][:], bg[:, 0:1], None, ALU.add)
                then(ins)
                for r in range(K1 // 8):
                    cols = bass.ts(r, 8)
                    then(dve.max(vals[:, cols], lg[:]))
                    if r == 0:
                        dve.tensor_scalar(nmax[:], vals[:, 0:1], -1.0, None, ALU.mult).then_inc(nmax_done, 1)
                    dve.max_index(idx[:, cols], vals[:, cols], lg[:])
                    if r == 0:
                        dve.wait_ge(exp_done, 1)
                    if r < K1 // 8 - 1:
                        then(dve.match_replace(lg[:], vals[:, cols], lg[:], LOWEST))
                then(dve.tensor_copy(ex[:, 0:1], tot[:]))
                dve.wait_ge(row_set, B)
                for a in range(2):
                    ins = dve.tensor_scalar(idxf[:, a, :], idx[:], first_row[:, 0:1], None, ALU.add)
                ins.then_inc(idx_ready, 1)
                dve.sem_inc(ev_done, 1)
                then(dve.reciprocal(rtot[:], tot[:]))
                dve.wait_ge(ev_done, 2)
                for a in range(2):
                    dve.tensor_scalar(pv[:, a, :], ev[:], rtot[:, 0:1], None, ALU.mult).then_inc(pv_done, 1)
                dve.wait_ge(turned, 2)
                for half in range(2):
                    lo = K1 * half
                    for dst, bank in ((rows, i_bank), (gatew, v_bank)):
                        src = bank[lo:lo + K1, 0:P].rearrange("p (q h e) -> p q h e", q=Q, h=2)[:, :, half, 0:E1]
                        dve.tensor_copy(dst[lo:lo + K1, :, :], src)

            @block.gpsimd
            def _(pool):
                pass

        with ExitStack() as ctx:
            def sb(nm, shape, dt=F32):
                return ctx.enter_context(nc.sbuf_tensor(f"f1.{nm}", shape, dt))

            def sem(nm):
                return pr.sem(f"f1_{nm}")

            raw = sb("raw", [P, 2, WC])
            w_hi = sb("w_hi", [P, 2, WC], F32R)
            w_lo = sb("w_lo", [P, 2, WC], F32R)
            bias = sb("bias", [P, 3, E1])
            bias_now = sb("bias_now", [P, 2, 4])
            gate_now = sb("gate_now", [P, 2, Q])
            bias_set = sem("bias_set")
            cur_in = sb("cur_in", [P, 2, Q], U32)
            cur_out = sb("cur_out", [P, 2, Q], U32)
            xg = sb("xg", [P, 2, Q, D])
            a_hi = sb("a_hi", [P, 2, KD, GT], F32R)
            a_lo = sb("a_lo", [P, 2, KD, GT], F32R)
            act_f = sb("act_f", [P, 2, KD * GT])
            yo = sb("yo", [P, 2, Q, D])
            raw_in = [sem("raw_in0"), sem("raw_in1")]
            bias_in = sem("bias_in")
            cur_set, cur_out_set, yo_free = sem("cur_set"), sem("cur_out_set"), sem("yo_free")
            xg_in = [[sem(f"xg_in{s}{q}") for q in range(Q)] for s in range(2)]
            w_hi_done, w_lo_done = sem("w_hi_done"), sem("w_lo_done")
            in_T, in_hi, in_lo = sem("in_T"), sem("in_hi"), sem("in_lo")
            h_done, relu_done, h_hi, h_lo = sem("h_done"), sem("relu_done"), sem("h_hi"), sem("h_lo")
            y_done, y_out_ready = sem("y_done"), sem("y_out_ready")
            added = [sem(f"added{q}") for q in range(Q)]
            t_bank = [pr.bank[0], pr.bank[1]]
            h_bank = [pr.bank[2], pr.bank[3]]
            y_bank = [pr.bank[4], pr.bank[5]]
            block = ctx.enter_context(nc.Block())
            PAIRS = E1 // 2

            def w_of(w, s, layer, kd, cols):
                base = (layer * KD + kd) * D
                return w[:, s, base + cols.start:base + cols.stop]

            @block.sync
            def _(sp):
                for n, bi in enumerate((b1_in, b2_in, b3_in)):
                    sp.dma_start(bias[:, n, :], bi.to_broadcast([P, E1])).then_inc(bias_in, 16)
                with sp.Fori(0, PAIRS) as it:
                    for s in range(2):
                        sp.wait_ge(w_lo_done, it * 2 + s + 1)
                        for n, w in enumerate((w1_in, w2_in, w3_in)):
                            sp.dma_start(raw[:, s, bass.ts(n, KD * D)].rearrange("p (c o) -> p c o", c=KD),
                                         w[bass.ds(it * 2 + s, 1)].rearrange("e (c p) o -> p (e c) o", p=P)).then_inc(raw_in[s], 16)
                for s in range(2):
                    sp.wait_ge(raw_in[s], 48 * PAIRS)
                sp.wait_ge(bias_in, 48)

            @block.gpsimd
            def _(pool):
                def fetch(it, s):
                    e = it * 2 + s
                    pr.wait_apart(pool, in_T, e + 1)
                    pool.tensor_copy(cur_in[:, s, :], rows[:, :, bass.ds(e, 1)].rearrange("p q o -> p (q o)")).then_inc(cur_set, 1)
                    pr.wait_apart(pool, cur_set, e + 1)
                    for q in range(Q):
                        pool.indirect_dma_start(xg[:, s, q, :], None, xn_dram,
                                                bass.IndirectOffsetOnAxis(ap=cur_in[:, s, q:q + 1], axis=0)).then_inc(xg_in[s][q], 16)

                def add_out(it, s):
                    e = it * 2 + s
                    pool.tensor_copy(cur_out[:, s, :], rows[:, :, bass.ds(e, 1)].rearrange("p q o -> p (q o)")).then_inc(cur_out_set, 1)
                    pr.wait_apart(pool, cur_out_set, e + 1)
                    pr.wait_apart(pool, y_out_ready, e + 3)
                    for q in range(Q):
                        pool.indirect_dma_start(y_out.rearrange("b s d -> (b s) d"),
                                                bass.IndirectOffsetOnAxis(ap=cur_out[:, s, q:q + 1], axis=0),
                                                yo[:, s, q, :], None, compute_op=ALU.add).then_inc(added[q], 16)
                    for q in range(Q):
                        pr.wait_apart(pool, added[q], e * 16 + 16)
                    pool.sem_inc(yo_free, 1)

                pool.sem_inc(in_T, 2)
                pool.sem_inc(yo_free, 2)
                for s in range(2):
                    fetch(0, s)
                with pool.Fori(0, PAIRS - 1) as it:
                    for s in range(2):
                        fetch(it + 1, s)
                    for s in range(2):
                        add_out(it, s)
                for s in range(2):
                    add_out(PAIRS - 1, s)

            @block.tensor
            def _(pe):
                def turn(it, s):
                    e = it * 2 + s
                    for q in range(Q):
                        pe.wait_ge(xg_in[s][q], it * 16 + 16)
                    pe.wait_ge(in_lo, e + 1)
                    for kd in range(KD):
                        for q in range(Q):
                            mm = pe.transpose(t_bank[s][:, kd * GT + q * P:kd * GT + q * P + P],
                                              xg[:, s, q, bass.ts(kd, P)], pr.ident[:])
                    mm.then_inc(in_T, 1)

                def layer(it, s, n):
                    e = it * 2 + s
                    if n == 0:
                        pe.wait_ge(in_lo, e + 3)
                        pe.wait_ge(w_lo_done, e + 3)
                    else:
                        pe.wait_ge(h_lo, it * 4 + (n - 1) * 2 + s + 1)
                    for m in range(KD):
                        i = 0
                        for kd in range(KD):
                            for wt, at in ((w_hi, a_hi), (w_hi, a_lo), (w_lo, a_hi)):
                                mm = pe.matmul(h_bank[s][:, bass.ts(m, GT)],
                                               w_of(wt, s, n, kd, slice(m * P, m * P + P)), at[:, s, kd, :],
                                               start=(i == 0), stop=(i == 3 * KD - 1))
                                i += 1
                    mm.then_inc(h_done, 1)

                def last(it, s):
                    e = it * 2 + s
                    pe.wait_ge(h_lo, it * 4 + 2 + s + 1)
                    pe.wait_ge(y_out_ready, e + 1)
                    for q in range(Q):
                        i = 0
                        for kd in range(KD):
                            for wt, at in ((w_hi, a_hi), (w_hi, a_lo), (w_lo, a_hi)):
                                mm = pe.matmul(y_bank[s][:, bass.ts(q, D)], at[:, s, kd, bass.ts(q, P)],
                                               w_of(wt, s, 2, kd, slice(0, D)), start=(i == 0), stop=(i == 3 * KD - 1))
                                i += 1
                    mm.then_inc(y_done, 1)

                with pe.Fori(0, PAIRS) as it:
                    for s in range(2):
                        turn(it, s)
                    for n in range(2):
                        for s in range(2):
                            layer(it, s, n)
                    for s in range(2):
                        last(it, s)

            @block.scalar
            def _(act):
                def split_weights(it, s):
                    act.wait_ge(raw_in[s], it * 48 + 48)
                    act.wait_ge(y_done, it * 2 + s + 1)
                    act.activation(w_hi[:, s, :], raw[:, s, :], ACT.Copy).then_inc(w_hi_done, 1)

                def input_hi(it, s):
                    act.wait_ge(in_T, it * 2 + s + 3)
                    act.activation(a_hi[:, s, :, :].rearrange("p c t -> p (c t)"), t_bank[s][:], ACT.Copy).then_inc(in_hi, 1)

                def relu(it, s, n):
                    k = it * 4 + n * 2 + s
                    act.wait_ge(h_done, k + 1)
                    act.activation(act_f[:, s, :], h_bank[s][:], ACT.Relu,
                                   bias=bias_now[:, s, n:n + 1]).then_inc(relu_done, 1)
                    act.wait_ge(relu_done, k + 1)
                    act.activation(a_hi[:, s, :, :].rearrange("p c t -> p (c t)"), act_f[:, s, :], ACT.Copy).then_inc(h_hi, 1)

                act.wait_ge(bias_in, 48)
                with act.Fori(0, PAIRS) as it:
                    for s in range(2):
                        split_weights(it, s)
                    for s in range(2):
                        input_hi(it, s)
                    for n in range(2):
                        for s in range(2):
                            if n == 0 and s == 0:
                                act.wait_ge(bias_set, it + 1)
                            relu(it, s, n)

            @block.vector
            def _(dve):
                dve.sem_inc(w_lo_done, 2)
                dve.sem_inc(in_lo, 2)
                dve.sem_inc(y_done, 2)
                dve.sem_inc(y_out_ready, 2)
                dve.wait_ge(bias_in, 48)
                with dve.Fori(0, PAIRS) as it:
                    pr.wait_apart(dve, y_out_ready, it * 2 + 2)
                    dve.tensor_copy(bias_now[:, :, 0:3], bias[:, :, bass.ds(it * 2, 2)].rearrange("p n s -> p s n")).then_inc(bias_set, 1)
                    dve.tensor_copy(gate_now[:], gatew[:, :, bass.ds(it * 2, 2)].rearrange("p q s -> p s q"))
                    for s in range(2):
                        dve.wait_ge(w_hi_done, it * 2 + s + 1)
                        dve.tensor_tensor(w_lo[:, s, :], raw[:, s, :], w_hi[:, s, :].bitcast(F32),
                                          ALU.subtract).then_inc(w_lo_done, 1)
                    for s in range(2):
                        dve.wait_ge(in_hi, it * 2 + s + 1)
                        dve.tensor_tensor(a_lo[:, s, :, :].rearrange("p c t -> p (c t)"), t_bank[s][:],
                                          a_hi[:, s, :, :].bitcast(F32).rearrange("p c t -> p (c t)"),
                                          ALU.subtract).then_inc(in_lo, 1)
                    for n in range(2):
                        for s in range(2):
                            dve.wait_ge(h_hi, it * 4 + n * 2 + s + 1)
                            dve.tensor_tensor(a_lo[:, s, :, :].rearrange("p c t -> p (c t)"), act_f[:, s, :],
                                              a_hi[:, s, :, :].bitcast(F32).rearrange("p c t -> p (c t)"),
                                              ALU.subtract).then_inc(h_lo, 1)
                    for s in range(2):
                        dve.wait_ge(y_done, it * 2 + s + 3)
                        dve.wait_ge(yo_free, it * 2 + s + 1)
                        for q in range(Q):
                            y = dve.tensor_scalar(yo[:, s, q, :], y_bank[s][:, bass.ts(q, D)], bias_now[:, s, 2:3],
                                                  gate_now[:, s, q:q + 1], ALU.add, ALU.mult)
                        y.then_inc(y_out_ready, 1)



def build(nc, x_in, ident_in, iota_in, ctxT_in, a0, gate_in, f0, a1, f1, xn_dram, y_out, upto=9):
    with ExitStack() as ctx:
        pr = Program(nc, ctx)
        load_phase(pr, x_in, ident_in)
        if upto >= 1:
            attention_phase(pr, "a0", 8, ctxT_in, *a0)
        if upto >= 2:
            router_phase(pr, gate_in, f0[3], iota_in)
            ffn0_phase(pr, f0[0], f0[1], f0[2])
        if upto >= 3:
            attention_phase(pr, "a1", 16, ctxT_in, *a1)
        if upto >= 4:
            expert_choice_phase(pr, y_out, xn_dram, *f1)
        else:
            out_written = pr.sem("out_written")
            with nc.Block() as block:
                @block.sync
                def _(sp):
                    for b in range(B):
                        sp.dma_start(y_out[b].rearrange("(t p) d -> p t d", p=P),
                                     pr.x[:, b * NT:(b + 1) * NT, :]).then_inc(out_written, 16)
                    sp.wait_ge(out_written, 16 * B)


def layout(inputs):
    import numpy as np

    def arr(name):
        return np.asarray(inputs[name])

    def whole(a):
        return np.ascontiguousarray(a)

    out = {
        "x_in": arr("x"),
        "ident_in": np.eye(P, dtype=np.float32),
        "iota_in": whole(np.broadcast_to(np.arange(E0, dtype=np.float32), (P, E0))),
        "ctxT_in": whole(arr("ctx_768").transpose(2, 0, 1).reshape(DC, B * NC)),
        "gate_in": arr("L0_ffn_gate_w"),
        "f0_w1": arr("L0_ffn_w1"),
        "f0_b1": whole(arr("L0_ffn_b1").reshape(E0, FT, P).transpose(0, 2, 1)),
        "f0_w2": arr("L0_ffn_w2"),
        "f0_b2": arr("L0_ffn_b2"),
    }
    for layer in (0, 1):
        a = f"L{layer}_xattn_"
        out[f"a{layer}_wqT"] = whole(arr(a + "Wq").T)
        out[f"a{layer}_wk"] = arr(a + "Wk")
        out[f"a{layer}_wv"] = arr(a + "Wv")
        out[f"a{layer}_wo"] = arr(a + "Wo")
        out[f"a{layer}_bo"] = arr(a + "bo").reshape(1, D)
    pad = np.zeros((D, 32 - E1), np.float32)
    out["f1_wg"] = np.concatenate([arr("L1_ffn_Wg"), pad], axis=1)
    out["f1_bg"] = np.tile(np.concatenate([arr("L1_ffn_bg"), pad[0]]), B).reshape(P, 1)
    for n in (1, 2, 3):
        out[f"f1_w{n}"] = arr(f"L1_ffn_w{n}")
        out[f"f1_b{n}"] = arr(f"L1_ffn_b{n}").reshape(1, E1)
    return {k: whole(v) for k, v in out.items()}


def build_all(nc, a, out, upto=9):
    att = [[a[f"a{n}_{w}"] for w in ("wqT", "wk", "wv", "wo", "bo")] for n in (0, 1)]
    build(nc, a["x_in"], a["ident_in"], a["iota_in"], a["ctxT_in"], att[0], a["gate_in"],
          [a["f0_w1"], a["f0_b1"], a["f0_w2"], a["f0_b2"]], att[1],
          [a[k] for k in ("f1_wg", "f1_bg", "f1_w1", "f1_b1", "f1_w2", "f1_b2", "f1_w3", "f1_b3")],
          nc.dram_tensor("xn_rows", [B * S, D], F32).ap(), out, upto)


def kernel(**inputs):
    import numpy as np
    from concourse import bacc
    from concourse.bass_utils import run_bass_kernel_spmd

    nc = bacc.Bacc("TRN2", target_bir_lowering=False, num_devices=1)
    arrays = layout(inputs)
    aps = {k: nc.dram_tensor(k, v.shape, mybir.dt.from_np(v.dtype), kind="ExternalInput").ap() for k, v in arrays.items()}
    out = nc.dram_tensor("out", (B, S, D), F32, kind="ExternalOutput").ap()
    build_all(nc, aps, out)
    r = run_bass_kernel_spmd(nc, [arrays], core_ids=[0])
    return np.asarray(r.results[0]["out"])
```

```python
from contextlib import ExitStack

import concourse.bass as bass
from concourse import mybir

F32 = mybir.dt.float32
F32R = mybir.dt.float32r
U32 = mybir.dt.uint32
ALU = mybir.AluOpType
ACT = mybir.ActivationFunctionType
AX_X = mybir.AxisListType.X

P = 128
B, S, D = 4, 1024, 256
KD = D // P
NT = S // P
NC, DC = 77, 192
CH = DC // 2
DH = 64
GH = 8
GP = GH // 2
GW = GH * NC
HALF = GW // 2
NCH = -(-GW // P)
PW = NCH * P
E0, F0, TOPK0 = 8, 1024, 2
FT = F0 // P
CHK = 512
NCK = S // CHK
TPC = CHK // P
E1, K1 = 16, 64
EPS = 1e-5
LOWEST = -3.0e38


class Program:

    def __init__(self, nc, ctx):
        self.nc, self.ctx = nc, ctx
        self.bank = [ctx.enter_context(nc.psum_tensor(f"bank{i}", [P, 512], F32)) for i in range(8)]
        self.x = self.sb("x_res", [P, B * NT, D])
        self.mean = self.sb("mean", [P, B * NT])
        self.rstd = self.sb("rstd", [P, B * NT])
        self.ident = self.sb("ident", [P, P])
        self.route_w = self.sb("route_w", [P, B, TOPK0])
        self.route_i = self.sb("route_i", [P, B, 8], U32)
        self.ffn_bias = self.sb("ffn_bias", [P, B, D])

        self.carry = self.sb("wait_carry", [P, 256])
        self.carries = 0
        self.one = self.sb("one", [P, 1])

    def wait_apart(self, engine, sem, value):
        engine.wait_ge(sem, value)
        spare = self.carry[:, self.carries:self.carries + 1]
        if engine is self.nc.vector:
            ins = engine.memset(spare, 0.0)
        else:
            ins = engine.tensor_tensor(spare, self.one[:], self.one[:], ALU.mult)
        self.carries += 1
        return ins

    def sb(self, name, shape, dt=F32):
        return self.ctx.enter_context(self.nc.sbuf_tensor(name, shape, dt))

    def sem(self, name):
        return self.ctx.enter_context(self.nc.semaphore(name))


def load_phase(pr, x_in, ident_in):
    nc = pr.nc
    with ExitStack() as ctx:
        stats = ctx.enter_context(nc.sbuf_tensor("ld_stats", [P, B, NT, 6], F32))
        mv = ctx.enter_context(nc.sbuf_tensor("ld_mv", [P, B, NT, 2], F32))
        ve = ctx.enter_context(nc.sbuf_tensor("ld_ve", [P, B, NT], F32))
        power = ctx.enter_context(nc.sbuf_tensor("ld_power", [P, NT], F32))
        batch_in = [pr.sem(f"ld_batch_in{b}") for b in range(B)]
        ident_ready = pr.sem("ld_ident_in")
        stats_done = pr.sem("ld_stats_done")
        mv_done = pr.sem("ld_mv_done")
        ve_done = pr.sem("ld_ve_done")
        power_set = pr.sem("ld_power_set")
        block = ctx.enter_context(nc.Block())

        @block.sync
        def _(sp):
            for b in range(B):
                sp.dma_start(pr.x[:, bass.ts(b, NT), :],
                             x_in[b].rearrange("(t p) d -> p t d", p=P)).then_inc(batch_in[b], 16)
            sp.dma_start(pr.ident[:], ident_in).then_inc(ident_ready, 16)
            sp.wait_ge(ident_ready, 16)

        @block.vector
        def _(dve):
            for b in range(B):
                dve.wait_ge(batch_in[b], 16)
                for t in range(NT):
                    dve.bn_stats(stats[:, b, t, :], pr.x[:, b * NT + t, :]).then_inc(stats_done, 1)
                for t in range(NT):
                    dve.wait_ge(stats_done, b * NT + t + 1)
                    dve.bn_aggr(mv[:, b, t, :], stats[:, b, t, :]).then_inc(mv_done, 1)
                dve.wait_ge(mv_done, b * NT + NT)
                dve.tensor_copy(pr.mean[:, bass.ts(b, NT)], mv[:, b, :, 0])
                dve.tensor_scalar(ve[:, b, :], mv[:, b, :, 1], EPS, None, ALU.add).then_inc(ve_done, 1)

        @block.gpsimd
        def _(pool):
            pool.memset(pr.one[:], 1.0)
            pool.memset(power[:], -0.5).then_inc(power_set, 1)
            pool.wait_ge(power_set, 1)
            for b in range(B):
                pool.wait_ge(ve_done, b + 1)
                pool.tensor_tensor(pr.rstd[:, bass.ts(b, NT)], ve[:, b, :], power[:], ALU.pow)

        @block.scalar
        def _(act):
            pass

        @block.tensor
        def _(pe):
            pass


def attention_phase(pr, name, heads, ctxT_in, wqT_in, wk_in, wv_in, wo_in, bo_in):
    nc = pr.nc
    groups = heads // GH
    pairs = heads // 2
    bodies = B * groups // 2
    UB = 2 * NT
    PREPS = NT * (2 // groups)
    AHEAD = 2
    LAG_T, LAG_AV, LAG_RES, LAG_ST, LAG_AG, LAG_FIN = 2, 3, 4, 6, 8, 9
    STEPS = UB + LAG_FIN + 1
    n = name

    def place(it, k):
        shift, kk = divmod(k, UB)
        p, t = divmod(kk, NT)
        return ((it + shift) * 2 + p if groups == 1 else it + shift), p, t

    def prep_due(k):
        return groups == 1 or k % UB < NT

    def prep_count(it, k):
        return it * PREPS + (k if groups == 1 else k // UB * NT + k % UB)

    with ExitStack() as ctx:
        def sb(nm, shape, dt=F32):
            return ctx.enter_context(nc.sbuf_tensor(f"{n}.{nm}", shape, dt))

        def sem(nm):
            return pr.sem(f"{n}_{nm}")

        kT = sb("kT", [P, pairs, B * NC])
        vT = sb("vT", [P, pairs, B * NC])
        wqT = sb("wqT", [P, pairs, D])
        wo = sb("wo", [P, pairs, D])
        bo = sb("bo", [P, D])
        vdiag = sb("vdiag", [P, GP * (PW + 2 * NC)])
        kb = sb("kb", [P, GP, NC])
        g_hi = sb("g_hi", [P, 2, KD, GW], F32R)
        g_lo = sb("g_lo", [P, 2, KD, GW], F32R)
        v_hi = sb("v_hi", [P, 2, NCH, D], F32R)
        v_lo = sb("v_lo", [P, 2, NCH, D], F32R)
        xT_hi = sb("xT_hi", [P, KD, S], F32R)
        xT_lo = sb("xT_lo", [P, KD, S], F32R)
        ER = 4
        ex = sb("ex", [P, ER, PW])
        pT = sb("pT", [P, 2, PW])
        pT_hi = sb("pT_hi", [P, 2, PW], F32R)
        pT_lo = sb("pT_lo", [P, 2, PW], F32R)
        xn = sb("xn", [P, 2, D])
        mx = sb("mx", [P, 2, GH])
        sm = sb("sm", [P, 2, GH])
        rc = sb("rc", [P, 2, GH])
        stats = sb("stats", [P, NT, 6])
        mv = sb("mv", [P, 2, NT, 2])
        ve = sb("ve", [P, 2, NT])
        power = sb("power", [P, NT])
        wk = sb("wk", [CH, 2, heads * DH])
        wv = sb("wv", [CH, 2, heads * DH])
        cT = sb("ctxT", [CH, 2, B * NC])

        proj_in, weights_in = sem("proj_in"), sem("weights_in")
        proj_done, proj_copied = sem("proj_done"), sem("proj_copied")
        zeroed, power_set = sem("zeroed"), sem("power_set")
        misc_written, misc_hi, misc_free = sem("misc_written"), sem("misc_hi"), sem("misc_free")
        vdiag_ready = sem("vdiag_ready")
        xn_ready, bo_added = sem("xn_ready"), sem("bo_added")
        sc_done, max_done, sub_done = sem("scores_done"), sem("max_done"), sem("sub_done")
        exp_done, sum_done, rec_done, mul_done = sem("exp_done"), sem("sum_done"), sem("rec_done"), sem("mul_done")
        tr_done, pT_copied, pT_lo_done = sem("probsT_done"), sem("pT_copied"), sem("pT_lo_done")
        av_done, res_done = sem("av_done"), sem("res_done")
        ve_done = sem("ve_done")

        score_bank = [[pr.bank[0], pr.bank[1]], [pr.bank[2], pr.bank[3]]]
        probT_bank = [pr.bank[4], pr.bank[5]]
        av_bank, misc_bank = pr.bank[6], pr.bank[7]
        CPB = 4

        V_USES = [(c, min(2, NCH - c)) for c in range(0, NCH, 2)]
        SETUP = 2 * KD + len(V_USES)
        assert SETUP <= NT

        def uses_of_step(it, k, last):
            uses = []
            if prep_due(k + AHEAD) and not (last and k + AHEAD >= UB):
                uses.append(("prep", k + AHEAD))
            if k % NT < SETUP and not (last and k >= NT):
                uses.append(("setup", k // NT + 1, k % NT))
            return uses

        FIRST_USES = [("setup", 0, j) for j in range(SETUP)] + [("prep", k) for k in range(AHEAD)]
        PER_BODY = PREPS + 2 * SETUP

        def numbered(it, last):
            at, out = len(FIRST_USES) + it * PER_BODY, []
            for k in range(UB):
                now = []
                for use in uses_of_step(it, k, last):
                    now.append((at, use))
                    at = at + 1
                out.append(now)
            return out

        def bodies_of(engine, body):
            body(0, first=True, last=bodies == 1)
            if bodies > 3:
                with engine.Fori(1, bodies - 1) as it:
                    body(it, first=False, last=False)
            elif bodies == 3:
                body(1, first=False, last=False)
            if bodies > 1:
                body(bodies - 1, first=False, last=True)

        def vdiag_rows(lo, off):
            v = vdiag[lo:lo + DH, :].rearrange("p (g z) -> p g z", g=GP)
            return v[:, :, off:off + NC]

        def misc_heads():
            return misc_bank[:, 0:HALF].rearrange("p (h j) -> p h j", h=GP)

        def heads_of(g, p, kd, odd):
            return g[:, p, kd, :].rearrange("p (h o j) -> p h o j", o=2, j=NC)[:, :, odd, :]

        def pass_of(it, q):
            b, p, _ = place(it, q * NT)
            return b, p, (0 if groups == 1 else p)

        block = ctx.enter_context(nc.Block())

        @block.sync
        def _(sp):
            for dst, src, done in ((cT[:], ctxT_in.rearrange("(c p) n -> p c n", p=CH), proj_in),
                                   (wk[:], wk_in.rearrange("(c p) n -> p c n", p=CH), proj_in),
                                   (wv[:], wv_in.rearrange("(c p) n -> p c n", p=CH), proj_in),
                                   (wqT[:], wqT_in.rearrange("(c p) n -> p c n", p=P), weights_in),
                                   (wo[:], wo_in.rearrange("(c p) n -> p c n", p=P), weights_in),
                                   (bo[:], bo_in.to_broadcast([P, D]), weights_in)):
                sp.dma_start(dst, src).then_inc(done, 16)
            sp.wait_ge(proj_in, 48)
            sp.wait_ge(weights_in, 48)

        @block.tensor
        def _(pe):
            pe.wait_ge(proj_in, 48)
            for j in range(2 * pairs):
                if j >= 4:
                    pe.wait_ge(proj_copied, j - 3)
                w = (wk if j < pairs else wv)[:, :, bass.ts(j % pairs, P)]
                for c in range(2):
                    mm = pe.matmul(pr.bank[j % 4][:, 0:B * NC], w[:, c, :], cT[:, c, :], start=(c == 0), stop=(c == 1))
                mm.then_inc(proj_done, 1)
            pe.wait_ge(proj_copied, 2 * pairs)
            pe.wait_ge(weights_in, 48)

            def setup(it, q, j):
                b, p, g = pass_of(it, q)
                if j < 2 * KD:
                    odd, kd = divmod(j, KD)
                    lo = DH * odd
                    for pair in range(GP):
                        mm = pe.matmul(misc_bank[:, bass.ts(pair, NC)], wqT[lo:lo + DH, g * GP + pair, bass.ts(kd, P)],
                                       kb[lo:lo + DH, pair, :], start=True, stop=True)
                else:
                    c0, m = V_USES[j - 2 * KD]
                    for c in range(c0, c0 + m):
                        inside = [h for h in range(GP) if h * 2 * NC < (c + 1) * P and (h + 1) * 2 * NC > c * P]
                        for h in inside:
                            mm = pe.matmul(misc_bank[:, bass.ts(c - c0, D)], vdiag[:, h * PW + c * P:h * PW + c * P + P],
                                           wo[:, g * GP + h, :], start=(h == inside[0]), stop=(h == inside[-1]))
                return mm

            def prep(it, k):
                for kd in range(KD):
                    mm = pe.transpose(misc_bank[:, bass.ts(kd, P)], xn[:, k % 2, bass.ts(kd, P)], pr.ident[:])
                return mm

            def misc(it, at, use):
                if use[0] == "prep":
                    pe.wait_ge(xn_ready, prep_count(it, use[1]) + 1)
                elif use[2] == 0:
                    pe.wait_ge(vdiag_ready, it * 2 + use[1] + 1)
                pe.wait_ge(misc_free, at + 1)
                (prep(it, use[1]) if use[0] == "prep" else setup(it, use[1], use[2])).then_inc(misc_written, 1)

            def scores(it, k, ready):
                u = it * UB + k
                _, p, t = place(it, k)
                pe.wait_ge(sub_done, u + 1)
                pe.wait_ge(misc_free, ready + 1)
                for half in range(2):
                    i = 0
                    for kd in range(KD):
                        for xt, gm in ((xT_hi, g_hi), (xT_lo, g_hi), (xT_hi, g_lo)):
                            mm = pe.matmul(score_bank[k % 2][half][:, 0:HALF], xt[:, kd, bass.ts(t, P)],
                                           gm[:, p, kd, bass.ts(half, HALF)], start=(i == 0), stop=(i == 3 * KD - 1))
                            i += 1
                mm.then_inc(sc_done, 1)

            def probs_transpose(it, k):
                u = it * UB + k
                pe.wait_ge(mul_done, u + 1)
                pe.wait_ge(pT_copied, u + 1)
                for c in range(NCH):
                    bk = probT_bank[c // CPB]
                    mm = pe.transpose(bk[:, bass.ts(c % CPB, P)], ex[:, k % ER, bass.ts(c, P)], pr.ident[:])
                mm.then_inc(tr_done, 1)

            def attend(it, k):
                u = it * UB + k
                _, p, _ = place(it, k)
                pe.wait_ge(pT_lo_done, u + 1)
                pe.wait_ge(res_done, u + 1)
                i = 0
                for c in range(NCH):
                    for pt, vm in ((pT_hi, v_hi), (pT_lo, v_hi), (pT_hi, v_lo)):
                        mm = pe.matmul(av_bank[:, 0:D], pt[:, k % 2, bass.ts(c, P)], vm[:, p, c, :],
                                       start=(i == 0), stop=(i == 3 * NCH - 1))
                        i += 1
                mm.then_inc(av_done, 1)

            for at, use in enumerate(FIRST_USES):
                misc(0, at, use)

            def body(it, first, last):
                uses = numbered(it, last)
                done = len(FIRST_USES) + it * PER_BODY
                for k in range(STEPS if last else UB):
                    if k < UB:
                        for at, use in uses[k][:1]:
                            misc(it, at, use)
                        scores(it, k, done)
                        for at, use in uses[k][1:]:
                            misc(it, at, use)
                        done = done + len(uses[k])
                    if (k >= LAG_T or not first) and k < UB + LAG_T:
                        probs_transpose(it, k - LAG_T)
                    if (k >= LAG_AV or not first) and k < UB + LAG_AV:
                        attend(it, k - LAG_AV)

            bodies_of(pe, body)

        @block.scalar
        def _(act):
            for j in range(2 * pairs):
                act.wait_ge(proj_done, j + 1)
                dst = (kT if j < pairs else vT)[:, j % pairs, :]
                act.activation(dst, pr.bank[j % 4][:, 0:B * NC], ACT.Copy).then_inc(proj_copied, 1)

            def misc(it, at, use):
                act.wait_ge(misc_written, at + 1)
                if use[0] == "prep":
                    t = use[1] % NT
                    ins = act.activation(xT_hi[:, :, bass.ts(t, P)], misc_bank[:, 0:D].rearrange("p (c t) -> p c t", c=KD),
                                         ACT.Copy)
                else:
                    _, p, _ = pass_of(it, use[1])
                    j = use[2]
                    if j < 2 * KD:
                        ins = act.activation(heads_of(g_hi, p, j % KD, j // KD), misc_heads(), ACT.Copy,
                                             scale=float(DH) ** -0.5)
                    else:
                        c0, m = V_USES[j - 2 * KD]
                        ins = act.activation(v_hi[:, p, c0:c0 + m, :].rearrange("p c d -> p (c d)"),
                                             misc_bank[:, 0:m * D], ACT.Copy)
                ins.then_inc(misc_hi, 1)

            def exp(it, k):
                u = it * UB + k
                act.wait_ge(sub_done, u + 3)
                act.activation(ex[:, k % ER, 0:GW], ex[:, k % ER, 0:GW], ACT.Exp).then_inc(exp_done, 1)

            def probT_copy(it, k):
                u = it * UB + k
                act.wait_ge(tr_done, u + 1 + ER)
                act.wait_ge(av_done, u + 1)
                for dst in (pT_hi, pT):
                    act.activation(dst[:, k % 2, 0:CPB * P], probT_bank[0][:], ACT.Copy)
                    ins = act.activation(dst[:, k % 2, CPB * P:PW], probT_bank[1][:, 0:PW - CPB * P], ACT.Copy)
                ins.then_inc(pT_copied, 1)

            act.wait_ge(zeroed, 2)
            for at, use in enumerate(FIRST_USES):
                misc(0, at, use)

            def body(it, first, last):
                uses = numbered(it, last)
                for k in range(UB + LAG_T if last else UB):
                    if k < UB:
                        for at, use in uses[k]:
                            misc(it, at, use)
                    if k >= LAG_T or not first:
                        probT_copy(it, k - LAG_T)
                    if k < UB:
                        exp(it, k)

            bodies_of(act, body)

        @block.vector
        def _(dve):
            dve.memset(vdiag[:], 0.0).then_inc(zeroed, 1)
            dve.memset(ex[:, :, GW:PW], 0.0).then_inc(zeroed, 1)
            dve.sem_inc(sub_done, 2)
            dve.sem_inc(tr_done, ER)
            dve.sem_inc(av_done, 2)
            dve.sem_inc(pT_copied, 1)
            dve.sem_inc(res_done, 1)
            dve.sem_inc(misc_free, 1)
            dve.wait_ge(zeroed, 2)
            dve.wait_ge(proj_copied, 2 * pairs)

            def place_kv(it, q, done):
                b, _, g = pass_of(it, q)
                pr.wait_apart(dve, misc_free, done + 1)
                for odd in range(2):
                    lo = DH * odd
                    dve.tensor_copy(vdiag_rows(lo, NC * odd), vT[lo:lo + DH, g * GP:(g + 1) * GP, bass.ts(b, NC)])
                dve.tensor_copy(kb[:], kT[:, g * GP:(g + 1) * GP, bass.ts(b, NC)]).then_inc(vdiag_ready, 1)

            def misc(it, at, use):
                if use[0] == "prep":
                    cols = bass.ts(use[1] % NT, P)
                    dve.wait_ge(misc_hi, at + 1)
                    ins = dve.tensor_tensor(xT_lo[:, :, cols], misc_bank[:, 0:D].rearrange("p (c t) -> p c t", c=KD),
                                            xT_hi[:, :, cols].bitcast(F32), ALU.subtract)
                else:
                    _, p, _ = pass_of(it, use[1])
                    j = use[2]
                    dve.wait_ge(misc_hi, at + 1)
                    if j < 2 * KD:
                        ins = dve.scalar_tensor_tensor(out=heads_of(g_lo, p, j % KD, j // KD), in0=misc_heads(),
                                                       scalar=float(DH) ** -0.5,
                                                       in1=heads_of(g_hi, p, j % KD, j // KD).bitcast(F32),
                                                       op0=ALU.mult, op1=ALU.subtract)
                    else:
                        c0, m = V_USES[j - 2 * KD]
                        ins = dve.tensor_tensor(v_lo[:, p, c0:c0 + m, :].rearrange("p c d -> p (c d)"),
                                                misc_bank[:, 0:m * D],
                                                v_hi[:, p, c0:c0 + m, :].bitcast(F32).rearrange("p c d -> p (c d)"),
                                                ALU.subtract)
                ins.then_inc(misc_free, 1)

            def normalise(it, k, at):
                b, _, t = place(it, k)
                dve.wait_ge(misc_written, at)
                dve.tensor_scalar(xn[:, k % 2, :], pr.x[:, b * NT + t, :], pr.mean[:, bass.ds(b * NT + t, 1)],
                                  pr.rstd[:, bass.ds(b * NT + t, 1)], ALU.subtract, ALU.mult).then_inc(xn_ready, 1)

            def score_max(it, k):
                u = it * UB + k
                dve.wait_ge(sc_done, u + 1)
                for half in range(2):
                    rd = dve.tensor_reduce(mx[:, k % 2, bass.ts(half, GH // 2)],
                                           score_bank[k % 2][half][:, 0:HALF].rearrange("p (h j) -> p h j", h=GH // 2),
                                           AX_X, ALU.max)
                rd.then_inc(max_done, 1)

            def score_sub(it, k):
                u = it * UB + k
                dve.wait_ge(max_done, u + 1)
                dve.wait_ge(tr_done, u + 1)
                for half in range(2):
                    m = mx[:, k % 2, bass.ts(half, GH // 2)].unsqueeze(2).to_broadcast([P, GH // 2, NC])
                    ss = dve.tensor_tensor(ex[:, k % ER, bass.ts(half, HALF)].rearrange("p (h j) -> p h j", h=GH // 2),
                                           score_bank[k % 2][half][:, 0:HALF].rearrange("p (h j) -> p h j", h=GH // 2),
                                           m, ALU.subtract)
                ss.then_inc(sub_done, 1)

            def exp_sum(it, k):
                u = it * UB + k
                dve.wait_ge(exp_done, u + 1)
                dve.tensor_reduce(sm[:, k % 2, :], ex[:, k % ER, 0:GW].rearrange("p (h j) -> p h j", h=GH),
                                  AX_X, ALU.add).then_inc(sum_done, 1)

            def exp_rec(it, k):
                u = it * UB + k
                dve.wait_ge(sum_done, u + 1)
                dve.reciprocal(rc[:, k % 2, :], sm[:, k % 2, :]).then_inc(rec_done, 1)

            def residual(it, k):
                u = it * UB + k
                b, _, t = place(it, k)
                dve.wait_ge(av_done, u + 3)
                if prep_due(k):
                    dve.wait_ge(bo_added, prep_count(it, k) + 1)
                xt = pr.x[:, b * NT + t, :]
                dve.tensor_tensor(xt, xt, av_bank[:, 0:D], ALU.add).then_inc(res_done, 1)

            def finishes(k):
                return groups == 1 or k % UB >= NT

            def tile_stats(it, k):
                b, _, t = place(it, k)
                dve.bn_stats(stats[:, t, :], pr.x[:, b * NT + t, :])

            def tile_mean(it, k):
                _, p, t = place(it, k)
                dve.bn_aggr(mv[:, p, t, :], stats[:, t, :])

            def batch_mean(it, k):
                b, p, _ = place(it, k)
                dve.tensor_copy(pr.mean[:, bass.ts(b, NT)], mv[:, p, :, 0])
                dve.tensor_scalar(ve[:, p, :], mv[:, p, :, 1], EPS, None, ALU.add).then_inc(ve_done, 1)

            place_kv(0, 0, 0)
            for at, use in enumerate(FIRST_USES):
                if use[0] == "prep":
                    normalise(0, use[1], at)
                misc(0, at, use)
            place_kv(0, 1, len(FIRST_USES))
            normalise(0, AHEAD, len(FIRST_USES) - 1)

            def body(it, first, last):
                uses = numbered(it, last)
                done = len(FIRST_USES) + it * PER_BODY
                for k in range(STEPS if last else UB):
                    if (k >= LAG_ST or not first) and finishes(k - LAG_ST) and k < UB + LAG_ST:
                        if k >= UB + LAG_RES:
                            pr.wait_apart(dve, res_done, it * UB + k - LAG_ST + 2)
                        tile_stats(it, k - LAG_ST)
                    if (k >= LAG_AG or not first) and finishes(k - LAG_AG) and k < UB + LAG_AG:
                        if k >= UB + LAG_RES:
                            dve.drain()
                        tile_mean(it, k - LAG_AG)
                    if (k >= LAG_FIN or not first) and finishes(k - LAG_FIN) and (k - LAG_FIN) % NT == NT - 1:
                        if k >= UB + LAG_RES:
                            dve.drain()
                        batch_mean(it, k - LAG_FIN)
                    if prep_due(k + AHEAD + 1) and not (last and k + AHEAD + 1 >= UB):
                        normalise(it, k + AHEAD + 1, done)
                    if (k >= LAG_RES or not first) and k < UB + LAG_RES:
                        residual(it, k - LAG_RES)
                    if k < UB:
                        for at, use in uses[k][:1]:
                            misc(it, at, use)
                        score_max(it, k)
                    if (k >= 1 or not first) and k <= UB:
                        exp_sum(it, k - 1)
                    if k < UB:
                        for at, use in uses[k][1:]:
                            misc(it, at, use)
                    if (k >= 1 or not first) and k <= UB:
                        exp_rec(it, k - 1)
                    if k < UB:
                        score_sub(it, k)
                        done = done + len(uses[k])
                        if k % NT == NT - 1 and not last:
                            place_kv(it, k // NT + 2, done)

            bodies_of(dve, body)

        @block.gpsimd
        def _(pool):
            pool.memset(power[:], -0.5).then_inc(power_set, 1)
            pool.wait_ge(power_set, 1)
            pool.wait_ge(weights_in, 48)

            def normalise_probs(it, k):
                u = it * UB + k
                pool.wait_ge(rec_done, u + 1)
                e3 = ex[:, k % ER, 0:GW].rearrange("p (h j) -> p h j", h=GH)
                pool.tensor_tensor(e3, e3, rc[:, k % 2, :].unsqueeze(2).to_broadcast([P, GH, NC]),
                                   ALU.mult).then_inc(mul_done, 1)

            def probT_lo(it, k):
                u = it * UB + k
                pool.wait_ge(pT_copied, u + 2)
                pool.tensor_tensor(pT_lo[:, k % 2, :], pT[:, k % 2, :], pT_hi[:, k % 2, :].bitcast(F32),
                                   ALU.subtract).then_inc(pT_lo_done, 1)

            def add_bo(it, k):
                b, _, t = place(it, k)
                pr.wait_apart(pool, xn_ready, prep_count(it, k) + 1)
                xt = pr.x[:, b * NT + t, :]
                pool.tensor_tensor(xt, xt, bo[:], ALU.add).then_inc(bo_added, 1)

            def rstd(it, k):
                b, p, _ = place(it, k)
                count = it * (2 // groups) + (k // NT if groups == 1 else k // UB) + 1
                pr.wait_apart(pool, ve_done, count)
                pool.tensor_tensor(pr.rstd[:, bass.ts(b, NT)], ve[:, p, :], power[:], ALU.pow)

            for k in range(AHEAD):
                add_bo(0, k)

            def body(it, first, last):
                for k in range(STEPS if last else UB):
                    if (k >= 1 or not first) and k <= UB:
                        normalise_probs(it, k - 1)
                    if (k >= LAG_T or not first) and k < UB + LAG_T:
                        probT_lo(it, k - LAG_T)
                    if k < UB and prep_due(k + AHEAD) and not (last and k + AHEAD >= UB):
                        add_bo(it, k + AHEAD)
                    if (k >= LAG_FIN or not first) and (groups == 1 or (k - LAG_FIN) % UB >= NT) and (k - LAG_FIN) % NT == NT - 1:
                        rstd(it, k - LAG_FIN)

            bodies_of(pool, body)


def router_phase(pr, gate_in, b2_in, iota_in):
    nc = pr.nc
    with ExitStack() as ctx:
        def sb(nm, shape, dt=F32):
            return ctx.enter_context(nc.sbuf_tensor(f"rt.{nm}", shape, dt))

        def sem(nm):
            return pr.sem(f"rt_{nm}")

        XR = 4
        STEPS = 8 + 4 * B
        xn = sb("xn", [P, XR, D])
        ones = sb("ones", [P, 1])
        gate = sb("gate", [P, KD, E0])
        b2 = sb("b2", [E0, D])
        iota = sb("iota", [P, E0])
        meanT = sb("meanT", [P, B, KD, P])
        top = sb("top", [P, B, 8])
        neg = sb("neg", [P, B])
        ez = sb("ez", [P, B, E0])
        tot = sb("tot", [P, B])
        rtot = sb("rtot", [P, B])
        probs = sb("probs", [P, B, E0])
        topi = sb("topi", [P, B, 8])
        pair = sb("pair", [P, B])
        rpair = sb("rpair", [P, B])
        hit = sb("hit", [P, B, TOPK0, E0])
        comb = sb("comb", [P, B, E0])
        combT = sb("combT", [E0, B, P])
        const_in, ones_set = sem("const_in"), sem("ones_set")
        xn_ready, summed = sem("xn_ready"), sem("summed")
        mean_copied, logits_done = sem("mean_copied"), sem("logits_done")
        step, exp_done = sem("step"), sem("exp_done")
        combT_done, combT_copied, bias_done = sem("combT_done"), sem("combT_copied"), sem("bias_done")
        mean_bank, logit_bank, comb_bank = pr.bank[0], pr.bank[1], pr.bank[2]
        bias_bank = [pr.bank[3], pr.bank[4]]
        block = ctx.enter_context(nc.Block())

        @block.sync
        def _(sp):
            sp.dma_start(gate[:], gate_in.rearrange("(c p) e -> p c e", p=P)).then_inc(const_in, 16)
            sp.dma_start(b2[:], b2_in).then_inc(const_in, 16)
            sp.dma_start(iota[:], iota_in).then_inc(const_in, 16)
            sp.wait_ge(const_in, 48)

        @block.tensor
        def _(pe):
            pe.wait_ge(ones_set, 1)
            for b in range(B):
                for t in range(NT):
                    i = b * NT + t
                    pe.wait_ge(xn_ready, i + 1)
                    for kd in range(KD):
                        mm = pe.matmul(mean_bank[:, b * KD + kd:b * KD + kd + 1], xn[:, i % XR, bass.ts(kd, P)], ones[:],
                                       start=(i == 0 and kd == 0), stop=(t == NT - 1), skip_group_check=True)
                    mm.then_inc(summed, 1)
            pe.wait_ge(mean_copied, 1)
            pe.wait_ge(const_in, 48)
            for b in range(B):
                for kd in range(KD):
                    mm = pe.matmul(logit_bank[:, bass.ts(b, E0)], meanT[:, b, kd, :], gate[:, kd, :],
                                   start=(kd == 0), stop=(kd == KD - 1))
            mm.then_inc(logits_done, 1)
            pe.wait_ge(step, STEPS)
            for b in range(B):
                mm = pe.transpose(comb_bank[0:E0, bass.ts(b, P)], comb[:, b, :], pr.ident[:])
            mm.then_inc(combT_done, 1)
            pe.wait_ge(combT_copied, 1)
            for b in range(B):
                mm = pe.matmul(bias_bank[b // 2][:, bass.ts(b % 2, D)], combT[:, b, :], b2[:], start=True, stop=True)
            mm.then_inc(bias_done, 1)

        @block.vector
        def _(dve):
            dve.memset(ones[:], 1.0).then_inc(ones_set, 1)
            for i in range(B * NT):
                if i >= XR:
                    dve.wait_ge(summed, i - XR + 1)
                dve.tensor_scalar(xn[:, i % XR, :], pr.x[:, i, :], pr.mean[:, i:i + 1], pr.rstd[:, i:i + 1],
                                  ALU.subtract, ALU.mult).then_inc(xn_ready, 1)
            dve.wait_ge(summed, B * NT)
            dve.tensor_scalar(meanT[:].rearrange("p b k m -> p (b k) m"),
                              mean_bank[:, 0:B * KD].unsqueeze(2).to_broadcast([P, B * KD, P]), 1.0 / S, None,
                              ALU.mult).then_inc(mean_copied, 1)
            dve.wait_ge(logits_done, 1)
            lg = logit_bank[:, 0:B * E0].rearrange("p (b e) -> p b e", b=B)
            count = [0]

            def then(ins):
                count[0] += 1
                ins.then_inc(step, 1)
                dve.wait_ge(step, count[0])

            def each(n):
                return n.unsqueeze(2).to_broadcast([P, B, E0])

            then(dve.tensor_reduce(neg[:], lg, AX_X, ALU.max))
            then(dve.tensor_tensor(ez[:], lg, each(neg[:]), ALU.subtract))
            dve.wait_ge(exp_done, 1)
            then(dve.tensor_reduce(tot[:], ez[:], AX_X, ALU.add))
            then(dve.reciprocal(rtot[:], tot[:]))
            then(dve.tensor_tensor(probs[:], ez[:], each(rtot[:]), ALU.mult))
            for b in range(B):
                then(dve.max(top[:, b, :], probs[:, b, :]))
                then(dve.max_index(pr.route_i[:, b, :], top[:, b, :], probs[:, b, :]))
            then(dve.tensor_copy(topi[:], pr.route_i[:]))
            then(dve.tensor_tensor(pair[:], top[:, :, 0], top[:, :, 1], ALU.add))
            then(dve.reciprocal(rpair[:], pair[:]))
            dve.tensor_tensor(pr.route_w[:], top[:, :, 0:TOPK0], rpair[:].unsqueeze(2).to_broadcast([P, B, TOPK0]),
                              ALU.mult).then_inc(bias_done, 2)
            dve.wait_ge(bias_done, 2)
            for b in range(B):
                dve.tensor_scalar(hit[:, b, 0, :], iota[:], topi[:, b, 0:1], pr.route_w[:, b, 0:1], ALU.is_equal, ALU.mult)
                then(dve.tensor_scalar(hit[:, b, 1, :], iota[:], topi[:, b, 1:2], pr.route_w[:, b, 1:2],
                                       ALU.is_equal, ALU.mult))
                then(dve.tensor_tensor(comb[:, b, :], hit[:, b, 0, :], hit[:, b, 1, :], ALU.add))
            assert count[0] == STEPS, count
            dve.wait_ge(combT_done, 1)
            dve.tensor_copy(combT[:].rearrange("e b p -> e (b p)"), comb_bank[0:E0, 0:B * P]).then_inc(combT_copied, 1)
            dve.wait_ge(bias_done, 3)
            for h in range(2):
                dve.tensor_copy(pr.ffn_bias[:, 2 * h:2 * h + 2, :].rearrange("p b d -> p (b d)"), bias_bank[h][:])

        @block.scalar
        def _(act):
            act.wait_ge(step, 2)
            act.activation(ez[:], ez[:], ACT.Exp).then_inc(exp_done, 1)

        @block.gpsimd
        def _(pool):
            pass


def ffn0_phase(pr, w1_in, b1_in, w2_in):
    nc = pr.nc
    JOBS = TOPK0
    PIECES = 8
    W1C = KD * F0
    WC = W1C + FT * D
    PIECE = WC // PIECES
    JH = NCK * FT
    HT = JOBS * JH
    LAG, RING = 2, 4
    LAG_RES = LAG + 1
    SPLIT_AT = LAG + 1
    NEXT_LN = HT - FT
    STATS_AT = LAG_RES + 1
    AGGR_AT = STATS_AT + NT
    with ExitStack() as ctx:
        def sb(nm, shape, dt=F32):
            return ctx.enter_context(nc.sbuf_tensor(f"f0.{nm}", shape, dt))

        def sem(nm):
            return pr.sem(f"f0_{nm}")

        raw = sb("raw", [P, WC])
        w_hi = sb("w_hi", [P, JOBS, WC], F32R)
        w_lo = sb("w_lo", [P, JOBS, WC], F32R)
        b1 = sb("b1", [P, JOBS, FT])
        xT_hi = sb("xT_hi", [P, KD, S], F32R)
        xT_lo = sb("xT_lo", [P, KD, S], F32R)
        xn = sb("xn", [P, 2, D])
        hid = sb("hid", [P, 2, CHK])
        h_hi = sb("h_hi", [P, RING, CHK], F32R)
        h_lo = sb("h_lo", [P, RING, CHK], F32R)
        stats = sb("stats", [P, NT, 6])
        mv = sb("mv", [P, NT, 2])
        ve = sb("ve", [P, NT])
        power = sb("power", [P, NT])
        w1_in_done, w2_in_done = sem("w1_in"), sem("w2_in")
        b1_in_done = [sem(f"b1_in{j}") for j in range(JOBS)]
        raw_hi, raw_free = sem("raw_hi"), sem("raw_free")
        xn_ready, bias_added = sem("xn_ready"), sem("bias_added")
        xT_written, xT_hi_done, xT_lo_done = sem("xT_written"), sem("xT_hi_done"), sem("xT_lo_done")
        h_done, gelu_done, h_hi_done, h_lo_done = sem("h_done"), sem("gelu_done"), sem("h_hi_done"), sem("h_lo_done")
        y_step, y_read = sem("y_step"), sem("y_read")
        stats_done, mv_done, ve_done, rstd_done = sem("stats_done"), sem("mv_done"), sem("ve_done"), sem("rstd_done")
        GELU_CR, Y_CR, READ_CR = JH + 2, RING, 2 * TPC
        h_bank = [pr.bank[0], pr.bank[1]]
        y_bank = pr.bank[2:6]
        t_bank = [pr.bank[6], pr.bank[7]]
        block = ctx.enter_context(nc.Block())

        def w1_of(w, j, kd, f):
            return w[:, j, kd * F0 + f * P:kd * F0 + f * P + P]

        def w2_of(w, j, f):
            return w[:, j, W1C + f * D:W1C + f * D + D]

        def y_of(i, t):
            return y_bank[2 * (i // FT % 2) + t // 2][:, bass.ts(t % 2, D)]

        def parts(i):
            i = i % HT
            return i // JH, i // FT % NCK, i % FT

        def bodies_of(engine, body):
            body(0, first=True, last=False)
            with engine.Fori(1, B - 1) as b:
                body(b, first=False, last=False)
            body(B - 1, first=False, last=True)

        def preps_of_step(i, last):
            if i < TPC:
                return [TPC + i]
            if i >= NEXT_LN and i < NEXT_LN + TPC and not last:
                return [NT + i - NEXT_LN]
            return []

        def split_of_step(i, last):
            j, q = i // JH, i % JH - SPLIT_AT
            if 0 <= q < PIECES and not (last and j == JOBS - 1):
                return [(j + 1) * PIECES + q]
            return []

        @block.sync
        def _(sp):
            with sp.Fori(0, B) as b:
                for j in range(JOBS):
                    e = sp.value_load(pr.route_i[0:1, b, j:j + 1], min_val=0, max_val=E0 - 1)
                    sp.wait_ge(raw_free, b * (JOBS * PIECES) + j * PIECES + 1)
                    sp.dma_start(raw[:, 0:W1C].rearrange("p (c f) -> p c f", c=KD),
                                 w1_in[bass.ds(e, 1)].rearrange("o (c p) f -> p (o c) f", p=P)).then_inc(w1_in_done, 16)
                    sp.dma_start(raw[:, W1C:WC].rearrange("p (c d) -> p c d", c=FT),
                                 w2_in[bass.ds(e, 1)].rearrange("o (c p) d -> p (o c) d", p=P)).then_inc(w2_in_done, 16)
                    sp.wait_ge(gelu_done, b * HT + j * JH + GELU_CR - JH)
                    sp.dma_start(b1[:, j, :],
                                 b1_in[bass.ds(e, 1)].rearrange("o p f -> p (o f)")).then_inc(b1_in_done[j], 16)
            sp.wait_ge(w1_in_done, 16 * JOBS * B)
            sp.wait_ge(w2_in_done, 16 * JOBS * B)
            for j in range(JOBS):
                sp.wait_ge(b1_in_done[j], 16 * B)

        @block.tensor
        def _(pe):
            def prep(b, t):
                pe.wait_ge(xn_ready, b * NT + t + 1)
                pe.wait_ge(xT_lo_done, b * NT + t + 1)
                for kd in range(KD):
                    mm = pe.transpose(t_bank[t % 2][:, bass.ts(kd, P)], xn[:, t % 2, bass.ts(kd, P)], pr.ident[:])
                mm.then_inc(xT_written, 1)

            def hidden(b, i):
                j, c, f = parts(i)
                if i % JH == 0:
                    pe.wait_ge(raw_free, b * (JOBS * PIECES) + j * PIECES + PIECES // 2 + 1)
                if j == 0 and f == 0:
                    pe.wait_ge(xT_lo_done, b * NT + (c + 1) * TPC + 2)
                pe.wait_ge(gelu_done, b * HT + i - 1 + GELU_CR)
                n = 0
                for kd in range(KD):
                    for wt, xt in ((w_hi, xT_hi), (w_hi, xT_lo), (w_lo, xT_hi)):
                        mm = pe.matmul(h_bank[i % 2][:], w1_of(wt, j, kd, f), xt[:, kd, bass.ts(c, CHK)],
                                       start=(n == 0), stop=(n == 3 * KD - 1))
                        n += 1
                mm.then_inc(h_done, 1)

            def output(b, i):
                j, c, f = parts(i)
                if i % JH == 0:
                    pe.wait_ge(raw_free, b * (JOBS * PIECES) + (i // JH + 1) * PIECES + 1)
                pe.wait_ge(h_lo_done, b * HT + i + 3)
                if f == 0:
                    pe.wait_ge(y_read, b * (HT // FT * TPC) + (i // FT - 1) * TPC + READ_CR)
                for t in range(TPC):
                    n = 0
                    for ht, wt in ((h_hi, w_hi), (h_lo, w_hi), (h_hi, w_lo)):
                        mm = pe.matmul(y_of(i, t), ht[:, i % RING, bass.ts(t, P)], w2_of(wt, j, f),
                                       start=(f == 0 and n == 0 and t % 2 == 0), stop=(f == FT - 1 and n == 2), skip_group_check=True)
                        n += 1
                mm.then_inc(y_step, 1)

            for t in range(TPC):
                prep(0, t)

            def body(b, first, last):
                for i in range(HT + LAG if last else HT):
                    if i < HT:
                        hidden(b, i)
                        for t in preps_of_step(i, last):
                            prep(b, t)
                    if i >= LAG or not first:
                        output(b, i - LAG)

            bodies_of(pe, body)

        @block.scalar
        def _(act):
            def split_hi(b, piece):
                g, q = divmod(piece, PIECES)
                if q == 0:
                    act.wait_ge(w1_in_done, b * (16 * JOBS) + 16 * (g + 1))
                    if g:
                        act.wait_ge(y_step, b * HT + (g - 1) * JH + Y_CR)
                if q == PIECES // 2:
                    act.wait_ge(w2_in_done, b * (16 * JOBS) + 16 * (g + 1))
                act.activation(w_hi[:, g % JOBS, bass.ts(q, PIECE)], raw[:, bass.ts(q, PIECE)],
                               ACT.Copy).then_inc(raw_hi, 1)

            def prep(b, t):
                act.wait_ge(xT_written, b * NT + t + 1)
                act.activation(xT_hi[:, :, bass.ts(t % NT, P)],
                               t_bank[t % 2][:, 0:D].rearrange("p (c t) -> p c t", c=KD),
                               ACT.Copy).then_inc(xT_hi_done, 1)

            def gelu(b, i):
                j, f = i // JH, i % FT
                if i % JH == 0:
                    act.wait_ge(b1_in_done[j], b * 16 + 16)
                act.wait_ge(h_done, b * HT + i + 1)
                act.wait_ge(h_lo_done, b * HT + i + 1)
                act.activation(hid[:, i % 2, :], h_bank[i % 2][:], ACT.Gelu, bias=b1[:, j, f:f + 1]).then_inc(gelu_done, 1)

            for t in range(TPC):
                prep(0, t)
            for piece in range(PIECES):
                split_hi(0, piece)

            def body(b, first, last):
                for i in range(HT):
                    gelu(b, i)
                    for t in preps_of_step(i, last):
                        prep(b, t)
                    for piece in split_of_step(i, last):
                        split_hi(b, piece)

            bodies_of(act, body)

        @block.vector
        def _(dve):
            dve.sem_inc(raw_free, 1)
            dve.sem_inc(xT_lo_done, 2)
            dve.sem_inc(gelu_done, GELU_CR)
            dve.sem_inc(h_lo_done, 2)
            dve.sem_inc(y_read, READ_CR)
            dve.sem_inc(y_step, Y_CR)

            def normalise(b, t):
                if t >= 2:
                    dve.wait_ge(xT_written, b * NT + t - 1)
                col = bass.ds(b * NT + t, 1)
                dve.tensor_scalar(xn[:, t % 2, :], pr.x[:, b * NT + t, :], pr.mean[:, col], pr.rstd[:, col],
                                  ALU.subtract, ALU.mult).then_inc(xn_ready, 1)

            def prep_lo(b, t):
                dve.wait_ge(xT_hi_done, b * NT + t + 1)
                cols = bass.ts(t % NT, P)
                dve.tensor_tensor(xT_lo[:, :, cols], t_bank[t % 2][:, 0:D].rearrange("p (c t) -> p c t", c=KD),
                                  xT_hi[:, :, cols].bitcast(F32), ALU.subtract).then_inc(xT_lo_done, 1)

            def split_lo(b, piece):
                g, q = divmod(piece, PIECES)
                dve.wait_ge(raw_hi, b * (JOBS * PIECES) + piece + 1)
                cols = bass.ts(q, PIECE)
                dve.tensor_tensor(w_lo[:, g % JOBS, cols], raw[:, cols], w_hi[:, g % JOBS, cols].bitcast(F32),
                                  ALU.subtract).then_inc(raw_free, 1)

            def split_hidden(b, i):
                dve.wait_ge(gelu_done, b * HT + i + 1 + GELU_CR)
                dve.wait_ge(y_step, b * HT + i - RING + 1 + Y_CR)
                dve.tensor_copy(h_hi[:, i % RING, :], hid[:, i % 2, :]).then_inc(h_hi_done, 1)
                dve.wait_ge(h_hi_done, b * HT + i + 1)
                dve.tensor_tensor(h_lo[:, i % RING, :], hid[:, i % 2, :], h_hi[:, i % RING, :].bitcast(F32),
                                  ALU.subtract).then_inc(h_lo_done, 1)

            def residual(b, i):
                j, c, _ = parts(i)
                shift = i // HT
                dve.wait_ge(y_step, b * HT + i + 1 + Y_CR)
                for t in range(TPC):
                    tile = c * TPC + t + shift * NT
                    xt = pr.x[:, b * NT + tile, :]
                    if j == 0:
                        dve.wait_ge(bias_added, b * NT + tile + 1)
                    elif t == 0:
                        dve.wait_ge(y_read, b * (HT // FT * TPC) + (i // FT + 1 - NCK) * TPC + READ_CR)
                    dve.scalar_tensor_tensor(out=xt, in0=y_of(i, t), scalar=pr.route_w[:, b + shift, j:j + 1], in1=xt,
                                             op0=ALU.mult, op1=ALU.add).then_inc(y_read, 1)

            def tile_stats(b, t):
                if t == 0:
                    pr.wait_apart(dve, y_read, (b + 1) * (HT // FT * TPC) + READ_CR)
                dve.bn_stats(stats[:, t, :], pr.x[:, b * NT + t, :]).then_inc(stats_done, 1)

            def batch_stats(b):
                pr.wait_apart(dve, stats_done, b * NT + NT)
                for t in range(NT):
                    dve.bn_aggr(mv[:, t, :], stats[:, t, :]).then_inc(mv_done, 1)
                pr.wait_apart(dve, mv_done, b * NT + NT)
                pr.wait_apart(dve, rstd_done, b + 1)
                dve.tensor_copy(pr.mean[:, bass.ts(b, NT)], mv[:, :, 0])
                dve.tensor_scalar(ve[:], mv[:, :, 1], EPS, None, ALU.add).then_inc(ve_done, 1)

            normalise(0, 0)
            for t in range(TPC):
                normalise(0, t + 1)
                prep_lo(0, t)
            for piece in range(PIECES):
                split_lo(0, piece)

            def body(b, first, last):
                for i in range(HT + LAG_RES + 1 if last else HT):
                    if i < HT:
                        split_hidden(b, i)
                        for t in preps_of_step(i, last):
                            if t + 1 < (NT if last else NT + TPC + 1):
                                normalise(b, t + 1)
                            prep_lo(b, t)
                        for piece in split_of_step(i, last):
                            split_lo(b, piece)
                    if (i >= LAG_RES or not first) and (i - LAG_RES) % FT == FT - 1:
                        residual(b, i - LAG_RES)
                    if not first and STATS_AT <= i < AGGR_AT:
                        tile_stats(b - 1, i - STATS_AT)
                    if not first and i == AGGR_AT:
                        batch_stats(b - 1)
                if last:
                    for t in range(NT):
                        tile_stats(b, t)
                    batch_stats(b)

            bodies_of(dve, body)

        @block.gpsimd
        def _(pool):
            def add_bias(b, t):
                shift = t // NT
                pr.wait_apart(pool, xn_ready, b * NT + t + 1)
                xt = pr.x[:, b * NT + t, :]
                pool.tensor_tensor(xt, xt, pr.ffn_bias[:, b + shift, :], ALU.add).then_inc(bias_added, 1)

            def rstd(b):
                pr.wait_apart(pool, ve_done, b + 1)
                pool.tensor_tensor(pr.rstd[:, bass.ts(b, NT)], ve[:], power[:], ALU.pow).then_inc(rstd_done, 1)

            pool.memset(power[:], -0.5).then_inc(rstd_done, 1)
            pool.wait_ge(rstd_done, 1)
            for t in range(TPC):
                add_bias(0, t)

            def body(b, first, last):
                for t in range(TPC, NT):
                    add_bias(b, t)
                if not first:
                    rstd(b - 1)
                if not last:
                    for t in range(NT, NT + TPC):
                        add_bias(b, t)
                else:
                    rstd(b)

            bodies_of(pool, body)


def expert_choice_phase(pr, y_out, xn_dram, wg_in, bg_in, w1_in, b1_in, w2_in, b2_in, w3_in, b3_in):
    nc = pr.nc
    Q = B // 2
    ER = 32
    WC = 3 * KD * D
    GT = Q * P
    R = 4
    PRE = 2
    with ExitStack() as outer:
        def osb(nm, shape, dt=F32):
            return outer.enter_context(nc.sbuf_tensor(f"f1.{nm}", shape, dt))

        rows = osb("rows", [P, Q, E1], U32)
        gatew = osb("gatew", [P, Q, E1])
        raw = osb("raw", [P, 2, WC])
        w_hi = osb("w_hi", [P, R, WC], F32R)
        w_lo = osb("w_lo", [P, R, WC], F32R)
        with ExitStack() as ctx:
            def sb(nm, shape, dt=F32):
                return ctx.enter_context(nc.sbuf_tensor(f"f1c.{nm}", shape, dt))

            def sem(nm):
                return pr.sem(f"f1c_{nm}")

            XR = 8
            xn = sb("xn", [P, XR, D])
            xT = sb("xT", [P, 2, KD, CHK])
            wg = sb("wg", [P, KD, ER])
            bg = sb("bg", [P, 1])
            lg = sb("lg", [P, S])
            ex = sb("ex", [P, S])
            vals = sb("vals", [P, K1])
            idx = sb("idx", [P, K1], U32)
            first_row = sb("first_row", [P, 1])
            nmax = sb("nmax", [P, 1])
            tot = sb("tot", [P, 1])
            rtot = sb("rtot", [P, 1])
            idxf = sb("idxf", [P, 2, K1])
            ev = sb("ev", [P, K1])
            pv = sb("pv", [P, 2, K1])
            const_in, row_set = sem("const_in"), sem("row_set")
            xn_ready, xn_sent = sem("xn_ready"), [sem(f"xn_sent{i}") for i in range(XR)]
            tr_done, xT_copied, logits_done = sem("tr_done"), sem("xT_copied"), sem("logits_done")
            step, nmax_done, exp_done, ev_done, pv_done = sem("step"), sem("nmax_done"), sem("exp_done"), sem("ev_done"), sem("pv_done")
            turned, x_written = sem("turned"), sem("x_written")
            idx_ready = sem("idx_ready")
            raw_in, w_hi_done, w_lo_done = [sem("raw_in0"), sem("raw_in1")], sem("w_hi_done"), sem("w_lo_done")
            lg_bank = [pr.bank[0], pr.bank[1]]
            t_bank = [pr.bank[2], pr.bank[3]]
            i_bank, v_bank = pr.bank[4], pr.bank[5]
            NCH8 = B * NCK
            block = ctx.enter_context(nc.Block())

            @block.sync
            def _(sp):
                sp.dma_start(wg[:], wg_in.rearrange("(c p) e -> p c e", p=P)).then_inc(const_in, 16)
                sp.dma_start(bg[:], bg_in).then_inc(const_in, 16)
                for e in range(PRE):
                    for n, w in enumerate((w1_in, w2_in, w3_in)):
                        sp.dma_start(raw[:, e, bass.ts(n, KD * D)].rearrange("p (c o) -> p c o", c=KD),
                                     w[e].rearrange("(c p) o -> p c o", p=P)).then_inc(raw_in[e], 16)
                for b in range(B):
                    sp.dma_start(y_out[b].rearrange("(t p) d -> p t d", p=P),
                                 pr.x[:, b * NT:(b + 1) * NT, :]).then_inc(x_written, 16)
                for i in range(B * NT):
                    sp.wait_ge(xn_ready, i + 1)
                    sp.dma_start(xn_dram[i * P:(i + 1) * P, :], xn[:, i % XR, :]).then_inc(xn_sent[i % XR], 16)
                for i in range(XR):
                    sp.wait_ge(xn_sent[i], 16 * (B * NT // XR))
                sp.wait_ge(x_written, 16 * B)

            @block.tensor
            def _(pe):
                pe.wait_ge(const_in, 32)
                for i in range(B * NT):
                    pe.wait_ge(xn_ready, i + 1)
                    if i >= 2:
                        pe.wait_ge(xT_copied, i - 1)
                    for kd in range(KD):
                        mm = pe.transpose(t_bank[i % 2][:, bass.ts(kd, P)], xn[:, i % XR, bass.ts(kd, P)], pr.ident[:])
                    mm.then_inc(tr_done, 1)
                    if i % TPC == TPC - 1:
                        c = i // TPC
                        b, half = c // NCK, c % NCK
                        pe.wait_ge(xT_copied, i + 1)
                        for kd in range(KD):
                            mm = pe.matmul(lg_bank[half][ER * b:ER * b + ER, :], wg[:, kd, :], xT[:, c % 2, kd, :],
                                           start=(kd == 0), stop=(kd == KD - 1))
                        mm.then_inc(logits_done, 1)
                pe.wait_ge(idx_ready, 1)
                pe.transpose(i_bank[:, 0:P], idxf[:].rearrange("p a k -> p (a k)"), pr.ident[:]).then_inc(turned, 1)
                pe.wait_ge(pv_done, 2)
                pe.transpose(v_bank[:, 0:P], pv[:].rearrange("p a k -> p (a k)"), pr.ident[:]).then_inc(turned, 1)

            @block.scalar
            def _(act):
                for i in range(B * NT):
                    act.wait_ge(tr_done, i + 1)
                    c, t = divmod(i, TPC)
                    if t == 0 and c >= 2:
                        act.wait_ge(logits_done, c - 1)
                    act.activation(xT[:, c % 2, :, bass.ts(t, P)],
                                   t_bank[i % 2][:, 0:D].rearrange("p (k t) -> p k t", k=KD), ACT.Copy).then_inc(xT_copied, 1)
                for e in range(PRE):
                    act.wait_ge(raw_in[e], 48)
                    act.activation(w_hi[:, e, :], raw[:, e, :], ACT.Copy).then_inc(w_hi_done, 1)
                act.wait_ge(nmax_done, 1)
                act.activation(ex[:], lg[:], ACT.Exp, bias=nmax[:], accum_out=tot[:]).then_inc(exp_done, 1)
                act.wait_ge(ev_done, 1)
                act.activation(ev[:], vals[:], ACT.Exp, bias=nmax[:]).then_inc(ev_done, 1)

            @block.vector
            def _(dve):
                for b in range(B):
                    dve.memset(first_row[ER * b:ER * b + ER, :], float(b * S)).then_inc(row_set, 1)
                for i in range(B * NT):
                    if i >= XR:
                        dve.wait_ge(xn_sent[i % XR], 16 * (i // XR))
                        dve.wait_ge(tr_done, i - XR + 1)
                    dve.tensor_scalar(xn[:, i % XR, :], pr.x[:, i, :], pr.mean[:, i:i + 1], pr.rstd[:, i:i + 1],
                                      ALU.subtract, ALU.mult).then_inc(xn_ready, 1)
                count = [0]

                def then(ins):
                    count[0] += 1
                    ins.then_inc(step, 1)
                    dve.wait_ge(step, count[0])

                dve.wait_ge(logits_done, NCH8)
                for half in range(2):
                    ins = dve.tensor_scalar(lg[:, bass.ts(half, CHK)], lg_bank[half][:], bg[:, 0:1], None, ALU.add)
                then(ins)
                for r in range(K1 // 8):
                    cols = bass.ts(r, 8)
                    then(dve.max(vals[:, cols], lg[:]))
                    if r == 0:
                        dve.tensor_scalar(nmax[:], vals[:, 0:1], -1.0, None, ALU.mult).then_inc(nmax_done, 1)
                    dve.max_index(idx[:, cols], vals[:, cols], lg[:])
                    if r == 0:
                        dve.wait_ge(exp_done, 1)
                    if r < K1 // 8 - 1:
                        then(dve.match_replace(lg[:], vals[:, cols], lg[:], LOWEST))
                then(dve.tensor_copy(ex[:, 0:1], tot[:]))
                dve.wait_ge(row_set, B)
                for a in range(2):
                    ins = dve.tensor_scalar(idxf[:, a, :], idx[:], first_row[:, 0:1], None, ALU.add)
                ins.then_inc(idx_ready, 1)
                dve.sem_inc(ev_done, 1)
                then(dve.reciprocal(rtot[:], tot[:]))
                dve.wait_ge(ev_done, 2)
                for a in range(2):
                    dve.tensor_scalar(pv[:, a, :], ev[:], rtot[:, 0:1], None, ALU.mult).then_inc(pv_done, 1)
                dve.wait_ge(turned, 2)
                for half in range(2):
                    lo = K1 * half
                    for dst, bank in ((rows, i_bank), (gatew, v_bank)):
                        src = bank[lo:lo + K1, 0:P].rearrange("p (q h e) -> p q h e", q=Q, h=2)[:, :, half, 0:E1]
                        dve.tensor_copy(dst[lo:lo + K1, :, :], src)

            @block.gpsimd
            def _(pool):
                for e in range(PRE):
                    pool.wait_ge(w_hi_done, e + 1)
                    pool.tensor_tensor(w_lo[:, e, :], raw[:, e, :], w_hi[:, e, :].bitcast(F32),
                                       ALU.subtract).then_inc(w_lo_done, 1)
                pool.wait_ge(w_lo_done, PRE)

        with ExitStack() as ctx:
            def sb(nm, shape, dt=F32):
                return ctx.enter_context(nc.sbuf_tensor(f"f1.{nm}", shape, dt))

            def sem(nm):
                return pr.sem(f"f1_{nm}")

            FETCH, L1, L2, OUT = 3, 1, 2, 3
            BODIES = E1 // R
            bias = sb("bias", [P, 3, E1])
            bias_now = sb("bias_now", [P, R, 3])
            gate_now = sb("gate_now", [P, R, Q])
            cur_in = sb("cur_in", [P, R, Q], U32)
            cur_out = sb("cur_out", [P, R, Q], U32)
            xg = sb("xg", [P, R, Q, D])
            a_hi = sb("a_hi", [P, 3, 2, KD * GT], F32R)
            a_lo = sb("a_lo", [P, 3, 2, KD * GT], F32R)
            act_f = sb("act_f", [P, 2, 2, KD * GT])
            yo = sb("yo", [P, R, Q, D])
            raw_in = [sem("raw_in0"), sem("raw_in1")]
            bias_in, bias_set = sem("bias_in"), sem("bias_set")
            cur_set, fetched = sem("cur_set"), sem("fetched")
            xg_in = [[sem(f"xg_in{s}{q}") for q in range(Q)] for s in range(R)]
            w_hi_done, w_lo_done = sem("w_hi_done"), sem("w_lo_done")
            in_T, in_hi, in_lo = sem("in_T"), sem("in_hi"), sem("in_lo")
            h_done, relu_done, h_hi, h_lo = ([sem(f"{nm}{n}") for n in range(2)]
                                             for nm in ("h_done", "relu_done", "h_hi", "h_lo"))
            y_done, y_out_ready, yo_free = sem("y_done"), sem("y_out_ready"), sem("yo_free")
            added = [sem(f"added{q}") for q in range(Q)]
            t_bank = [pr.bank[0], pr.bank[1]]
            h_bank = [[pr.bank[2], pr.bank[3]], [pr.bank[4], pr.bank[5]]]
            y_bank = [pr.bank[6], pr.bank[7]]
            block = ctx.enter_context(nc.Block())

            def w_of(s, n, kd, lo, hi):
                base = (n * KD + kd) * D
                return (w_hi[:, s % R, base + lo:base + hi], w_lo[:, s % R, base + lo:base + hi])

            def bodies_of(engine, body):
                body(0, first=True, last=False)
                with engine.Fori(1, BODIES - 1) as it:
                    body(it, first=False, last=False)
                body(BODIES - 1, first=False, last=True)

            def valid(s, first, last):
                return (s >= 0 or not first) and (s < R or not last)

            @block.sync
            def _(sp):
                for n, bi in enumerate((b1_in, b2_in, b3_in)):
                    sp.dma_start(bias[:, n, :], bi.to_broadcast([P, E1])).then_inc(bias_in, 16)

                def body(it, first, last):
                    for s in range(PRE if first else 0, R):
                        sp.wait_ge(w_lo_done, it * R + s - 1)
                        for n, w in enumerate((w1_in, w2_in, w3_in)):
                            sp.dma_start(raw[:, s % 2, bass.ts(n, KD * D)].rearrange("p (c o) -> p c o", c=KD),
                                         w[bass.ds(it * R + s, 1)].rearrange("e (c p) o -> p (e c) o", p=P)
                                         ).then_inc(raw_in[s % 2], 16)

                bodies_of(sp, body)
                for s in range(2):
                    sp.wait_ge(raw_in[s], 48 * (E1 - PRE) // 2)
                sp.wait_ge(bias_in, 48)

            @block.gpsimd
            def _(pool):
                def fetch(it, s):
                    pr.wait_apart(pool, cur_set, it * R + s + 1).then_inc(fetched, 1)
                    for q in range(Q):
                        pool.indirect_dma_start(xg[:, s % R, q, :], None, xn_dram,
                                                bass.IndirectOffsetOnAxis(ap=cur_in[:, s % R, q:q + 1], axis=0)
                                                ).then_inc(xg_in[s % R][q], 16)

                def add_out(it, s, first):
                    e = it * R + s
                    pr.wait_apart(pool, y_out_ready, e + 1)
                    for q in range(Q):
                        if not (first and s == 0):
                            before = pr.wait_apart(pool, added[q], e * 16)
                            if q == Q - 1:
                                before.then_inc(yo_free, 1)
                        pool.indirect_dma_start(y_out.rearrange("b s d -> (b s) d"),
                                                bass.IndirectOffsetOnAxis(ap=cur_out[:, s % R, q:q + 1], axis=0),
                                                yo[:, s % R, q, :], None, compute_op=ALU.add).then_inc(added[q], 16)

                pool.sem_inc(yo_free, R)
                for s in range(FETCH):
                    fetch(0, s)

                def body(it, first, last):
                    for s in range(R + OUT if last else R):
                        if valid(s + FETCH, first, last):
                            fetch(it, s + FETCH)
                        if valid(s - OUT, first, last):
                            add_out(it, s - OUT, first)

                bodies_of(pool, body)
                for q in range(Q):
                    pool.wait_ge(added[q], 16 * E1)

            @block.tensor
            def _(pe):
                def turn(it, s):
                    rnd, slot = divmod(s, R)
                    for q in range(Q):
                        pe.wait_ge(xg_in[slot][q], it * 16 + (rnd + 1) * 16)
                    pe.wait_ge(in_lo, it * R + s + 1)
                    for kd in range(KD):
                        for q in range(Q):
                            mm = pe.transpose(t_bank[s % 2][:, kd * GT + q * P:kd * GT + q * P + P],
                                              xg[:, slot, q, bass.ts(kd, P)], pr.ident[:])
                    mm.then_inc(in_T, 1)

                def products(dst, s, n, kd, lo, hi, a0, a1, weights_first):
                    a = slice(kd * GT + a0, kd * GT + a1)
                    ah, al = a_hi[:, n, s % 2, a], a_lo[:, n, s % 2, a]
                    wh, wl = w_of(s, n, kd, lo, hi)
                    for i, (w, x) in enumerate(((wh, ah), (wh, al), (wl, ah))):
                        left, right = (w, x) if weights_first else (x, w)
                        mm = pe.matmul(dst, left, right, start=(kd == 0 and i == 0), stop=(kd == KD - 1 and i == 2))
                    return mm

                def layer(it, s, n):
                    e = it * R + s
                    if n == 0:
                        pe.wait_ge(in_lo, e + 3)
                        pe.wait_ge(w_lo_done, e + 1)
                    else:
                        pe.wait_ge(h_lo[0], e + 3)
                    pe.wait_ge(h_lo[n], e + 1)
                    for m in range(KD):
                        for kd in range(KD):
                            mm = products(h_bank[n][s % 2][:, bass.ts(m, GT)], s, n, kd, m * P, m * P + P, 0, GT, True)
                    mm.then_inc(h_done[n], 1)

                def last_layer(it, s, first):
                    e = it * R + s
                    pe.wait_ge(h_lo[1], e + 3)
                    if not first or s >= 2:
                        pe.wait_ge(y_out_ready, e - 1)
                    for q in range(Q):
                        for kd in range(KD):
                            mm = products(y_bank[s % 2][:, bass.ts(q, D)], s, 2, kd, 0, D, q * P, q * P + P, False)
                    mm.then_inc(y_done, 1)

                turn(0, 0)

                def body(it, first, last):
                    for s in range(R + L2 if last else R):
                        if valid(s + 1, first, last):
                            turn(it, s + 1)
                        if valid(s, first, last):
                            layer(it, s, 0)
                        if valid(s - L1, first, last):
                            layer(it, s - L1, 1)
                        if valid(s - L2, first, last):
                            last_layer(it, s - L2, first)

                bodies_of(pe, body)

            @block.scalar
            def _(act):
                def split_weights(it, s):
                    rnd, half = divmod(s, 2)
                    act.wait_ge(raw_in[half], it * (R // 2 * 48) + rnd * 48)
                    act.wait_ge(y_done, it * R + s + 1)
                    act.activation(w_hi[:, s % R, :], raw[:, half, :], ACT.Copy).then_inc(w_hi_done, 1)

                def input_hi(it, s):
                    e = it * R + s
                    act.wait_ge(in_T, e + 1)
                    act.wait_ge(h_done[0], e + 1)
                    act.activation(a_hi[:, 0, s % 2, :], t_bank[s % 2][:], ACT.Copy).then_inc(in_hi, 1)

                def relu(it, s, n):
                    e = it * R + s
                    if n == 0:
                        act.wait_ge(bias_set, e + 1)
                    act.wait_ge(h_done[n], e + 3)
                    act.wait_ge(h_lo[n], e + 1)
                    act.activation(act_f[:, n, s % 2, :], h_bank[n][s % 2][:], ACT.Relu,
                                   bias=bias_now[:, s % R, n:n + 1]).then_inc(relu_done[n], 1)
                    act.wait_ge(relu_done[n], e + 1)
                    if n == 0:
                        act.wait_ge(h_done[1], e + 1)
                    else:
                        act.wait_ge(y_done, e - 1 + R)
                    act.activation(a_hi[:, n + 1, s % 2, :], act_f[:, n, s % 2, :], ACT.Copy).then_inc(h_hi[n], 1)

                act.wait_ge(bias_in, 48)
                input_hi(0, 0)

                def body(it, first, last):
                    for s in range(R + L1 if last else R):
                        if valid(s + 1, first, last):
                            if not (first and s + 1 < PRE):
                                split_weights(it, s + 1)
                            input_hi(it, s + 1)
                        if valid(s, first, last):
                            relu(it, s, 0)
                        if valid(s - L1, first, last):
                            relu(it, s - L1, 1)

                bodies_of(act, body)

            @block.vector
            def _(dve):
                dve.sem_inc(w_lo_done, PRE)
                dve.sem_inc(in_lo, 2)
                for n in range(2):
                    dve.sem_inc(h_done[n], 2)
                    dve.sem_inc(h_lo[n], 2)
                dve.sem_inc(y_done, R)
                dve.wait_ge(bias_in, 48)

                def rows_of(it, s):
                    return rows[:, :, bass.ds(it * R + s, 1)].rearrange("p q o -> p (q o)")

                def set_rows(it, s, again):
                    if again:
                        pr.wait_apart(dve, fetched, (it - 1) * R + s + 1)
                    dve.tensor_copy(cur_in[:, s % R, :], rows_of(it, s)).then_inc(cur_set, 1)

                def set_scales(it, s, again):
                    e = it * R + s
                    if again:
                        pr.wait_apart(dve, y_out_ready, e - R + 1)
                    dve.tensor_copy(bias_now[:, s % R, :], bias[:, :, bass.ds(e, 1)].rearrange("p n o -> p (n o)"))
                    dve.tensor_copy(gate_now[:, s % R, :],
                                    gatew[:, :, bass.ds(e, 1)].rearrange("p q o -> p (q o)")).then_inc(bias_set, 1)

                def weights_lo(it, s):
                    dve.wait_ge(w_hi_done, it * R + s - PRE + 1)
                    dve.tensor_tensor(w_lo[:, s % R, :], raw[:, s % 2, :], w_hi[:, s % R, :].bitcast(F32),
                                      ALU.subtract).then_inc(w_lo_done, 1)

                def input_lo(it, s):
                    dve.wait_ge(in_hi, it * R + s + 1)
                    dve.tensor_tensor(a_lo[:, 0, s % 2, :], t_bank[s % 2][:], a_hi[:, 0, s % 2, :].bitcast(F32),
                                      ALU.subtract).then_inc(in_lo, 1)

                def hidden_lo(it, s, n):
                    dve.wait_ge(h_hi[n], it * R + s + 1)
                    dve.tensor_tensor(a_lo[:, n + 1, s % 2, :], act_f[:, n, s % 2, :],
                                      a_hi[:, n + 1, s % 2, :].bitcast(F32), ALU.subtract).then_inc(h_lo[n], 1)

                def weigh(it, s):
                    e = it * R + s
                    dve.wait_ge(y_done, e + 1 + R)
                    dve.wait_ge(yo_free, e + 1)
                    for q in range(Q):
                        dve.tensor_scalar(yo[:, s % R, q, :], y_bank[s % 2][:, bass.ts(q, D)], bias_now[:, s % R, 2:3],
                                          gate_now[:, s % R, q:q + 1], ALU.add, ALU.mult)
                    dve.tensor_copy(cur_out[:, s % R, :], rows_of(it, s)).then_inc(y_out_ready, 1)

                for s in range(R):
                    set_rows(0, s, False)
                set_scales(0, 0, False)
                input_lo(0, 0)

                def body(it, first, last):
                    for s in range(R + OUT if last else R):
                        if valid(s - OUT, first, last):
                            weigh(it, s - OUT)
                        if valid(s + 1, first, last):
                            if not (first and s + 1 < PRE):
                                weights_lo(it, s + 1)
                            input_lo(it, s + 1)
                        if valid(s + R, first, last) and s < R and not last:
                            set_rows(it, s + R, True)
                        if valid(s, first, last):
                            hidden_lo(it, s, 0)
                        if valid(s - L1, first, last):
                            hidden_lo(it, s - L1, 1)
                        if valid(s + 1, first, last):
                            set_scales(it, s + 1, not first or s + 1 >= R)

                bodies_of(dve, body)


def build(nc, x_in, ident_in, iota_in, ctxT_in, a0, gate_in, f0, a1, f1, xn_dram, y_out, upto=9):
    with ExitStack() as ctx:
        pr = Program(nc, ctx)
        load_phase(pr, x_in, ident_in)
        if upto >= 1:
            attention_phase(pr, "a0", 8, ctxT_in, *a0)
        if upto >= 2:
            router_phase(pr, gate_in, f0[3], iota_in)
            ffn0_phase(pr, f0[0], f0[1], f0[2])
        if upto >= 3:
            attention_phase(pr, "a1", 16, ctxT_in, *a1)
        if upto >= 4:
            expert_choice_phase(pr, y_out, xn_dram, *f1)
        else:
            out_written = pr.sem("out_written")
            with nc.Block() as block:
                @block.sync
                def _(sp):
                    for b in range(B):
                        sp.dma_start(y_out[b].rearrange("(t p) d -> p t d", p=P),
                                     pr.x[:, b * NT:(b + 1) * NT, :]).then_inc(out_written, 16)
                    sp.wait_ge(out_written, 16 * B)


def layout(inputs):
    import numpy as np

    def arr(name):
        return np.asarray(inputs[name])

    def whole(a):
        return np.ascontiguousarray(a)

    out = {
        "x_in": arr("x"),
        "ident_in": np.eye(P, dtype=np.float32),
        "iota_in": whole(np.broadcast_to(np.arange(E0, dtype=np.float32), (P, E0))),
        "ctxT_in": whole(arr("ctx_768").transpose(2, 0, 1).reshape(DC, B * NC)),
        "gate_in": arr("L0_ffn_gate_w"),
        "f0_w1": arr("L0_ffn_w1"),
        "f0_b1": whole(arr("L0_ffn_b1").reshape(E0, FT, P).transpose(0, 2, 1)),
        "f0_w2": arr("L0_ffn_w2"),
        "f0_b2": arr("L0_ffn_b2"),
    }
    for layer in (0, 1):
        a = f"L{layer}_xattn_"
        out[f"a{layer}_wqT"] = whole(arr(a + "Wq").T)
        out[f"a{layer}_wk"] = arr(a + "Wk")
        out[f"a{layer}_wv"] = arr(a + "Wv")
        out[f"a{layer}_wo"] = arr(a + "Wo")
        out[f"a{layer}_bo"] = arr(a + "bo").reshape(1, D)
    pad = np.zeros((D, 32 - E1), np.float32)
    out["f1_wg"] = np.concatenate([arr("L1_ffn_Wg"), pad], axis=1)
    out["f1_bg"] = np.tile(np.concatenate([arr("L1_ffn_bg"), pad[0]]), B).reshape(P, 1)
    for n in (1, 2, 3):
        out[f"f1_w{n}"] = arr(f"L1_ffn_w{n}")
        out[f"f1_b{n}"] = arr(f"L1_ffn_b{n}").reshape(1, E1)
    return {k: whole(v) for k, v in out.items()}


def build_all(nc, a, out, upto=9):
    att = [[a[f"a{n}_{w}"] for w in ("wqT", "wk", "wv", "wo", "bo")] for n in (0, 1)]
    build(nc, a["x_in"], a["ident_in"], a["iota_in"], a["ctxT_in"], att[0], a["gate_in"],
          [a["f0_w1"], a["f0_b1"], a["f0_w2"], a["f0_b2"]], att[1],
          [a[k] for k in ("f1_wg", "f1_bg", "f1_w1", "f1_b1", "f1_w2", "f1_b2", "f1_w3", "f1_b3")],
          nc.dram_tensor("xn_rows", [B * S, D], F32).ap(), out, upto)


def kernel(**inputs):
    import numpy as np
    from concourse import bacc
    from concourse.bass_utils import run_bass_kernel_spmd

    nc = bacc.Bacc("TRN2", target_bir_lowering=False, num_devices=1)
    arrays = layout(inputs)
    aps = {k: nc.dram_tensor(k, v.shape, mybir.dt.from_np(v.dtype), kind="ExternalInput").ap() for k, v in arrays.items()}
    out = nc.dram_tensor("out", (B, S, D), F32, kind="ExternalOutput").ap()
    build_all(nc, aps, out)
    r = run_bass_kernel_spmd(nc, [arrays], core_ids=[0])
    return np.asarray(r.results[0]["out"])
```

```python
from contextlib import ExitStack

import concourse.bass as bass
from concourse import mybir

F32 = mybir.dt.float32
F32R = mybir.dt.float32r
U32 = mybir.dt.uint32
ALU = mybir.AluOpType
ACT = mybir.ActivationFunctionType
AX_X = mybir.AxisListType.X

P = 128
B, S, D = 4, 1024, 256
KD = D // P
NT = S // P
NC, DC = 77, 192
CH = DC // 2
DH = 64
GH = 8
GP = GH // 2
GW = GH * NC
HALF = GW // 2
NCH = -(-GW // P)
PW = NCH * P
E0, F0, TOPK0 = 8, 1024, 2
FT = F0 // P
CHK = 512
NCK = S // CHK
TPC = CHK // P
E1, K1 = 16, 64
HEADS = (8, 16)
STAGE = max(KD * F0 + FT * D, HEADS[1] * D)
EPS = 1e-5
LOWEST = -3.0e38


class Program:

    def __init__(self, nc, ctx):
        self.nc, self.ctx = nc, ctx
        self.bank = [ctx.enter_context(nc.psum_tensor(f"bank{i}", [P, 512], F32)) for i in range(8)]
        self.x = self.sb("x_res", [P, B * NT, D])
        self.mean = self.sb("mean", [P, B * NT])
        self.rstd = self.sb("rstd", [P, B * NT])
        self.ident = self.sb("ident", [P, P])
        self.route_w = self.sb("route_w", [P, B, TOPK0])
        self.route_i = self.sb("route_i", [P, B, 8], U32)
        self.ffn_bias = self.sb("ffn_bias", [P, B, D])

        self.stage = self.sb("stage", [P, STAGE])
        pairs = [heads // 2 for heads in HEADS]
        self.kT = [self.sb(f"kT{n}", [P, pairs[n], B * NC]) for n in range(2)]
        self.vT = [self.sb(f"vT{n}", [P, pairs[n], B * NC]) for n in range(2)]
        self.weights_in = [self.sem(f"weights_in{n}") for n in range(2)]

        self.acc = self.sb("acc0", [P, 2, D])
        self.acc_done = self.sem("acc0_done")

        self.carry = self.sb("wait_carry", [P, 224])
        self.carries = 0
        self.one = self.sb("one", [P, 1])

    def wait_apart(self, engine, sem, value):
        engine.wait_ge(sem, value)
        spare = self.carry[:, self.carries:self.carries + 1]
        if engine is self.nc.vector:
            ins = engine.memset(spare, 0.0)
        else:
            ins = engine.tensor_tensor(spare, self.one[:], self.one[:], ALU.mult)
        self.carries += 1
        return ins

    def query_weights(self, layer):
        pairs = HEADS[layer] // 2
        return (self.stage[:, 0:pairs * D].rearrange("p (c n) -> p c n", c=pairs),
                self.stage[:, STAGE // 2:STAGE // 2 + pairs * D].rearrange("p (c n) -> p c n", c=pairs))

    def sb(self, name, shape, dt=F32):
        return self.ctx.enter_context(self.nc.sbuf_tensor(name, shape, dt))

    def sem(self, name):
        return self.ctx.enter_context(self.nc.semaphore(name))


def attention_phase(pr, name, heads, kT, vT, bo_in, load=None):
    nc = pr.nc
    groups = heads // GH
    pairs = heads // 2
    bodies = B * groups // 2
    UB = 2 * NT
    PREPS = NT * (2 // groups)
    AHEAD = 2
    LAG_T, LAG_AV, LAG_RES, LAG_ST, LAG_AG, LAG_FIN = 2, 3, 4, 6, 8, 9
    STEPS = UB + LAG_FIN + 1
    ROUTER_AT = 12

    def place(it, k):
        shift, kk = divmod(k, UB)
        p, t = divmod(kk, NT)
        return ((it + shift) * 2 + p if groups == 1 else it + shift), p, t

    def prep_due(k):
        return groups == 1 or k % UB < NT

    def prep_count(it, k):
        return it * PREPS + (k if groups == 1 else k // UB * NT + k % UB)

    with ExitStack() as ctx:
        def sb(nm, shape, dt=F32):
            return ctx.enter_context(nc.sbuf_tensor(f"{name}.{nm}", shape, dt))

        def sem(nm):
            return pr.sem(f"{name}_{nm}")

        layer = HEADS.index(heads)
        wqT, wo = pr.query_weights(layer)
        bo = sb("bo", [P, D])
        vdiag = sb("vdiag", [P, GP * (PW + 2 * NC)])
        kdiag = sb("kdiag", [P, GP, 2, NC])
        g_hi = sb("g_hi", [P, 2, KD, GW], F32R)
        g_lo = sb("g_lo", [P, 2, KD, GW], F32R)
        v_hi = sb("v_hi", [P, 2, NCH, D], F32R)
        v_lo = sb("v_lo", [P, 2, NCH, D], F32R)
        xT_hi = sb("xT_hi", [P, KD, S], F32R)
        xT_lo = sb("xT_lo", [P, KD, S], F32R)
        ER = 4
        ex = sb("ex", [P, ER, PW])
        pT = sb("pT", [P, 2, PW])
        pT_hi = sb("pT_hi", [P, 2, PW], F32R)
        pT_lo = sb("pT_lo", [P, 2, PW], F32R)
        xn = sb("xn", [P, 2, D])
        mx = sb("mx", [P, 2, GH])
        sm = sb("sm", [P, 2, GH])
        rc = sb("rc", [P, 2, GH])
        stats = sb("stats", [P, NT, 6])
        mv = sb("mv", [P, 2, NT, 2])
        ve = sb("ve", [P, 2, NT])
        power = sb("power", [P, NT])
        if load:
            wk, wv = ex[0:CH, 0:2, 0:heads * DH], ex[0:CH, 2:4, 0:heads * DH]
            w_next = sb("w_next", [CH, 2, 2, HEADS[1] * DH])
            cT = sb("ctxT", [CH, 2, B * NC])
            proj_in, next_in = sem("proj_in"), [sem("next_wk_in"), sem("next_wv_in")]
            ident_in = sem("ident_in")
            proj_done, proj_copied = sem("proj_done"), sem("proj_copied")
        bo_read = sem("bo_in")
        kdiag_ready = sem("kdiag_ready")
        kdiag_zeroed, vdiag_zeroed, power_set = sem("kdiag_zeroed"), sem("vdiag_zeroed"), sem("power_set")
        misc_written, misc_hi, misc_free = sem("misc_written"), sem("misc_hi"), sem("misc_free")
        vdiag_ready = sem("vdiag_ready")
        xn_ready, bo_added = sem("xn_ready"), sem("bo_added")
        sc_done, max_done, sub_done = sem("scores_done"), sem("max_done"), sem("sub_done")
        exp_done, sum_done, rec_done, mul_done = sem("exp_done"), sem("sum_done"), sem("rec_done"), sem("mul_done")
        tr_done, pT_copied, pT_lo_done = sem("probsT_done"), sem("pT_copied"), sem("pT_lo_done")
        av_done, res_done = sem("av_done"), sem("res_done")
        ve_done, rstd_done = sem("ve_done"), sem("rstd_done")

        BARE, LATE = (0, 2) if load else (B - 1, B - 1)
        bare_stats = sb("bare_stats", [P, B, NT, 6])
        bare_mv = sb("bare_mv", [P, B, NT, 2])
        bare_ve = sb("bare_ve", [P, B, NT])
        bare_stats_done, bare_mv_done, bare_ve_done = sem("bare_stats_done"), sem("bare_mv_done"), sem("bare_ve_done")
        if load:
            batch_in = [sem(f"batch_in{b}") for b in range(B)]

        score_bank = [[pr.bank[0], pr.bank[1]], [pr.bank[2], pr.bank[3]]]
        probT_bank = [pr.bank[4], pr.bank[5]]
        av_bank, misc_bank = pr.bank[6], pr.bank[7]
        first_bank = [pr.bank[j] for j in (4, 5, 6, 7, 0, 1, 4, 3, 2)]
        CPB = 4

        V_USES = [(c, min(2, NCH - c)) for c in range(0, NCH, 2)]
        SETUP = 2 * KD + len(V_USES)
        assert SETUP <= NT

        def uses_of_step(it, k, last):
            uses = []
            if prep_due(k + AHEAD) and not (last and k + AHEAD >= UB):
                uses.append(("prep", k + AHEAD))
            if k % NT < SETUP and not (last and k >= NT):
                uses.append(("setup", k // NT + 1, k % NT))
            return uses

        FIRST_USES = [("setup", 0, j) for j in range(SETUP)] + [("prep", k) for k in range(AHEAD)]
        PER_BODY = PREPS + 2 * SETUP

        def numbered(it, last):
            at, out = len(FIRST_USES) + it * PER_BODY, []
            for k in range(UB):
                now = []
                for use in uses_of_step(it, k, last):
                    now.append((at, use))
                    at = at + 1
                out.append(now)
            return out

        def bodies_of(engine, body):
            body(0, first=True, last=bodies == 1)
            if bodies > 3:
                with engine.Fori(1, bodies - 1) as it:
                    body(it, first=False, last=False)
            elif bodies == 3:
                body(1, first=False, last=False)
            if bodies > 1:
                body(bodies - 1, first=False, last=True)

        def finishes(k):
            return groups == 1 or k % UB >= NT

        def vdiag_rows(lo, off):
            v = vdiag[lo:lo + DH, :].rearrange("p (g z) -> p g z", g=GP)
            return v[:, :, off:off + NC]

        def pass_of(it, q):
            b, p, _ = place(it, q * NT)
            return b, p, (0 if groups == 1 else p)

        def first_preps():
            return [(at, use) for at, use in enumerate(FIRST_USES) if use[0] == "prep"]

        def setup(pe, it, bank, q, j):
            b, p, g = pass_of(it, q)
            if j < 2 * KD:
                kd, half = divmod(j, 2)
                for k in range(GP // 2):
                    pair = half * GP // 2 + k
                    mm = pe.matmul(bank[:, bass.ts(k, 2 * NC)], wqT[:, g * GP + pair, bass.ts(kd, P)],
                                   kdiag[:, pair, :, :].rearrange("p o j -> p (o j)"), start=True, stop=True)
            else:
                c0, m = V_USES[j - 2 * KD]
                for c in range(c0, c0 + m):
                    inside = [h for h in range(GP) if h * 2 * NC < (c + 1) * P and (h + 1) * 2 * NC > c * P]
                    for h in inside:
                        mm = pe.matmul(bank[:, bass.ts(c - c0, D)], vdiag[:, h * PW + c * P:h * PW + c * P + P],
                                       wo[:, g * GP + h, :], start=(h == inside[0]), stop=(h == inside[-1]))
            return mm

        def setup_hi(act, it, bank, q, j):
            _, p, _ = pass_of(it, q)
            if j < 2 * KD:
                return act.activation(g_hi[:, p, j // 2, bass.ts(j % 2, HALF)], bank[:, 0:HALF], ACT.Copy,
                                      scale=float(DH) ** -0.5)
            c0, m = V_USES[j - 2 * KD]
            return act.activation(v_hi[:, p, c0:c0 + m, :].rearrange("p c d -> p (c d)"), bank[:, 0:m * D], ACT.Copy)

        def setup_lo(dve, it, bank, q, j):
            _, p, _ = pass_of(it, q)
            if j < 2 * KD:
                return dve.scalar_tensor_tensor(out=g_lo[:, p, j // 2, bass.ts(j % 2, HALF)], in0=bank[:, 0:HALF],
                                                scalar=float(DH) ** -0.5,
                                                in1=g_hi[:, p, j // 2, bass.ts(j % 2, HALF)].bitcast(F32),
                                                op0=ALU.mult, op1=ALU.subtract)
            c0, m = V_USES[j - 2 * KD]
            return dve.tensor_tensor(v_lo[:, p, c0:c0 + m, :].rearrange("p c d -> p (c d)"), bank[:, 0:m * D],
                                     v_hi[:, p, c0:c0 + m, :].bitcast(F32).rearrange("p c d -> p (c d)"), ALU.subtract)

        def place_kv(dve, it, q, done):
            b, _, g = pass_of(it, q)
            pr.wait_apart(dve, misc_free, done + 1)
            for odd in range(2):
                lo = DH * odd
                dve.tensor_copy(vdiag_rows(lo, NC * odd), vT[lo:lo + DH, g * GP:(g + 1) * GP, bass.ts(b, NC)])
                ins = dve.tensor_copy(kdiag[lo:lo + DH, :, odd, :], kT[lo:lo + DH, g * GP:(g + 1) * GP, bass.ts(b, NC)])
            ins.then_inc(vdiag_ready, 1)

        OWN = 2 * pairs
        NEXT = HEADS[1] if load else 0

        def next_of_setup(j):
            if j < 0:
                return range(0, NEXT // 2)
            return range(NEXT // 2 + j * NEXT // 2 // SETUP, NEXT // 2 + (j + 1) * NEXT // 2 // SETUP)

        def take_stats(dve, b, t):
            if load and t == 0:
                dve.wait_ge(batch_in[b], 16)
            dve.bn_stats(bare_stats[:, b, t, :], pr.x[:, b * NT + t, :]).then_inc(bare_stats_done, 1)

        def take_mean(dve, b):
            dve.wait_ge(bare_stats_done, ((b + 1 if b < LATE else B) - BARE) * NT)
            for t in range(NT):
                dve.bn_aggr(bare_mv[:, b, t, :], bare_stats[:, b, t, :]).then_inc(bare_mv_done, 1)
            dve.wait_ge(bare_mv_done, (b + 1 - BARE) * NT)
            dve.tensor_copy(pr.mean[:, bass.ts(b, NT)], bare_mv[:, b, :, 0])
            dve.tensor_scalar(bare_ve[:, b, :], bare_mv[:, b, :, 1], EPS, None, ALU.add).then_inc(bare_ve_done, 1)

        def take_rstd(pool, b):
            pool.wait_ge(bare_ve_done, b + 1 - BARE)
            pool.tensor_tensor(pr.rstd[:, bass.ts(b, NT)], bare_ve[:, b, :], power[:], ALU.pow)

        with nc.Block() as block:
            @block.sync
            def _(sp):
                if load:
                    x_in, ident, ctxT_in, wk_in, wv_in, wqT_in, wo_in = load

                    def halves(w):
                        return w.rearrange("(c p) n -> p c n", p=CH)

                    def batch(b):
                        return pr.x[:, bass.ts(b, NT), :], x_in[b].rearrange("(t p) d -> p t d", p=P), batch_in[b]

                    for dst, src, done in ((cT[:], halves(ctxT_in), proj_in), (wk, halves(wk_in[0]), proj_in),
                                           (wv, halves(wv_in[0]), proj_in), (w_next[:, 0], halves(wk_in[1]), next_in[0]),
                                           batch(0),
                                           (wqT, wqT_in.rearrange("(c p) n -> p c n", p=P), pr.weights_in[0]),
                                           (wo, wo_in.rearrange("(c p) n -> p c n", p=P), pr.weights_in[0]),
                                           (pr.ident[:], ident, ident_in), batch(1),
                                           (w_next[:, 1], halves(wv_in[1]), next_in[1]), batch(2), batch(3)):
                        sp.dma_start(dst, src).then_inc(done, 16)
                sp.dma_start(bo[:], bo_in.to_broadcast([P, D])).then_inc(bo_read, 16)
                if load:
                    sp.wait_ge(ident_in, 16)
                sp.wait_ge(bo_read, 16)

            @block.tensor
            def _(pe):
                def project(dst, w, j):
                    for c in range(2):
                        mm = pe.matmul(dst[:, 0:B * NC], w[:, c, bass.ts(j, P)], cT[:, c, :], start=(c == 0), stop=(c == 1))
                    mm.then_inc(proj_done, 1)

                def project_next(j):
                    for m in next_of_setup(j):
                        half, mm = divmod(m, NEXT // 2)
                        if mm == 0:
                            pe.wait_ge(next_in[half], 16)
                        pe.wait_ge(proj_copied, OWN + m - 1)
                        project(pr.bank[2 + m % 2], w_next[:, half], mm)

                if load:
                    pe.wait_ge(proj_in, 48)
                    for j in range(OWN):
                        if j >= 4:
                            pe.wait_ge(proj_copied, j - 3)
                        project(pr.bank[j % 4], wk if j < pairs else wv, j % pairs)
                    project_next(-1)
                pe.wait_ge(pr.weights_in[layer], 32)
                for j in range(SETUP):
                    if j == 0:
                        pe.wait_ge(kdiag_ready, 1)
                    if j == 2 * KD:
                        pe.wait_ge(vdiag_ready, 1)
                    if j == SETUP - 1:
                        pe.wait_ge(misc_free, 2)
                    setup(pe, 0, first_bank[j], 0, j).then_inc(misc_written, 1)
                    project_next(j)

            @block.scalar
            def _(act):
                def project_copy(n, m, bank):
                    act.wait_ge(proj_done, m + 1 + (OWN if n else 0))
                    kv, j = divmod(m, HEADS[n] // 2)
                    dst = (pr.vT if kv else pr.kT)[n][:, j, :]
                    act.activation(dst, bank[:, 0:B * NC], ACT.Copy).then_inc(proj_copied, 1)

                if load:
                    for j in range(OWN):
                        project_copy(0, j, pr.bank[j % 4])
                    for m in next_of_setup(-1):
                        project_copy(1, m, pr.bank[2 + m % 2])
                for j in range(SETUP):
                    act.wait_ge(misc_written, j + 1)
                    setup_hi(act, 0, first_bank[j], 0, j).then_inc(misc_hi, 1)
                    for m in next_of_setup(j):
                        project_copy(1, m, pr.bank[2 + m % 2])

            @block.vector
            def _(dve):
                dve.memset(ex[:, :, GW:PW], 0.0)
                dve.sem_inc(sub_done, 2)
                dve.sem_inc(tr_done, ER)
                dve.sem_inc(av_done, 2)
                dve.sem_inc(pT_copied, 1)
                dve.sem_inc(res_done, 1)
                dve.sem_inc(misc_free, 1)
                if load:
                    for b in range(BARE, LATE):
                        for t in range(NT):
                            take_stats(dve, b, t)
                        take_mean(dve, b)
                    dve.wait_ge(proj_copied, OWN)
                dve.wait_ge(kdiag_zeroed, 1)
                for odd in range(2):
                    lo = DH * odd
                    ins = dve.tensor_copy(kdiag[lo:lo + DH, :, odd, :], kT[lo:lo + DH, 0:GP, 0:NC])
                ins.then_inc(kdiag_ready, 1)
                dve.wait_ge(vdiag_zeroed, 1)
                for odd in range(2):
                    lo = DH * odd
                    ins = dve.tensor_copy(vdiag_rows(lo, NC * odd), vT[lo:lo + DH, 0:GP, 0:NC])
                ins.then_inc(vdiag_ready, 1)
                for j in range(SETUP):
                    dve.wait_ge(misc_hi, j + 1)
                    setup_lo(dve, 0, first_bank[j], 0, j).then_inc(misc_free, 1)
                place_kv(dve, 0, 1, SETUP)

            @block.gpsimd
            def _(pool):
                pool.memset(kdiag[:], 0.0).then_inc(kdiag_zeroed, 1)
                pool.memset(vdiag[:], 0.0).then_inc(vdiag_zeroed, 1)
                pool.memset(power[:], -0.5).then_inc(power_set, 1)
                pool.wait_ge(power_set, 1)
                if load:
                    pool.memset(pr.one[:], 1.0)
                    for b in range(BARE, LATE):
                        take_rstd(pool, b)

        block = ctx.enter_context(nc.Block())

        @block.tensor
        def _(pe):
            def prep(bank, k):
                for kd in range(KD):
                    mm = pe.transpose(bank[:, bass.ts(kd, P)], xn[:, k % 2, bass.ts(kd, P)], pr.ident[:])
                return mm

            def misc(it, at, use, bank=misc_bank):
                if use[0] == "prep":
                    pe.wait_ge(xn_ready, prep_count(it, use[1]) + 1)
                elif use[2] == 0:
                    pe.wait_ge(vdiag_ready, it * 2 + use[1] + 1)
                if bank is misc_bank:
                    pe.wait_ge(misc_free, at + 1)
                (prep(bank, use[1]) if use[0] == "prep" else setup(pe, it, bank, use[1], use[2])).then_inc(misc_written, 1)

            def scores(it, k, ready):
                u = it * UB + k
                _, p, t = place(it, k)
                pe.wait_ge(sub_done, u + 1)
                pe.wait_ge(misc_free, ready + 1)
                for half in range(2):
                    i = 0
                    for kd in range(KD):
                        for xt, gm in ((xT_hi, g_hi), (xT_lo, g_hi), (xT_hi, g_lo)):
                            mm = pe.matmul(score_bank[k % 2][half][:, 0:HALF], xt[:, kd, bass.ts(t, P)],
                                           gm[:, p, kd, bass.ts(half, HALF)], start=(i == 0), stop=(i == 3 * KD - 1))
                            i += 1
                mm.then_inc(sc_done, 1)

            def probs_transpose(it, k):
                u = it * UB + k
                pe.wait_ge(mul_done, u + 1)
                pe.wait_ge(pT_copied, u + 1)
                for c in range(NCH):
                    bk = probT_bank[c // CPB]
                    mm = pe.transpose(bk[:, bass.ts(c % CPB, P)], ex[:, k % ER, bass.ts(c, P)], pr.ident[:])
                mm.then_inc(tr_done, 1)

            def attend(it, k):
                u = it * UB + k
                _, p, _ = place(it, k)
                pe.wait_ge(pT_lo_done, u + 1)
                pe.wait_ge(res_done, u + 1)
                i = 0
                for c in range(NCH):
                    for pt, vm in ((pT_hi, v_hi), (pT_lo, v_hi), (pT_hi, v_lo)):
                        mm = pe.matmul(av_bank[:, 0:D], pt[:, k % 2, bass.ts(c, P)], vm[:, p, c, :],
                                       start=(i == 0), stop=(i == 3 * NCH - 1))
                        i += 1
                mm.then_inc(av_done, 1)

            for at, use in first_preps():
                misc(0, at, use, first_bank[at])

            def body(it, first, last):
                uses = numbered(it, last)
                done = len(FIRST_USES) + it * PER_BODY
                for k in range(STEPS if last else UB):
                    if k < UB:
                        for at, use in uses[k][:1]:
                            misc(it, at, use)
                        scores(it, k, done)
                        for at, use in uses[k][1:]:
                            misc(it, at, use)
                        done = done + len(uses[k])
                    if (k >= LAG_T or not first) and k < UB + LAG_T:
                        probs_transpose(it, k - LAG_T)
                    if (k >= LAG_AV or not first) and k < UB + LAG_AV:
                        attend(it, k - LAG_AV)

            bodies_of(pe, body)

        @block.scalar
        def _(act):
            def misc(it, at, use, bank=misc_bank):
                act.wait_ge(misc_written, at + 1)
                if use[0] == "prep":
                    t = use[1] % NT
                    ins = act.activation(xT_hi[:, :, bass.ts(t, P)], bank[:, 0:D].rearrange("p (c t) -> p c t", c=KD),
                                         ACT.Copy)
                else:
                    ins = setup_hi(act, it, bank, use[1], use[2])
                ins.then_inc(misc_hi, 1)

            def exp(it, k):
                u = it * UB + k
                act.wait_ge(sub_done, u + 3)
                act.activation(ex[:, k % ER, 0:GW], ex[:, k % ER, 0:GW], ACT.Exp).then_inc(exp_done, 1)

            def probT_copy(it, k):
                u = it * UB + k
                act.wait_ge(tr_done, u + 1 + ER)
                act.wait_ge(av_done, u + 1)
                for dst in (pT_hi, pT):
                    act.activation(dst[:, k % 2, 0:CPB * P], probT_bank[0][:], ACT.Copy)
                    ins = act.activation(dst[:, k % 2, CPB * P:PW], probT_bank[1][:, 0:PW - CPB * P], ACT.Copy)
                ins.then_inc(pT_copied, 1)

            for at, use in first_preps():
                misc(0, at, use, first_bank[at])

            def body(it, first, last):
                uses = numbered(it, last)
                for k in range(UB + LAG_T if last else UB):
                    if k < UB:
                        for at, use in uses[k]:
                            misc(it, at, use)
                    if k >= LAG_T or not first:
                        probT_copy(it, k - LAG_T)
                    if k < UB:
                        exp(it, k)

            bodies_of(act, body)

        @block.vector
        def _(dve):
            def misc(it, at, use, bank=misc_bank):
                if use[0] == "prep":
                    cols = bass.ts(use[1] % NT, P)
                    dve.wait_ge(misc_hi, at + 1)
                    ins = dve.tensor_tensor(xT_lo[:, :, cols], bank[:, 0:D].rearrange("p (c t) -> p c t", c=KD),
                                            xT_hi[:, :, cols].bitcast(F32), ALU.subtract)
                else:
                    dve.wait_ge(misc_hi, at + 1)
                    ins = setup_lo(dve, it, bank, use[1], use[2])
                ins.then_inc(misc_free, 1)

            def normalise(it, k, at):
                b, _, t = place(it, k)
                dve.wait_ge(misc_written, at)
                dve.tensor_scalar(xn[:, k % 2, :], pr.x[:, b * NT + t, :], pr.mean[:, bass.ds(b * NT + t, 1)],
                                  pr.rstd[:, bass.ds(b * NT + t, 1)], ALU.subtract, ALU.mult).then_inc(xn_ready, 1)

            def score_max(it, k):
                u = it * UB + k
                dve.wait_ge(sc_done, u + 1)
                for half in range(2):
                    rd = dve.tensor_reduce(mx[:, k % 2, bass.ts(half, GH // 2)],
                                           score_bank[k % 2][half][:, 0:HALF].rearrange("p (h j) -> p h j", h=GH // 2),
                                           AX_X, ALU.max)
                rd.then_inc(max_done, 1)

            def score_sub(it, k):
                u = it * UB + k
                dve.wait_ge(max_done, u + 1)
                dve.wait_ge(tr_done, u + 1)
                for half in range(2):
                    m = mx[:, k % 2, bass.ts(half, GH // 2)].unsqueeze(2).to_broadcast([P, GH // 2, NC])
                    ss = dve.tensor_tensor(ex[:, k % ER, bass.ts(half, HALF)].rearrange("p (h j) -> p h j", h=GH // 2),
                                           score_bank[k % 2][half][:, 0:HALF].rearrange("p (h j) -> p h j", h=GH // 2),
                                           m, ALU.subtract)
                ss.then_inc(sub_done, 1)

            def exp_sum(it, k):
                u = it * UB + k
                dve.wait_ge(exp_done, u + 1)
                dve.tensor_reduce(sm[:, k % 2, :], ex[:, k % ER, 0:GW].rearrange("p (h j) -> p h j", h=GH),
                                  AX_X, ALU.add).then_inc(sum_done, 1)

            def exp_rec(it, k):
                u = it * UB + k
                dve.wait_ge(sum_done, u + 1)
                dve.reciprocal(rc[:, k % 2, :], sm[:, k % 2, :]).then_inc(rec_done, 1)

            def residual(it, k):
                u = it * UB + k
                b, _, t = place(it, k)
                dve.wait_ge(av_done, u + 3)
                if prep_due(k):
                    dve.wait_ge(bo_added, prep_count(it, k) + 1)
                xt = pr.x[:, b * NT + t, :]
                dve.tensor_tensor(xt, xt, av_bank[:, 0:D], ALU.add).then_inc(res_done, 1)

            def tile_stats(it, k):
                b, _, t = place(it, k)
                dve.bn_stats(stats[:, t, :], pr.x[:, b * NT + t, :])

            def tile_mean(it, k):
                _, p, t = place(it, k)
                dve.bn_aggr(mv[:, p, t, :], stats[:, t, :])

            def router_sum(t):
                if t == 0:
                    dve.wait_ge(rstd_done, 1)
                to, xt, r = pr.acc[:, t % 2, :], pr.x[:, t, :], pr.rstd[:, t:t + 1]
                if t < 2:
                    dve.tensor_scalar(to, xt, r, None, ALU.mult).then_inc(pr.acc_done, 1)
                else:
                    dve.wait_ge(pr.acc_done, t - 1)
                    dve.scalar_tensor_tensor(out=to, in0=xt, scalar=r, in1=to, op0=ALU.mult,
                                             op1=ALU.add).then_inc(pr.acc_done, 1)

            def batch_mean(it, k):
                b, p, _ = place(it, k)
                dve.tensor_copy(pr.mean[:, bass.ts(b, NT)], mv[:, p, :, 0])
                dve.tensor_scalar(ve[:, p, :], mv[:, p, :, 1], EPS, None, ALU.add).then_inc(ve_done, 1)

            for at, use in first_preps():
                normalise(0, use[1], SETUP)
            for at, use in first_preps():
                misc(0, at, use, first_bank[at])
            normalise(0, AHEAD, len(FIRST_USES) - 1)

            def body(it, first, last):
                uses = numbered(it, last)
                done = len(FIRST_USES) + it * PER_BODY
                for k in range(STEPS if last else UB):
                    if (k >= LAG_ST or not first) and finishes(k - LAG_ST) and k < UB + LAG_ST:
                        if k >= UB + LAG_RES:
                            pr.wait_apart(dve, res_done, it * UB + k - LAG_ST + 2)
                        tile_stats(it, k - LAG_ST)
                    if (k >= LAG_AG or not first) and finishes(k - LAG_AG) and k < UB + LAG_AG:
                        if k >= UB + LAG_RES:
                            dve.drain()
                        tile_mean(it, k - LAG_AG)
                    if (k >= LAG_FIN or not first) and finishes(k - LAG_FIN) and (k - LAG_FIN) % NT == NT - 1:
                        if k >= UB + LAG_RES:
                            dve.drain()
                        batch_mean(it, k - LAG_FIN)
                    if prep_due(k + AHEAD + 1) and not (last and k + AHEAD + 1 >= UB):
                        normalise(it, k + AHEAD + 1, done)
                    if (k >= LAG_RES or not first) and k < UB + LAG_RES:
                        residual(it, k - LAG_RES)
                    if k < UB:
                        for at, use in uses[k][:1]:
                            misc(it, at, use)
                        score_max(it, k)
                    if (k >= 1 or not first) and k <= UB:
                        exp_sum(it, k - 1)
                    if k < UB:
                        for at, use in uses[k][1:]:
                            misc(it, at, use)
                    if (k >= 1 or not first) and k <= UB:
                        exp_rec(it, k - 1)
                    if k < UB:
                        score_sub(it, k)
                        done = done + len(uses[k])
                        if k % NT == NT - 1 and not last:
                            place_kv(dve, it, k // NT + 2, done)
                    if load and last and 0 <= k - ROUTER_AT < NT:
                        router_sum(k - ROUTER_AT)
                    if first:
                        for b in range(LATE, B):
                            if k < NT:
                                take_stats(dve, b, k)
                            if k == NT + b - LATE:
                                take_mean(dve, b)

            bodies_of(dve, body)

        @block.gpsimd
        def _(pool):
            def normalise_probs(it, k):
                u = it * UB + k
                pool.wait_ge(rec_done, u + 1)
                e3 = ex[:, k % ER, 0:GW].rearrange("p (h j) -> p h j", h=GH)
                pool.tensor_tensor(e3, e3, rc[:, k % 2, :].unsqueeze(2).to_broadcast([P, GH, NC]),
                                   ALU.mult).then_inc(mul_done, 1)

            def probT_lo(it, k):
                u = it * UB + k
                pool.wait_ge(pT_copied, u + 2)
                pool.tensor_tensor(pT_lo[:, k % 2, :], pT[:, k % 2, :], pT_hi[:, k % 2, :].bitcast(F32),
                                   ALU.subtract).then_inc(pT_lo_done, 1)

            def add_bo(it, k):
                b, _, t = place(it, k)
                pr.wait_apart(pool, xn_ready, prep_count(it, k) + 1)
                xt = pr.x[:, b * NT + t, :]
                pool.tensor_tensor(xt, xt, bo[:], ALU.add).then_inc(bo_added, 1)

            def rstd(it, k):
                b, p, _ = place(it, k)
                count = it * (2 // groups) + (k // NT if groups == 1 else k // UB) + 1
                pr.wait_apart(pool, ve_done, count)
                pool.tensor_tensor(pr.rstd[:, bass.ts(b, NT)], ve[:, p, :], power[:], ALU.pow).then_inc(rstd_done, 1)

            for k in range(AHEAD):
                add_bo(0, k)

            def body(it, first, last):
                for k in range(STEPS if last else UB):
                    if (k >= 1 or not first) and k <= UB:
                        normalise_probs(it, k - 1)
                    if (k >= LAG_T or not first) and k < UB + LAG_T:
                        probT_lo(it, k - LAG_T)
                    if k < UB and prep_due(k + AHEAD) and not (last and k + AHEAD >= UB):
                        add_bo(it, k + AHEAD)
                    if first and NT <= k < NT + B - LATE:
                        take_rstd(pool, k - NT + LATE)
                    if (k >= LAG_FIN or not first) and finishes(k - LAG_FIN) and (k - LAG_FIN) % NT == NT - 1:
                        rstd(it, k - LAG_FIN)

            bodies_of(pool, body)


def ffn0_phase(pr, gate_in, iota_in, w1_in, b1_in, w2_in, b2_in, next_wqT_in, next_wo_in):
    nc = pr.nc
    JOBS = TOPK0
    PIECES = 8
    W1C = KD * F0
    WC = W1C + FT * D
    PIECE = WC // PIECES
    JH = NCK * FT
    HT = JOBS * JH
    LAG, RING = 2, 4
    LAG_RES = LAG + 1
    SPLIT_AT = LAG + 1
    NEXT_LN = HT - FT
    STATS_AT = LAG_RES + 1
    AGGR_AT = STATS_AT + NT
    with ExitStack() as ctx:
        def sb(nm, shape, dt=F32):
            return ctx.enter_context(nc.sbuf_tensor(f"f0.{nm}", shape, dt))

        def sem(nm):
            return pr.sem(f"f0_{nm}")

        raw = pr.stage
        w_hi = sb("w_hi", [P, JOBS, WC], F32R)
        w_lo = sb("w_lo", [P, JOBS, WC], F32R)
        b1 = sb("b1", [P, JOBS, FT])
        xT_hi = sb("xT_hi", [P, KD, S], F32R)
        xT_lo = sb("xT_lo", [P, KD, S], F32R)
        xn = sb("xn", [P, 2, D])
        hid = sb("hid", [P, 2, CHK])
        h_hi = sb("h_hi", [P, RING, CHK], F32R)
        h_lo = sb("h_lo", [P, RING, CHK], F32R)
        stats = sb("stats", [P, NT, 6])
        mv = sb("mv", [P, NT, 2])
        ve = sb("ve", [P, NT])
        power = sb("power", [P, NT])
        gate = sb("gate", [P, KD, E0])
        b2 = sb("b2", [E0, D])
        iota = sb("iota", [P, E0])
        mr = sb("mean_rstd", [P, B * NT])
        mr_sum = sb("mean_rstd_sum", [P, B])
        minus = sb("minus_ones", [P, D])
        ones_row = sb("ones_row", [1, P])
        ones = sb("ones", [P, 1])
        acc = sb("acc", [P, B - 1, 2, D])
        scaled = sb("scaled", [P, 2, D])
        row = sb("row", [1, B - 1, D])
        meanT = sb("meanT", [P, B - 1, KD, P])
        lg = sb("logits", [P, B, E0])
        top = sb("top", [P, B, 8])
        topi = sb("topi", [P, B, 8])
        neg = sb("neg", [P, B])
        ez = sb("ez", [P, B, E0])
        tot = sb("tot", [P, B])
        rtot = sb("rtot", [P, B])
        probs = sb("probs", [P, B, E0])
        pair = sb("pair", [P, B])
        rpair = sb("rpair", [P, B])
        hit = sb("hit", [P, B, TOPK0, E0])
        comb = sb("comb", [P, B, E0])
        combT = sb("combT", [E0, B - 1, P])
        const_in, const_set, mr_done = sem("const_in"), sem("const_set"), sem("mr_done")
        scaled_done = sem("scaled_done")
        pool_acc_done = sem("pool_acc_done")
        routed_pe, routed_copy = sem("routed_pe"), sem("routed_copy")
        step, exp_ready = sem("step"), sem("exp_ready")
        exp_done, routed, comb_done = sem("exp_done"), sem("routed"), sem("comb_done")
        combT_done, combT_copied = sem("combT_done"), sem("combT_copied")
        bias_done, bias_copied = sem("bias_done"), sem("bias_copied")
        w1_in_done, w2_in_done = sem("w1_in"), sem("w2_in")
        b1_in_done = [sem(f"b1_in{j}") for j in range(JOBS)]
        raw_hi, raw_free = sem("raw_hi"), sem("raw_free")
        xn_ready, bias_added = sem("xn_ready"), sem("bias_added")
        xT_written, xT_hi_done, xT_lo_done = sem("xT_written"), sem("xT_hi_done"), sem("xT_lo_done")
        h_done, gelu_done, h_hi_done, h_lo_done = sem("h_done"), sem("gelu_done"), sem("h_hi_done"), sem("h_lo_done")
        y_step, y_read = sem("y_step"), sem("y_read")
        stats_done, mv_done, ve_done, rstd_done = sem("stats_done"), sem("mv_done"), sem("ve_done"), sem("rstd_done")
        GELU_CR, Y_CR, READ_CR = JH + 2, RING, 2 * TPC
        h_bank = [pr.bank[0], pr.bank[1]]
        y_bank = pr.bank[2:6]
        t_bank = [pr.bank[6], pr.bank[7]]
        PARTS = [(0, 1), (1, B)]
        COMBT_AT, ROUTE_AT, COMBT2_AT = TPC + 1, TPC + 3, TPC + 11
        block = ctx.enter_context(nc.Block())

        def place(b):
            return max(b - 1, 0)

        def half_of(n, b):
            k = b - PARTS[n][0]
            return t_bank[k // 2][:, bass.ts(k % 2, D)]

        def w1_of(w, j, kd, f):
            return w[:, j, kd * F0 + f * P:kd * F0 + f * P + P]

        def w2_of(w, j, f):
            return w[:, j, W1C + f * D:W1C + f * D + D]

        def y_of(i, t):
            return y_bank[2 * (i // FT % 2) + t // 2][:, bass.ts(t % 2, D)]

        def parts(i):
            i = i % HT
            return i // JH, i // FT % NCK, i % FT

        def bodies_of(engine, body):
            body(0, first=True, last=False)
            with engine.Fori(1, B - 1) as b:
                body(b, first=False, last=False)
            body(B - 1, first=False, last=True)

        def preps_of_step(i, last):
            if i < TPC:
                return [TPC + i]
            if i >= NEXT_LN and i < NEXT_LN + TPC and not last:
                return [NT + i - NEXT_LN]
            return []

        def split_of_step(i, last):
            j, q = i // JH, i % JH - SPLIT_AT
            if 0 <= q < PIECES and not (last and j == JOBS - 1):
                return [(j + 1) * PIECES + q]
            return []

        @block.sync
        def _(sp):
            sp.dma_start(gate[:], gate_in.rearrange("(c p) e -> p c e", p=P)).then_inc(const_in, 16)
            sp.dma_start(b2[:], b2_in).then_inc(const_in, 16)
            sp.dma_start(iota[:], iota_in).then_inc(const_in, 16)

            def body(b):
                for j in range(JOBS):
                    e = sp.value_load(pr.route_i[0:1, b, j:j + 1], min_val=0, max_val=E0 - 1)
                    sp.wait_ge(raw_free, b * (JOBS * PIECES) + j * PIECES + 1)
                    sp.dma_start(raw[:, 0:W1C].rearrange("p (c f) -> p c f", c=KD),
                                 w1_in[bass.ds(e, 1)].rearrange("o (c p) f -> p (o c) f", p=P)).then_inc(w1_in_done, 16)
                    sp.dma_start(raw[:, W1C:WC].rearrange("p (c d) -> p c d", c=FT),
                                 w2_in[bass.ds(e, 1)].rearrange("o (c p) d -> p (o c) d", p=P)).then_inc(w2_in_done, 16)
                    sp.wait_ge(gelu_done, b * HT + j * JH + GELU_CR - JH)
                    sp.dma_start(b1[:, j, :],
                                 b1_in[bass.ds(e, 1)].rearrange("o p f -> p (o f)")).then_inc(b1_in_done[j], 16)
            sp.wait_ge(routed, 1)
            body(0)
            sp.wait_ge(routed, 2)
            with sp.Fori(1, B) as b:
                body(b)
            sp.wait_ge(raw_free, JOBS * B * PIECES + 1)
            for dst, src in zip(pr.query_weights(1), (next_wqT_in, next_wo_in)):
                sp.dma_start(dst, src.rearrange("(c p) n -> p c n", p=P)).then_inc(pr.weights_in[1], 16)
            sp.wait_ge(const_in, 48)
            sp.wait_ge(pr.weights_in[1], 32)
            sp.wait_ge(w1_in_done, 16 * JOBS * B)
            sp.wait_ge(w2_in_done, 16 * JOBS * B)
            for j in range(JOBS):
                sp.wait_ge(b1_in_done[j], 16 * B)

        @block.tensor
        def _(pe):
            def prep(b, t):
                pe.wait_ge(xn_ready, b * NT + t + 1)
                pe.wait_ge(xT_lo_done, b * NT + t + 1)
                for kd in range(KD):
                    mm = pe.transpose(t_bank[t % 2][:, bass.ts(kd, P)], xn[:, t % 2, bass.ts(kd, P)], pr.ident[:])
                mm.then_inc(xT_written, 1)

            def hidden(b, i):
                j, c, f = parts(i)
                if i % JH == 0:
                    pe.wait_ge(raw_free, b * (JOBS * PIECES) + j * PIECES + PIECES // 2 + 1)
                if j == 0 and f == 0:
                    pe.wait_ge(xT_lo_done, b * NT + (c + 1) * TPC + 2)
                pe.wait_ge(gelu_done, b * HT + i - 1 + GELU_CR)
                n = 0
                for kd in range(KD):
                    for wt, xt in ((w_hi, xT_hi), (w_hi, xT_lo), (w_lo, xT_hi)):
                        mm = pe.matmul(h_bank[i % 2][:], w1_of(wt, j, kd, f), xt[:, kd, bass.ts(c, CHK)],
                                       start=(n == 0), stop=(n == 3 * KD - 1))
                        n += 1
                mm.then_inc(h_done, 1)

            def output(b, i):
                j, c, f = parts(i)
                if i % JH == 0:
                    pe.wait_ge(raw_free, b * (JOBS * PIECES) + (i // JH + 1) * PIECES + 1)
                pe.wait_ge(h_lo_done, b * HT + i + 3)
                if f == 0:
                    pe.wait_ge(y_read, b * (HT // FT * TPC) + (i // FT - 1) * TPC + READ_CR)
                for t in range(TPC):
                    n = 0
                    for ht, wt in ((h_hi, w_hi), (h_lo, w_hi), (h_hi, w_lo)):
                        mm = pe.matmul(y_of(i, t), ht[:, i % RING, bass.ts(t, P)], w2_of(wt, j, f),
                                       start=(f == 0 and n == 0 and t % 2 == 0), stop=(f == FT - 1 and n == 2),
                                       skip_group_check=True)
                        n += 1
                mm.then_inc(y_step, 1)

            def route(n, stage):
                lo, hi = PARTS[n]
                if stage == 0:
                    if n:
                        pe.wait_ge(bias_copied, n)
                    if n:
                        pe.wait_ge(pool_acc_done, (B - 1) * NT)
                    else:
                        pe.wait_ge(pr.acc_done, NT)
                    for b in range(lo, hi):
                        for half in range(2):
                            pe.matmul(half_of(n, b)[0:1, :], ones[:],
                                      acc[:, b - 1, half, :] if b else pr.acc[:, half, :], start=(half == 0), stop=False)
                        mm = pe.matmul(half_of(n, b)[0:1, :], mr_sum[:, b:b + 1], minus[:], start=False, stop=True)
                    mm.then_inc(routed_pe, 1)
                if stage == 1:
                    pe.wait_ge(routed_copy, 3 * n + 1)
                    for b in range(lo, hi):
                        for kd in range(KD):
                            mm = pe.matmul(half_of(n, b)[:, bass.ts(kd, P)], row[:, place(b), bass.ts(kd, P)], ones_row[:],
                                           start=True, stop=True)
                    mm.then_inc(routed_pe, 1)
                if stage == 2:
                    pe.wait_ge(routed_copy, 3 * n + 2)
                    pe.wait_ge(const_in, 48)
                    for b in range(lo, hi):
                        for kd in range(KD):
                            mm = pe.matmul(t_bank[0][:, bass.ts(b, E0)], meanT[:, place(b), kd, :], gate[:, kd, :],
                                           start=(kd == 0), stop=(kd == KD - 1))
                    mm.then_inc(routed_pe, 1)

            def weighted_b2(n, stage):
                lo, hi = PARTS[n]
                if stage == 0:
                    if n == 0:
                        pe.wait_ge(xT_lo_done, NT + 2)
                    pe.wait_ge(comb_done, hi)
                    for b in range(lo, hi):
                        mm = pe.transpose(t_bank[0][0:E0, bass.ts(b, P)], comb[:, b, :], pr.ident[:])
                    mm.then_inc(combT_done, 1)
                if stage == 1:
                    pe.wait_ge(combT_copied, n + 1)
                    for b in range(lo, hi):
                        mm = pe.matmul(half_of(n, b), combT[:, place(b), :], b2[:], start=True, stop=True)
                    mm.then_inc(bias_done, 1)

            pe.wait_ge(const_set, 4)
            for stage in range(3):
                route(0, stage)
            pe.wait_ge(routed_copy, 3)
            for t in range(TPC):
                prep(0, t)

            def body(b, first, last):
                for i in range(HT + LAG if last else HT):
                    if i < HT:
                        hidden(b, i)
                        if first:
                            for n, at in enumerate((COMBT_AT, COMBT2_AT)):
                                if i - at in (0, 1):
                                    weighted_b2(n, i - at)
                            if i - ROUTE_AT in range(3):
                                route(1, i - ROUTE_AT)
                        if first and i == NEXT_LN:
                            pe.wait_ge(bias_copied, 2)
                        for t in preps_of_step(i, last):
                            prep(b, t)
                    if i >= LAG or not first:
                        output(b, i - LAG)

            bodies_of(pe, body)

        @block.scalar
        def _(act):
            def split_hi(b, piece):
                g, q = divmod(piece, PIECES)
                if q == 0:
                    act.wait_ge(w1_in_done, b * (16 * JOBS) + 16 * (g + 1))
                    if g:
                        act.wait_ge(y_step, b * HT + (g - 1) * JH + Y_CR)
                if q == PIECES // 2:
                    act.wait_ge(w2_in_done, b * (16 * JOBS) + 16 * (g + 1))
                act.activation(w_hi[:, g % JOBS, bass.ts(q, PIECE)], raw[:, bass.ts(q, PIECE)],
                               ACT.Copy).then_inc(raw_hi, 1)

            def prep(b, t):
                act.wait_ge(xT_written, b * NT + t + 1)
                act.activation(xT_hi[:, :, bass.ts(t % NT, P)],
                               t_bank[t % 2][:, 0:D].rearrange("p (c t) -> p c t", c=KD),
                               ACT.Copy).then_inc(xT_hi_done, 1)

            def gelu(b, i):
                j, f = i // JH, i % FT
                if i % JH == 0:
                    act.wait_ge(b1_in_done[j], b * 16 + 16)
                act.wait_ge(h_done, b * HT + i + 1)
                act.wait_ge(h_lo_done, b * HT + i + 1)
                act.activation(hid[:, i % 2, :], h_bank[i % 2][:], ACT.Gelu, bias=b1[:, j, f:f + 1]).then_inc(gelu_done, 1)

            def route(n, stage):
                lo, hi = PARTS[n]
                if stage == 0:
                    act.wait_ge(routed_pe, 3 * n + 1)
                    for b in range(lo, hi):
                        cp = act.activation(row[:, place(b), :], half_of(n, b)[0:1, :], ACT.Copy)
                    cp.then_inc(routed_copy, 1)
                if stage == 1:
                    act.wait_ge(routed_pe, 3 * n + 2)
                    for b in range(lo, hi):
                        cp = act.activation(meanT[:, place(b), :, :].rearrange("p k m -> p (k m)"), half_of(n, b), ACT.Copy,
                                            scale=1.0 / S)
                    cp.then_inc(routed_copy, 1)
                if stage == 2:
                    act.wait_ge(routed_pe, 3 * n + 3)
                    act.activation(lg[:, lo:hi, :].rearrange("p b e -> p (b e)"), t_bank[0][:, lo * E0:hi * E0],
                                   ACT.Copy).then_inc(routed_copy, 1)
                if stage == 3:
                    act.wait_ge(exp_ready, n + 1)
                    act.activation(ez[:, lo:hi, :], ez[:, lo:hi, :], ACT.Exp).then_inc(exp_done, 1)

            def bias_copy(n):
                lo, hi = PARTS[n]
                act.wait_ge(bias_done, n + 1)
                for b in range(lo, hi):
                    cp = act.activation(pr.ffn_bias[:, b, :], half_of(n, b), ACT.Copy)
                cp.then_inc(bias_copied, 1)

            for stage in range(4):
                route(0, stage)
            for t in range(TPC):
                prep(0, t)
            for piece in range(PIECES):
                split_hi(0, piece)

            def body(b, first, last):
                for i in range(HT):
                    gelu(b, i)
                    if first:
                        for n, at in enumerate((COMBT_AT, COMBT2_AT)):
                            if i == at + 1:
                                bias_copy(n)
                        if i - ROUTE_AT in range(4):
                            route(1, i - ROUTE_AT)
                    for t in preps_of_step(i, last):
                        prep(b, t)
                    for piece in split_of_step(i, last):
                        split_hi(b, piece)

            bodies_of(act, body)

        @block.vector
        def _(dve):
            dve.sem_inc(raw_free, 1)
            dve.sem_inc(xT_lo_done, 2)
            dve.sem_inc(gelu_done, GELU_CR)
            dve.sem_inc(h_lo_done, 2)
            dve.sem_inc(y_read, READ_CR)
            dve.sem_inc(y_step, Y_CR)

            def normalise(b, t):
                if t >= 2:
                    dve.wait_ge(xT_written, b * NT + t - 1)
                col = bass.ds(b * NT + t, 1)
                dve.tensor_scalar(xn[:, t % 2, :], pr.x[:, b * NT + t, :], pr.mean[:, col], pr.rstd[:, col],
                                  ALU.subtract, ALU.mult).then_inc(xn_ready, 1)

            def prep_lo(b, t):
                dve.wait_ge(xT_hi_done, b * NT + t + 1)
                cols = bass.ts(t % NT, P)
                dve.tensor_tensor(xT_lo[:, :, cols], t_bank[t % 2][:, 0:D].rearrange("p (c t) -> p c t", c=KD),
                                  xT_hi[:, :, cols].bitcast(F32), ALU.subtract).then_inc(xT_lo_done, 1)

            def split_lo(b, piece):
                g, q = divmod(piece, PIECES)
                dve.wait_ge(raw_hi, b * (JOBS * PIECES) + piece + 1)
                cols = bass.ts(q, PIECE)
                dve.tensor_tensor(w_lo[:, g % JOBS, cols], raw[:, cols], w_hi[:, g % JOBS, cols].bitcast(F32),
                                  ALU.subtract).then_inc(raw_free, 1)

            def split_hidden(b, i):
                dve.wait_ge(gelu_done, b * HT + i + 1 + GELU_CR)
                dve.wait_ge(y_step, b * HT + i - RING + 1 + Y_CR)
                dve.tensor_copy(h_hi[:, i % RING, :], hid[:, i % 2, :]).then_inc(h_hi_done, 1)
                dve.wait_ge(h_hi_done, b * HT + i + 1)
                dve.tensor_tensor(h_lo[:, i % RING, :], hid[:, i % 2, :], h_hi[:, i % RING, :].bitcast(F32),
                                  ALU.subtract).then_inc(h_lo_done, 1)

            def residual(b, i):
                j, c, _ = parts(i)
                shift = i // HT
                dve.wait_ge(y_step, b * HT + i + 1 + Y_CR)
                for t in range(TPC):
                    tile = c * TPC + t + shift * NT
                    xt = pr.x[:, b * NT + tile, :]
                    if j == 0:
                        dve.wait_ge(bias_added, b * NT + tile + 1)
                    elif t == 0:
                        dve.wait_ge(y_read, b * (HT // FT * TPC) + (i // FT + 1 - NCK) * TPC + READ_CR)
                    dve.scalar_tensor_tensor(out=xt, in0=y_of(i, t), scalar=pr.route_w[:, b + shift, j:j + 1], in1=xt,
                                             op0=ALU.mult, op1=ALU.add).then_inc(y_read, 1)

            def tile_stats(b, t):
                if t == 0:
                    pr.wait_apart(dve, y_read, (b + 1) * (HT // FT * TPC) + READ_CR)
                dve.bn_stats(stats[:, t, :], pr.x[:, b * NT + t, :]).then_inc(stats_done, 1)

            def batch_stats(b):
                pr.wait_apart(dve, stats_done, b * NT + NT)
                for t in range(NT):
                    dve.bn_aggr(mv[:, t, :], stats[:, t, :]).then_inc(mv_done, 1)
                pr.wait_apart(dve, mv_done, b * NT + NT)
                pr.wait_apart(dve, rstd_done, b + 1)
                dve.tensor_copy(pr.mean[:, bass.ts(b, NT)], mv[:, :, 0])
                dve.tensor_scalar(ve[:], mv[:, :, 1], EPS, None, ALU.add).then_inc(ve_done, 1)

            count = [0]

            def then(ins):
                count[0] += 1
                ins.then_inc(step, 1)
                dve.wait_ge(step, count[0])

            def route(n, stage):
                lo, hi = PARTS[n]
                part = slice(lo, hi)

                def each(v):
                    return v[:, part].unsqueeze(2).to_broadcast([P, hi - lo, E0])

                if stage == 0:
                    dve.wait_ge(routed_copy, 3 * n + 3)
                    then(dve.tensor_reduce(neg[:, part], lg[:, part, :], AX_X, ALU.max))
                    dve.tensor_tensor(ez[:, part, :], lg[:, part, :], each(neg), ALU.subtract).then_inc(exp_ready, 1)
                if stage == 1:
                    dve.wait_ge(exp_done, n + 1)
                    then(dve.tensor_reduce(tot[:, part], ez[:, part, :], AX_X, ALU.add))
                    then(dve.reciprocal(rtot[:, part], tot[:, part]))
                    then(dve.tensor_tensor(probs[:, part, :], ez[:, part, :], each(rtot), ALU.mult))
                    for b in range(lo, hi):
                        ins = dve.max(top[:, b, :], probs[:, b, :])
                    then(ins)
                    for b in range(lo, hi):
                        ins = dve.max_index(pr.route_i[:, b, :], top[:, b, :], probs[:, b, :])
                    ins.then_inc(routed, 1)
                    dve.wait_ge(routed, n + 1)
                if stage == 2:
                    dve.tensor_copy(topi[:, part, :], pr.route_i[:, part, :])
                    then(dve.tensor_tensor(pair[:, part], top[:, part, 0], top[:, part, 1], ALU.add))
                    then(dve.reciprocal(rpair[:, part], pair[:, part]))
                    then(dve.tensor_tensor(pr.route_w[:, part, :], top[:, part, 0:TOPK0],
                                           rpair[:, part].unsqueeze(2).to_broadcast([P, hi - lo, TOPK0]), ALU.mult))
                if stage == 3:
                    for b in range(lo, hi):
                        for j in range(TOPK0):
                            ins = dve.tensor_scalar(hit[:, b, j, :], iota[:], topi[:, b, j:j + 1],
                                                    pr.route_w[:, b, j:j + 1], ALU.is_equal, ALU.mult)
                    then(ins)
                    for b in range(lo, hi):
                        dve.tensor_tensor(comb[:, b, :], hit[:, b, 0, :], hit[:, b, 1, :], ALU.add).then_inc(comb_done, 1)

            def combT_copy(n):
                lo, hi = PARTS[n]
                dve.wait_ge(combT_done, n + 1)
                dve.tensor_copy(combT[:, place(lo):place(hi - 1) + 1, :].rearrange("e b p -> e (b p)"),
                                t_bank[0][0:E0, lo * P:hi * P]).then_inc(combT_copied, 1)

            dve.memset(ones[:], 1.0).then_inc(const_set, 1)
            dve.memset(minus[:], -1.0).then_inc(const_set, 1)
            dve.memset(ones_row[:], 1.0).then_inc(const_set, 1)
            dve.tensor_tensor(mr[:], pr.mean[:], pr.rstd[:], ALU.mult).then_inc(mr_done, 1)
            dve.wait_ge(mr_done, 1)
            dve.tensor_reduce(mr_sum[:], mr[:].rearrange("p (b t) -> p b t", b=B), AX_X, ALU.add).then_inc(const_set, 1)
            normalise(0, 0)
            normalise(0, 1)
            dve.wait_ge(const_in, 48)
            for stage in range(2):
                route(0, stage)
            for t in range(TPC):
                if t:
                    normalise(0, t + 1)
                prep_lo(0, t)
            for stage in range(2, 4):
                route(0, stage)
            for piece in range(PIECES):
                split_lo(0, piece)

            def body(b, first, last):
                for i in range(HT + LAG_RES + 1 if last else HT):
                    if i < HT:
                        split_hidden(b, i)
                        if first:
                            for n, at in enumerate((COMBT_AT, COMBT2_AT)):
                                if i == at:
                                    combT_copy(n)
                            stage = i - ROUTE_AT - 3
                            if 0 <= stage < 4:
                                route(1, stage)
                        for t in preps_of_step(i, last):
                            if t + 1 < (NT if last else NT + TPC + 1):
                                normalise(b, t + 1)
                            prep_lo(b, t)
                        for piece in split_of_step(i, last):
                            split_lo(b, piece)
                    if (i >= LAG_RES or not first) and (i - LAG_RES) % FT == FT - 1:
                        residual(b, i - LAG_RES)
                    if not first and STATS_AT <= i < AGGR_AT:
                        tile_stats(b - 1, i - STATS_AT)
                    if not first and i == AGGR_AT:
                        batch_stats(b - 1)
            bodies_of(dve, body)

        @block.gpsimd
        def _(pool):
            def add_bias(b, t):
                shift = t // NT
                pr.wait_apart(pool, xn_ready, b * NT + t + 1)
                xt = pr.x[:, b * NT + t, :]
                pool.tensor_tensor(xt, xt, pr.ffn_bias[:, b + shift, :], ALU.add).then_inc(bias_added, 1)

            def rstd(b):
                pr.wait_apart(pool, ve_done, b + 1)
                pool.tensor_tensor(pr.rstd[:, bass.ts(b, NT)], ve[:], power[:], ALU.pow).then_inc(rstd_done, 1)

            pool.memset(power[:], -0.5).then_inc(rstd_done, 1)
            pool.wait_ge(rstd_done, 1)
            for i in range(NT, B * NT):
                b, t = divmod(i, NT)
                n = i - NT
                r = pr.rstd[:, i:i + 1].to_broadcast([P, D])
                to, xt = acc[:, b - 1, t % 2, :], pr.x[:, i, :]
                if t < 2:
                    ins = pool.tensor_tensor(to, xt, r, ALU.mult)
                else:
                    if t >= 4:
                        pool.wait_ge(pool_acc_done, n - 1)
                    pool.tensor_tensor(scaled[:, t % 2, :], xt, r, ALU.mult).then_inc(scaled_done, 1)
                    pool.wait_ge(scaled_done, (b - 1) * (NT - 2) + t - 1)
                    pool.wait_ge(pool_acc_done, n - 1)
                    ins = pool.tensor_tensor(to, to, scaled[:, t % 2, :], ALU.add)
                ins.then_inc(pool_acc_done, 1)
            pool.wait_ge(bias_copied, 1)
            for t in range(TPC):
                add_bias(0, t)

            def body(b, first, last):
                for t in range(TPC, NT):
                    add_bias(b, t)
                if first:
                    pool.wait_ge(bias_copied, 2)
                if not first:
                    rstd(b - 1)
                if not last:
                    for t in range(NT, NT + TPC):
                        add_bias(b, t)

            bodies_of(pool, body)


def expert_choice_phase(pr, y_out, xn_dram, wg_in, bg_in, first_row_in, w1_in, b1_in, w2_in, b2_in, w3_in, b3_in):
    nc = pr.nc
    Q = B // 2
    WC = 3 * KD * D
    GT = Q * P
    R = 4
    PRE = 2
    with ExitStack() as outer:
        def osb(nm, shape, dt=F32):
            return outer.enter_context(nc.sbuf_tensor(f"f1.{nm}", shape, dt))

        rows = osb("rows", [P, Q, E1], U32)
        gatew = osb("gatew", [P, Q, E1])
        raw = osb("raw", [P, 2, WC])
        w_hi = osb("w_hi", [P, R, WC], F32R)
        w_lo = osb("w_lo", [P, R, WC], F32R)
        bias = osb("bias", [P, 3, E1])
        bias_in = pr.sem("f1_bias_in")
        raw_in = [pr.sem("f1_raw_in0"), pr.sem("f1_raw_in1")]
        w_hi_done, w_lo_done = pr.sem("f1_w_hi_done"), pr.sem("f1_w_lo_done")
        with ExitStack() as ctx:
            def sb(nm, shape, dt=F32):
                return ctx.enter_context(nc.sbuf_tensor(f"f1c.{nm}", shape, dt))

            def sem(nm):
                return pr.sem(f"f1c_{nm}")

            HB = B * E1
            XT, TB = 3, 4
            NCHUNK = B * NCK
            xn = sb("xn", [P, B * NT, D])
            xT = sb("xT", [P, XT, KD, CHK])
            wg = sb("wg", [P, KD, 3 * E1])
            bg = sb("bg", [P, 1])
            first_row = sb("first_row", [P, 1])
            lg = sb("lg", [P, CHK])
            ex = sb("ex", [P, CHK])
            vals = sb("vals", [P, K1])
            idx = sb("idx", [P, K1], U32)
            nmax = sb("nmax", [P, 1])
            tot = sb("tot", [P, 1])
            wide = sb("wide", [P, 4, P])
            turned = sb("turned", [P, 4, P])
            pick = sb("pick", [P, HB])
            diff = sb("diff", [P, HB])
            diff_picked = sb("diff_picked", [P, HB])
            best = sb("best", [P, HB])
            nmax_all = sb("nmax_all", [P, HB])
            chosen = sb("chosen", [P, HB])
            e_arg = sb("e_arg", [P, 3, HB])
            e_val = sb("e_val", [P, 3, HB])
            z_half = sb("z_half", [P, 2, HB])
            z = sb("z", [P, HB])
            rz = sb("rz", [P, HB])
            weight = sb("weight", [P, HB])
            const_in, xn_ready, xn_sent = sem("const_in"), sem("xn_ready"), sem("xn_sent")
            tr_done, xT_copied, logits_done = sem("tr_done"), sem("xT_copied"), sem("logits_done")
            step, nmax_done, exp_done = sem("step"), sem("nmax_done"), sem("exp_done")
            wide_done, turn_done, args_done = sem("wide_done"), sem("turn_done"), sem("args_done")
            x_written = sem("x_written")
            lg_bank = [pr.bank[0], pr.bank[1]]
            t_bank = [pr.bank[2], pr.bank[3], pr.bank[4], pr.bank[5]]
            turn_bank = pr.bank[6]
            block = ctx.enter_context(nc.Block())

            @block.sync
            def _(sp):
                sp.dma_start(wg[:], wg_in.rearrange("(c p) e -> p c e", p=P)).then_inc(const_in, 16)
                sp.dma_start(bg[:], bg_in).then_inc(const_in, 16)
                sp.dma_start(first_row[:], first_row_in).then_inc(const_in, 16)
                for n, bi in enumerate((b1_in, b2_in, b3_in)):
                    sp.dma_start(bias[:, n, :], bi.to_broadcast([P, E1])).then_inc(bias_in, 16)
                for b in range(B):
                    sp.wait_ge(xn_ready, (b + 1) * NT)
                    sp.dma_start(xn_dram[b * S:(b + 1) * S, :].rearrange("(t p) d -> p t d", p=P),
                                 xn[:, b * NT:(b + 1) * NT, :]).then_inc(xn_sent, 16)
                for e in range(PRE):
                    for n, w in enumerate((w1_in, w2_in, w3_in)):
                        sp.dma_start(raw[:, e, bass.ts(n, KD * D)].rearrange("p (c o) -> p c o", c=KD),
                                     w[e].rearrange("(c p) o -> p c o", p=P)).then_inc(raw_in[e], 16)
                for b in range(B):
                    sp.dma_start(y_out[b].rearrange("(t p) d -> p t d", p=P),
                                 pr.x[:, b * NT:(b + 1) * NT, :]).then_inc(x_written, 16)
                sp.wait_ge(bias_in, 48)
                sp.wait_ge(xn_sent, 16 * B)
                sp.wait_ge(x_written, 16 * B)

            @block.tensor
            def _(pe):
                def logits(c):
                    b, half = divmod(c, NCK)
                    pe.wait_ge(xT_copied, (c + 1) * TPC)
                    rows0 = HB * half + 2 * E1 * (b // 2)
                    cols = slice(0, 2 * E1) if b % 2 else slice(E1, 3 * E1)
                    for kd in range(KD):
                        mm = pe.matmul(lg_bank[half][rows0:rows0 + 2 * E1, :], wg[:, kd, cols], xT[:, c % XT, kd, :],
                                       start=(b % 2 == 0 and kd == 0), stop=(b % 2 == 1 and kd == KD - 1),
                                       skip_group_check=True)
                    mm.then_inc(logits_done, 1)

                pe.wait_ge(const_in, 48)
                for i in range(B * NT):
                    pe.wait_ge(xn_ready, i + 1)
                    if i >= TB:
                        pe.wait_ge(xT_copied, i - TB + 1)
                    for kd in range(KD):
                        mm = pe.transpose(t_bank[i % TB][:, bass.ts(kd, P)], xn[:, i, bass.ts(kd, P)], pr.ident[:])
                    mm.then_inc(tr_done, 1)
                    if i % TPC == 2 and i > TPC:
                        logits(i // TPC - 1)
                logits(NCHUNK - 1)
                pe.wait_ge(wide_done, 1)
                for n in range(4):
                    mm = pe.matmul(turn_bank[:, bass.ts(n, P)], wide[:, n, :], pr.ident[:], start=True, stop=True)
                mm.then_inc(turn_done, 1)

            @block.scalar
            def _(act):
                for i in range(B * NT):
                    act.wait_ge(tr_done, i + 1)
                    c, t = divmod(i, TPC)
                    if t == 0 and c >= XT:
                        act.wait_ge(logits_done, c - XT + 1)
                    act.activation(xT[:, c % XT, :, bass.ts(t, P)],
                                   t_bank[i % TB][:, 0:D].rearrange("p (k t) -> p k t", k=KD), ACT.Copy).then_inc(xT_copied, 1)
                act.wait_ge(nmax_done, 1)
                act.activation(ex[:], lg[:], ACT.Exp, bias=nmax[:], accum_out=tot[:]).then_inc(exp_done, 1)
                for e in range(PRE):
                    act.wait_ge(raw_in[e], 48)
                    act.activation(w_hi[:, e, :], raw[:, e, :], ACT.Copy).then_inc(w_hi_done, 1)
                act.wait_ge(args_done, 3)
                act.activation(e_val[:], e_arg[:], ACT.Exp).then_inc(exp_done, 1)

            @block.vector
            def _(dve):
                for i in range(B * NT):
                    dve.tensor_scalar(xn[:, i, :], pr.x[:, i, :], pr.mean[:, i:i + 1], pr.rstd[:, i:i + 1],
                                      ALU.subtract, ALU.mult).then_inc(xn_ready, 1)
                count = [0]

                def then(ins):
                    count[0] += 1
                    ins.then_inc(step, 1)
                    dve.wait_ge(step, count[0])

                dve.wait_ge(const_in, 48)
                dve.wait_ge(logits_done, NCHUNK)
                for half in range(2):
                    at = slice(HB * half, HB * half + HB)
                    ins = dve.tensor_scalar(lg[at, :], lg_bank[half][at, :], bg[at, 0:1], None, ALU.add)
                then(ins)
                for r in range(K1 // 8):
                    cols = bass.ts(r, 8)
                    then(dve.max(vals[:, cols], lg[:]))
                    if r == 0:
                        dve.tensor_scalar(nmax[:], vals[:, 0:1], -1.0, None, ALU.mult).then_inc(nmax_done, 1)
                    ins = dve.max_index(idx[:, cols], vals[:, cols], lg[:])
                    if r == 0:
                        dve.wait_ge(exp_done, 1)
                    if r < K1 // 8 - 1:
                        ins = dve.match_replace(lg[:], vals[:, cols], lg[:], LOWEST)
                    then(ins)
                for half in range(2):
                    at = slice(HB * half, HB * half + HB)
                    way = slice(None, None, -1) if half else slice(None)
                    i3, v3 = (t[at, way].unsqueeze(1).to_broadcast([HB, 2, K1]) for t in (idx, vals))
                    dve.tensor_scalar(wide[at, 0, :].rearrange("p (a k) -> p a k", a=2), i3, first_row[at, 0:1], None, ALU.add)
                    dve.tensor_copy(wide[at, 1, :].rearrange("p (a k) -> p a k", a=2), v3)
                dve.tensor_copy(wide[:, 2, :], nmax[:].to_broadcast([P, P]))
                dve.tensor_copy(wide[:, 3, :], tot[:].to_broadcast([P, P])).then_inc(wide_done, 1)
                dve.wait_ge(turn_done, 1)
                then(dve.tensor_copy(turned[:].rearrange("p n c -> p (n c)"), turn_bank[:]))
                lower, upper = turned[:, :, 0:HB], turned[:, :, HB:2 * HB]
                dve.tensor_tensor(nmax_all[:], lower[:, 2, :], upper[:, 2, :], ALU.min)
                dve.tensor_tensor(pick[:], lower[:, 1, :], upper[:, 1, :], ALU.is_ge)
                dve.tensor_tensor(diff[:], lower[:, 0, :], upper[:, 0, :], ALU.subtract)
                then(dve.tensor_tensor(best[:], lower[:, 1, :], upper[:, 1, :], ALU.max))
                dve.tensor_tensor(e_arg[:, 0, :], best[:], nmax_all[:], ALU.add).then_inc(args_done, 1)
                dve.tensor_tensor(e_arg[:, 1, :], nmax_all[:], lower[:, 2, :], ALU.subtract).then_inc(args_done, 1)
                dve.tensor_tensor(e_arg[:, 2, :], nmax_all[:], upper[:, 2, :], ALU.subtract).then_inc(args_done, 1)
                then(dve.tensor_tensor(diff_picked[:], diff[:], pick[:], ALU.mult))
                then(dve.tensor_tensor(chosen[:], upper[:, 0, :], diff_picked[:], ALU.add))
                dve.wait_ge(exp_done, 2)
                for half, part in enumerate((lower, upper)):
                    ins = dve.tensor_tensor(z_half[:, half, :], part[:, 3, :], e_val[:, 1 + half, :], ALU.mult)
                then(ins)
                then(dve.tensor_tensor(z[:], z_half[:, 0, :], z_half[:, 1, :], ALU.add))
                then(dve.reciprocal(rz[:], z[:]))
                then(dve.tensor_tensor(weight[:], e_val[:, 0, :], rz[:], ALU.mult))
                for half in range(2):
                    lo = K1 * half
                    for dst, src in ((rows, chosen), (gatew, weight)):
                        dve.tensor_copy(dst[lo:lo + K1, :, :],
                                        src[lo:lo + K1, :].rearrange("p (q h e) -> p q h e", q=Q, h=2)[:, :, half, :])

            @block.gpsimd
            def _(pool):
                for e in range(PRE):
                    pool.wait_ge(w_hi_done, e + 1)
                    pool.tensor_tensor(w_lo[:, e, :], raw[:, e, :], w_hi[:, e, :].bitcast(F32),
                                       ALU.subtract).then_inc(w_lo_done, 1)
                pool.wait_ge(w_lo_done, PRE)

        with ExitStack() as ctx:
            def sb(nm, shape, dt=F32):
                return ctx.enter_context(nc.sbuf_tensor(f"f1.{nm}", shape, dt))

            def sem(nm):
                return pr.sem(f"f1_{nm}")

            FETCH, L1, L2, OUT = 3, 1, 2, 3
            BODIES = E1 // R
            bias_now = sb("bias_now", [P, R, 3])
            gate_now = sb("gate_now", [P, R, Q])
            cur_in = sb("cur_in", [P, R, Q], U32)
            cur_out = sb("cur_out", [P, R, Q], U32)
            xg = sb("xg", [P, R, Q, D])
            a_hi = sb("a_hi", [P, 3, 2, KD * GT], F32R)
            a_lo = sb("a_lo", [P, 3, 2, KD * GT], F32R)
            act_f = sb("act_f", [P, 2, 2, KD * GT])
            yo = sb("yo", [P, R, Q, D])
            bias_set = sem("bias_set")
            cur_set, fetched = sem("cur_set"), sem("fetched")
            xg_in = [[sem(f"xg_in{s}{q}") for q in range(Q)] for s in range(R)]
            in_T, in_hi, in_lo = sem("in_T"), sem("in_hi"), sem("in_lo")
            h_done, relu_done, h_hi, h_lo = ([sem(f"{nm}{n}") for n in range(2)]
                                             for nm in ("h_done", "relu_done", "h_hi", "h_lo"))
            y_done, y_out_ready, yo_free = sem("y_done"), sem("y_out_ready"), sem("yo_free")
            added = [sem(f"added{q}") for q in range(Q)]
            t_bank = [pr.bank[0], pr.bank[1]]
            h_bank = [[pr.bank[2], pr.bank[3]], [pr.bank[4], pr.bank[5]]]
            y_bank = [pr.bank[6], pr.bank[7]]
            block = ctx.enter_context(nc.Block())

            def w_of(s, n, kd, lo, hi):
                base = (n * KD + kd) * D
                return (w_hi[:, s % R, base + lo:base + hi], w_lo[:, s % R, base + lo:base + hi])

            def bodies_of(engine, body):
                body(0, first=True, last=False)
                with engine.Fori(1, BODIES - 1) as it:
                    body(it, first=False, last=False)
                body(BODIES - 1, first=False, last=True)

            def valid(s, first, last):
                return (s >= 0 or not first) and (s < R or not last)

            @block.sync
            def _(sp):
                for q in range(Q):
                    sp.wait_ge(xg_in[0][q], 16)

                def body(it, first, last):
                    for s in range(PRE if first else 0, R):
                        sp.wait_ge(w_lo_done, it * R + s - 1)
                        for n, w in enumerate((w1_in, w2_in, w3_in)):
                            sp.dma_start(raw[:, s % 2, bass.ts(n, KD * D)].rearrange("p (c o) -> p c o", c=KD),
                                         w[bass.ds(it * R + s, 1)].rearrange("e (c p) o -> p (e c) o", p=P)
                                         ).then_inc(raw_in[s % 2], 16)

                bodies_of(sp, body)
                for s in range(2):
                    sp.wait_ge(raw_in[s], 48 * E1 // 2)

            @block.gpsimd
            def _(pool):
                def fetch(it, s):
                    pr.wait_apart(pool, cur_set, it * R + s + 1).then_inc(fetched, 1)
                    for q in range(Q):
                        pool.indirect_dma_start(xg[:, s % R, q, :], None, xn_dram,
                                                bass.IndirectOffsetOnAxis(ap=cur_in[:, s % R, q:q + 1], axis=0)
                                                ).then_inc(xg_in[s % R][q], 16)

                def add_out(it, s, first):
                    e = it * R + s
                    pr.wait_apart(pool, y_out_ready, e + 1)
                    for q in range(Q):
                        if not (first and s == 0):
                            before = pr.wait_apart(pool, added[q], e * 16)
                            if q == Q - 1:
                                before.then_inc(yo_free, 1)
                        pool.indirect_dma_start(y_out.rearrange("b s d -> (b s) d"),
                                                bass.IndirectOffsetOnAxis(ap=cur_out[:, s % R, q:q + 1], axis=0),
                                                yo[:, s % R, q, :], None, compute_op=ALU.add).then_inc(added[q], 16)

                pool.sem_inc(yo_free, R)
                for s in range(FETCH):
                    fetch(0, s)

                def body(it, first, last):
                    for s in range(R + OUT if last else R):
                        if valid(s + FETCH, first, last):
                            fetch(it, s + FETCH)
                        if valid(s - OUT, first, last):
                            add_out(it, s - OUT, first)

                bodies_of(pool, body)
                for q in range(Q):
                    pool.wait_ge(added[q], 16 * E1)

            @block.tensor
            def _(pe):
                def turn(it, s):
                    rnd, slot = divmod(s, R)
                    for q in range(Q):
                        pe.wait_ge(xg_in[slot][q], it * 16 + (rnd + 1) * 16)
                    pe.wait_ge(in_lo, it * R + s + 1)
                    for kd in range(KD):
                        for q in range(Q):
                            mm = pe.transpose(t_bank[s % 2][:, kd * GT + q * P:kd * GT + q * P + P],
                                              xg[:, slot, q, bass.ts(kd, P)], pr.ident[:])
                    mm.then_inc(in_T, 1)

                def products(dst, s, n, kd, lo, hi, a0, a1, weights_first):
                    a = slice(kd * GT + a0, kd * GT + a1)
                    ah, al = a_hi[:, n, s % 2, a], a_lo[:, n, s % 2, a]
                    wh, wl = w_of(s, n, kd, lo, hi)
                    for i, (w, x) in enumerate(((wh, ah), (wh, al), (wl, ah))):
                        left, right = (w, x) if weights_first else (x, w)
                        mm = pe.matmul(dst, left, right, start=(kd == 0 and i == 0), stop=(kd == KD - 1 and i == 2))
                    return mm

                def layer(it, s, n):
                    e = it * R + s
                    if n == 0:
                        pe.wait_ge(in_lo, e + 3)
                        pe.wait_ge(w_lo_done, e + 1)
                    else:
                        pe.wait_ge(h_lo[0], e + 3)
                    pe.wait_ge(h_lo[n], e + 1)
                    for m in range(KD):
                        for kd in range(KD):
                            mm = products(h_bank[n][s % 2][:, bass.ts(m, GT)], s, n, kd, m * P, m * P + P, 0, GT, True)
                    mm.then_inc(h_done[n], 1)

                def last_layer(it, s, first):
                    e = it * R + s
                    pe.wait_ge(h_lo[1], e + 3)
                    if not first or s >= 2:
                        pe.wait_ge(y_out_ready, e - 1)
                    for q in range(Q):
                        for kd in range(KD):
                            mm = products(y_bank[s % 2][:, bass.ts(q, D)], s, 2, kd, 0, D, q * P, q * P + P, False)
                    mm.then_inc(y_done, 1)

                turn(0, 0)

                def body(it, first, last):
                    for s in range(R + L2 if last else R):
                        if valid(s + 1, first, last):
                            turn(it, s + 1)
                        if valid(s, first, last):
                            layer(it, s, 0)
                        if valid(s - L1, first, last):
                            layer(it, s - L1, 1)
                        if valid(s - L2, first, last):
                            last_layer(it, s - L2, first)

                bodies_of(pe, body)

            @block.scalar
            def _(act):
                def split_weights(it, s):
                    rnd, half = divmod(s, 2)
                    act.wait_ge(raw_in[half], it * (R // 2 * 48) + rnd * 48 + 48)
                    act.wait_ge(y_done, it * R + s + 1)
                    act.activation(w_hi[:, s % R, :], raw[:, half, :], ACT.Copy).then_inc(w_hi_done, 1)

                def input_hi(it, s):
                    e = it * R + s
                    act.wait_ge(in_T, e + 1)
                    act.wait_ge(h_done[0], e + 1)
                    act.activation(a_hi[:, 0, s % 2, :], t_bank[s % 2][:], ACT.Copy).then_inc(in_hi, 1)

                def relu(it, s, n):
                    e = it * R + s
                    if n == 0:
                        act.wait_ge(bias_set, e + 1)
                    act.wait_ge(h_done[n], e + 3)
                    act.wait_ge(h_lo[n], e + 1)
                    act.activation(act_f[:, n, s % 2, :], h_bank[n][s % 2][:], ACT.Relu,
                                   bias=bias_now[:, s % R, n:n + 1]).then_inc(relu_done[n], 1)
                    act.wait_ge(relu_done[n], e + 1)
                    if n == 0:
                        act.wait_ge(h_done[1], e + 1)
                    else:
                        act.wait_ge(y_done, e - 1 + R)
                    act.activation(a_hi[:, n + 1, s % 2, :], act_f[:, n, s % 2, :], ACT.Copy).then_inc(h_hi[n], 1)

                input_hi(0, 0)

                def body(it, first, last):
                    for s in range(R + L1 if last else R):
                        if valid(s + 1, first, last):
                            if not (first and s + 1 < PRE):
                                split_weights(it, s + 1)
                            input_hi(it, s + 1)
                        if valid(s, first, last):
                            relu(it, s, 0)
                        if valid(s - L1, first, last):
                            relu(it, s - L1, 1)

                bodies_of(act, body)

            @block.vector
            def _(dve):
                dve.sem_inc(in_lo, 2)
                for n in range(2):
                    dve.sem_inc(h_done[n], 2)
                    dve.sem_inc(h_lo[n], 2)
                dve.sem_inc(y_done, R)

                def rows_of(it, s):
                    return rows[:, :, bass.ds(it * R + s, 1)].rearrange("p q o -> p (q o)")

                def set_rows(it, s, again):
                    if again:
                        pr.wait_apart(dve, fetched, (it - 1) * R + s + 1)
                    dve.tensor_copy(cur_in[:, s % R, :], rows_of(it, s)).then_inc(cur_set, 1)

                def set_scales(it, s, again):
                    e = it * R + s
                    if again:
                        pr.wait_apart(dve, y_out_ready, e - R + 1)
                    dve.tensor_copy(bias_now[:, s % R, :], bias[:, :, bass.ds(e, 1)].rearrange("p n o -> p (n o)"))
                    dve.tensor_copy(gate_now[:, s % R, :],
                                    gatew[:, :, bass.ds(e, 1)].rearrange("p q o -> p (q o)")).then_inc(bias_set, 1)

                def weights_lo(it, s):
                    dve.wait_ge(w_hi_done, it * R + s + 1)
                    dve.tensor_tensor(w_lo[:, s % R, :], raw[:, s % 2, :], w_hi[:, s % R, :].bitcast(F32),
                                      ALU.subtract).then_inc(w_lo_done, 1)

                def input_lo(it, s):
                    dve.wait_ge(in_hi, it * R + s + 1)
                    dve.tensor_tensor(a_lo[:, 0, s % 2, :], t_bank[s % 2][:], a_hi[:, 0, s % 2, :].bitcast(F32),
                                      ALU.subtract).then_inc(in_lo, 1)

                def hidden_lo(it, s, n):
                    dve.wait_ge(h_hi[n], it * R + s + 1)
                    dve.tensor_tensor(a_lo[:, n + 1, s % 2, :], act_f[:, n, s % 2, :],
                                      a_hi[:, n + 1, s % 2, :].bitcast(F32), ALU.subtract).then_inc(h_lo[n], 1)

                def weigh(it, s):
                    e = it * R + s
                    dve.wait_ge(y_done, e + 1 + R)
                    dve.wait_ge(yo_free, e + 1)
                    for q in range(Q):
                        dve.tensor_scalar(yo[:, s % R, q, :], y_bank[s % 2][:, bass.ts(q, D)], bias_now[:, s % R, 2:3],
                                          gate_now[:, s % R, q:q + 1], ALU.add, ALU.mult)
                    dve.tensor_copy(cur_out[:, s % R, :], rows_of(it, s)).then_inc(y_out_ready, 1)

                for s in range(R):
                    set_rows(0, s, False)
                set_scales(0, 0, False)
                input_lo(0, 0)

                def body(it, first, last):
                    for s in range(R + OUT if last else R):
                        if valid(s - OUT, first, last):
                            weigh(it, s - OUT)
                        if valid(s + 1, first, last):
                            if not (first and s + 1 < PRE):
                                weights_lo(it, s + 1)
                            input_lo(it, s + 1)
                        if valid(s + R, first, last) and s < R and not last:
                            set_rows(it, s + R, True)
                        if valid(s, first, last):
                            hidden_lo(it, s, 0)
                        if valid(s - L1, first, last):
                            hidden_lo(it, s - L1, 1)
                        if valid(s + 1, first, last):
                            set_scales(it, s + 1, not first or s + 1 >= R)

                bodies_of(dve, body)


def build(nc, x_in, ident_in, iota_in, ctxT_in, a0, gate_in, f0, a1, f1, xn_dram, y_out, upto=9):
    with ExitStack() as ctx:
        pr = Program(nc, ctx)
        wqT, wk, wv, wo, bo = zip(a0, a1)
        attention_phase(pr, "a0", HEADS[0], pr.kT[0], pr.vT[0], bo[0],
                        load=(x_in, ident_in, ctxT_in, wk, wv, wqT[0], wo[0]))
        if upto >= 2:
            ffn0_phase(pr, gate_in, iota_in, *f0, wqT[1], wo[1])
        if upto >= 3:
            attention_phase(pr, "a1", HEADS[1], pr.kT[1], pr.vT[1], bo[1])
        if upto >= 4:
            expert_choice_phase(pr, y_out, xn_dram, *f1)
        else:
            out_written = pr.sem("out_written")
            with nc.Block() as block:
                @block.sync
                def _(sp):
                    for b in range(B):
                        sp.dma_start(y_out[b].rearrange("(t p) d -> p t d", p=P),
                                     pr.x[:, b * NT:(b + 1) * NT, :]).then_inc(out_written, 16)
                    sp.wait_ge(out_written, 16 * B)


def layout(inputs):
    import numpy as np

    def arr(name):
        return np.asarray(inputs[name])

    def whole(a):
        return np.ascontiguousarray(a)

    out = {
        "x_in": arr("x"),
        "ident_in": np.eye(P, dtype=np.float32),
        "iota_in": whole(np.broadcast_to(np.arange(E0, dtype=np.float32), (P, E0))),
        "ctxT_in": whole(arr("ctx_768").transpose(2, 0, 1).reshape(DC, B * NC)),
        "gate_in": arr("L0_ffn_gate_w"),
        "f0_w1": arr("L0_ffn_w1"),
        "f0_b1": whole(arr("L0_ffn_b1").reshape(E0, FT, P).transpose(0, 2, 1)),
        "f0_w2": arr("L0_ffn_w2"),
        "f0_b2": arr("L0_ffn_b2"),
    }
    for layer in (0, 1):
        a = f"L{layer}_xattn_"
        out[f"a{layer}_wqT"] = whole(arr(a + "Wq").T)
        out[f"a{layer}_wk"] = arr(a + "Wk")
        out[f"a{layer}_wv"] = arr(a + "Wv")
        out[f"a{layer}_wo"] = arr(a + "Wo")
        out[f"a{layer}_bo"] = arr(a + "bo").reshape(1, D)
    pad = np.zeros((D, E1), np.float32)
    out["f1_wg"] = np.concatenate([pad, arr("L1_ffn_Wg"), pad], axis=1)
    out["f1_bg"] = np.tile(arr("L1_ffn_bg"), NCK * B).reshape(P, 1)
    out["f1_first_row"] = np.repeat((np.arange(NCK)[:, None] * CHK + np.arange(B) * S).reshape(-1), E1
                                    ).astype(np.float32).reshape(P, 1)
    for n in (1, 2, 3):
        out[f"f1_w{n}"] = arr(f"L1_ffn_w{n}")
        out[f"f1_b{n}"] = arr(f"L1_ffn_b{n}").reshape(1, E1)
    return {k: whole(v) for k, v in out.items()}


def build_all(nc, a, out, upto=9):
    att = [[a[f"a{n}_{w}"] for w in ("wqT", "wk", "wv", "wo", "bo")] for n in (0, 1)]
    build(nc, a["x_in"], a["ident_in"], a["iota_in"], a["ctxT_in"], att[0], a["gate_in"],
          [a["f0_w1"], a["f0_b1"], a["f0_w2"], a["f0_b2"]], att[1],
          [a[k] for k in ("f1_wg", "f1_bg", "f1_first_row", "f1_w1", "f1_b1", "f1_w2", "f1_b2", "f1_w3", "f1_b3")],
          nc.dram_tensor("xn_rows", [B * S, D], F32).ap(), out, upto)


def kernel(**inputs):
    import numpy as np
    from concourse import bacc
    from concourse.bass_utils import run_bass_kernel_spmd

    nc = bacc.Bacc("TRN2", target_bir_lowering=False, num_devices=1)
    arrays = layout(inputs)
    aps = {k: nc.dram_tensor(k, v.shape, mybir.dt.from_np(v.dtype), kind="ExternalInput").ap() for k, v in arrays.items()}
    out = nc.dram_tensor("out", (B, S, D), F32, kind="ExternalOutput").ap()
    build_all(nc, aps, out)
    r = run_bass_kernel_spmd(nc, [arrays], core_ids=[0])
    return np.asarray(r.results[0]["out"])
```
